# Optimizing a Trainium2 kernel written in Bass

```python
import numpy as np
import jax
import jax.numpy as jnp

def _softmax(x, axis=-1):
    return jax.nn.softmax(x, axis=axis)

def _gelu(x):
    return jax.nn.gelu(x, approximate=True)

def _silu(x):
    return jax.nn.silu(x)

def _sigmoid(x):
    return jax.nn.sigmoid(x)

def _layernorm(x, axis=-1, eps=1e-05):
    m = jnp.mean(x, axis=axis, keepdims=True)
    v = jnp.var(x, axis=axis, keepdims=True)
    return (x - m) / jnp.sqrt(v + eps)

def _scatter_add(tgt, idx, src, axis=0):
    return tgt.at[idx].add(src)

def _segment_sum(src, seg, n):
    return jax.ops.segment_sum(src, seg, n)
kernel_name = 'mk_seq_postln_d1_jaxref_r4_920df3'

def setup_inputs(seed: int=0):
    np.random.seed(seed)
    _w = jnp.asarray

    def _L0_attn_setup():
        import jax, jax.numpy as jnp
        import numpy as np
        B, T, C, H = (2, 512, 256, 16)
        HS = C // H

        def _rope_cos_sin(t, hs):
            pos = jnp.arange(t, dtype=jnp.float32)[:, None]
            i = jnp.arange(1, hs // 2 + 1, dtype=jnp.float32)[None]
            theta = 1.0 / 10000.0 ** (2.0 * (i - 1.0) / hs)
            ang = pos * theta
            return (jnp.cos(ang), jnp.sin(ang))

        def _apply_rope(u, cos, sin):
            u2 = u.reshape(*u.shape[:-1], HS // 2, 2)
            x0, x1 = (u2[..., 0], u2[..., 1])
            c = cos[None, None]
            s = sin[None, None]
            r0 = x0 * c - x1 * s
            r1 = x0 * s + x1 * c
            return jnp.stack([r0, r1], axis=-1).reshape(u.shape)
        key = jax.random.key(seed)
        ks = jax.random.split(key, 5)
        return {'x': jax.random.normal(ks[0], (B, T, C), dtype=jnp.float32), 'W_qkv': jax.random.normal(ks[1], (C, 3 * C), dtype=jnp.float32) * 0.02, 'b_qkv': jax.random.normal(ks[2], (3 * C,), dtype=jnp.float32) * 0.02, 'W_proj': jax.random.normal(ks[3], (C, C), dtype=jnp.float32) * 0.02, 'b_proj': jax.random.normal(ks[4], (C,), dtype=jnp.float32) * 0.02}
    _L0_attn_in = _L0_attn_setup()

    def _L0_ffn_setup():
        import jax, jax.numpy as jnp
        import numpy as np
        B, S, D = (4, 512, 256)
        E = 8
        DFF = 1024
        CAP_FACTOR = 1.25
        key = jax.random.key(seed)
        ks = jax.random.split(key, 4)
        std_gate = float(np.sqrt(0.1 / D))
        inputs = jax.random.normal(ks[0], (B, S, D), dtype=jnp.float32)
        gate_w = jax.random.normal(ks[1], (E, D), dtype=jnp.float32) * std_gate
        w1 = jax.random.normal(ks[2], (E, D, DFF), dtype=jnp.float32) * (1.0 / np.sqrt(D))
        b1 = jnp.zeros((E, DFF), dtype=jnp.float32)
        w2 = jax.random.normal(ks[3], (E, DFF, D), dtype=jnp.float32) * (1.0 / np.sqrt(DFF))
        b2 = jnp.zeros((E, D), dtype=jnp.float32)
        return {'inputs': inputs, 'gate_w': gate_w, 'w1': w1, 'b1': b1, 'w2': w2, 'b2': b2}
    _L0_ffn_in = _L0_ffn_setup()
    _d = {'L0_attn_x': _L0_attn_in['x'], 'L0_attn_W_qkv': _L0_attn_in['W_qkv'], 'L0_attn_b_qkv': _L0_attn_in['b_qkv'], 'L0_attn_W_proj': _L0_attn_in['W_proj'], 'L0_attn_b_proj': _L0_attn_in['b_proj'], 'L0_ffn_gate_w': _L0_ffn_in['gate_w'], 'L0_ffn_w1': _L0_ffn_in['w1'], 'L0_ffn_b1': _L0_ffn_in['b1'], 'L0_ffn_w2': _L0_ffn_in['w2'], 'L0_ffn_b2': _L0_ffn_in['b2']}
    _x0 = _d['L0_attn_x']
    _d['L0_attn_x'] = jax.random.normal(jax.random.fold_in(jax.random.key(seed), 1), (2, 2048, 256), dtype=_x0.dtype)
    del _x0
    return _d

def reference(L0_attn_x, L0_attn_W_qkv, L0_attn_b_qkv, L0_attn_W_proj, L0_attn_b_proj, L0_ffn_gate_w, L0_ffn_w1, L0_ffn_b1, L0_ffn_w2, L0_ffn_b2):

    def _L0_attn_ref(x, W_qkv, b_qkv, W_proj, b_proj):
        import jax, jax.numpy as jnp
        import numpy as np
        B, T, C, H = (2, 512, 256, 16)
        HS = C // H

        def _rope_cos_sin(t, hs):
            pos = jnp.arange(t, dtype=jnp.float32)[:, None]
            i = jnp.arange(1, hs // 2 + 1, dtype=jnp.float32)[None]
            theta = 1.0 / 10000.0 ** (2.0 * (i - 1.0) / hs)
            ang = pos * theta
            return (jnp.cos(ang), jnp.sin(ang))

        def _apply_rope(u, cos, sin):
            u2 = u.reshape(*u.shape[:-1], HS // 2, 2)
            x0, x1 = (u2[..., 0], u2[..., 1])
            c = cos[None, None]
            s = sin[None, None]
            r0 = x0 * c - x1 * s
            r1 = x0 * s + x1 * c
            return jnp.stack([r0, r1], axis=-1).reshape(u.shape)
        b, t, c = x.shape
        qkv = x @ W_qkv + b_qkv
        qkv = qkv.reshape(b, t, H, 3 * HS).transpose(0, 2, 1, 3)
        q, k, v = jnp.split(qkv, 3, axis=-1)
        cos, sin = _rope_cos_sin(t, HS)
        q = _apply_rope(q, cos, sin)
        k = _apply_rope(k, cos, sin)
        att = jnp.einsum('bhqd,bhkd->bhqk', q, k) / jnp.sqrt(jnp.float32(HS))
        causal = jnp.tril(jnp.ones((t, t), dtype=bool))[None, None]
        att = jnp.where(causal, att, jnp.float32(-1000000000.0))
        att = jax.nn.softmax(att, axis=-1)
        y = jnp.einsum('bhqk,bhkd->bhqd', att, v)
        y = y.transpose(0, 2, 1, 3).reshape(b, t, c)
        return y @ W_proj + b_proj

    def _L0_ffn_ref(inputs, gate_w, w1, b1, w2, b2):
        import jax, jax.numpy as jnp
        import numpy as np
        B, S, D = (4, 512, 256)
        E = 8
        DFF = 1024
        CAP_FACTOR = 1.25
        d_model = inputs.shape[-1]
        tokens = inputs.reshape(-1, d_model)
        T = tokens.shape[0]
        num_experts = gate_w.shape[0]
        capacity = int(np.ceil(CAP_FACTOR * T / num_experts))
        logits = jnp.einsum('td,ed->te', tokens.astype(jnp.float32), gate_w)
        probs = jax.nn.softmax(logits, axis=-1)
        expert_idx = jnp.argmax(probs, axis=-1)
        mask = jax.nn.one_hot(expert_idx, num_experts, dtype=jnp.float32)
        ranks = jnp.cumsum(mask, axis=0) - 1.0
        keep = (ranks < capacity) * mask
        pos = ranks.astype(jnp.int32)
        sec_mask = jax.nn.one_hot(pos, capacity, dtype=jnp.float32) * keep[:, :, None]
        combine_weights = probs[:, :, None] * sec_mask
        dispatch = jnp.einsum('tec,td->ecd', sec_mask, tokens)
        h = jax.nn.relu(jnp.einsum('ecd,edh->ech', dispatch, w1) + b1[:, None, :])
        expert_out = jnp.einsum('ech,ehd->ecd', h, w2) + b2[:, None, :]
        ans = jnp.einsum('tec,ecd->td', combine_weights, expert_out)
        return ans.reshape(inputs.shape)
    x = L0_attn_x
    x = _layernorm(x + _L0_attn_ref(x, L0_attn_W_qkv, L0_attn_b_qkv, L0_attn_W_proj, L0_attn_b_proj), axis=-1)
    x = _layernorm(x + _L0_ffn_ref(x, L0_ffn_gate_w, L0_ffn_w1, L0_ffn_b1, L0_ffn_w2, L0_ffn_b2), axis=-1)
    return x

_drawn_inputs = setup_inputs


def setup_inputs(seed=0):
    import zlib

    import numpy as np

    out = dict(_drawn_inputs(seed))
    spreads = {'L0_ffn_b1': (0.0, 0.569), 'L0_ffn_b2': (0.0, 0.406)}
    factors = {'L0_attn_W_qkv': 6.14, 'L0_attn_b_qkv': 4.281, 'L0_attn_W_proj': 3.342}
    for name, (base, spread) in spreads.items():
        noise = np.random.default_rng([zlib.crc32(name.encode()), seed]).standard_normal(out[name].shape)
        drawn = base * np.exp(spread * noise) if base else spread * noise
        out[name] = jnp.asarray(drawn.astype(out[name].dtype))
    for name, factor in factors.items():
        out[name] = (out[name] * factor).astype(out[name].dtype)
    return out
```

```python
import math
from contextlib import ExitStack

import numpy as np

import concourse.bass as bass
from concourse import mybir

F32 = mybir.dt.float32
BF16 = mybir.dt.bfloat16
I32 = mybir.dt.int32
U32 = mybir.dt.uint32
ALU = mybir.AluOpType
ACT = mybir.ActivationFunctionType
AX = mybir.AxisListType

P = 128
B, T, C, H = 2, 2048, 256, 16
HS = C // H
KT = C // P
E, DFF = 8, 1024
CAP = math.ceil(1.25 * B * T / E)
CHUNK = 512
NCH = T // CHUNK
TPC = CHUNK // P
QKG = 2 * C // P
SCALE = 1.0 / math.sqrt(HS)
EPS = 1e-5

TERMS = [(0, 0), (0, 1), (1, 0), (1, 1), (0, 2), (2, 0)]
NTERM = len(TERMS)
SROWS = NTERM * HS
NPIECE = 3
KROWS = SROWS + NPIECE
HPU = 4
NG = H // HPU
UNITS = B * NG
VW = 2 * HS
LOWEST = -3.0e38


def in_register(engine, value):
    return value if isinstance(value, int) else engine.to_reg(value)


def project_qkv(nc, x, wqk, wv, bqk, bv2, rope_cos, rope_sin, ident, no_rows, pieces_d, v_d, slots_d):
    with ExitStack() as ctx:
        def sb(name, shape, dt=F32):
            return ctx.enter_context(nc.sbuf_tensor(name, shape, dt))

        def ps(name, shape, dt=F32):
            return ctx.enter_context(nc.psum_tensor(name, shape, dt))

        def sem(name):
            return ctx.enter_context(nc.semaphore(name))

        wqk_s = sb("wqk_s", [P, KT, 2 * C])
        wv_s = sb("wv_s", [P, KT, C])
        bqk_s = sb("bqk_s", [P, QKG])
        bv_s = sb("bv_s", [P, 2, C])
        cos_s = sb("cos_s", [P, T])
        sin_s = sb("sin_s", [P, T])
        id_s = sb("p1_id", [P, P])
        xin = [sb(f"xin{i}", [P, TPC, C]) for i in range(2)]
        xT = [sb(f"xT{i}", [P, KT, CHUNK]) for i in range(2)]
        raw = [sb(f"raw{i}", [P, QKG, CHUNK]) for i in range(2)]
        rot = [sb(f"rot{i}", [P, QKG, CHUNK]) for i in range(2)]
        rots = [sb(f"rots{i}", [P, QKG, CHUNK]) for i in range(2)]
        xcos = [sb(f"xcos{i}", [P, QKG, CHUNK]) for i in range(2)]
        hi = [sb(f"hi{i}", [P, QKG, CHUNK], BF16) for i in range(2)]
        mid = [sb(f"mid{i}", [P, QKG, CHUNK], BF16) for i in range(2)]
        low = [sb(f"low{i}", [P, QKG, CHUNK], BF16) for i in range(2)]
        vt = [sb(f"vt{i}", [P, TPC, H, VW]) for i in range(2)]
        psT = ps("psT", [P, KT, CHUNK])
        psP = ps("psP", [P, QKG, CHUNK])
        psV = ps("psV", [P, TPC, C])

        w_loaded = sem("w_loaded")
        x_loaded = [sem(f"x_loaded{i}") for i in range(2)]
        x_turned = [sem(f"x_turned{i}") for i in range(2)]
        xT_ready = sem("xT_ready")
        qk_projected = sem("qk_projected")
        v_projected = sem("v_projected")
        raw_ready = sem("raw_ready")
        rotated = sem("rotated")
        rot_scaled = sem("rot_scaled")
        cos_scaled = sem("cos_scaled")
        roped = sem("roped")
        hi_ready = sem("hi_ready")
        rest_ready = sem("rest_ready")
        mid_ready = sem("mid_ready")
        low_ready = sem("low_ready")
        ones_set = sem("ones_set")
        v_ready = sem("v_ready")
        slots_filled = sem("slots_filled")
        pieces_stored = [sem(f"pieces_stored{i}") for i in range(2)]
        v_stored = [sem(f"v_stored{i}") for i in range(2)]
        n_w = 7

        block = ctx.enter_context(nc.Block())

        @block.sync
        def _(sp):
            def load_x(b, c):
                k = 2 * b + c // 2
                sp.wait_ge(x_turned[c % 2], k)
                sp.dma_start(xin[c % 2][:], x[b, c]).then_inc(x_loaded[c % 2], 16)

            def store(b, c):
                done = (NCH * b + c + 1)
                cols = slice(c * CHUNK, (c + 1) * CHUNK)
                sp.wait_ge(v_ready, 2 * done)
                sp.dma_start(v_d[b, c], vt[c % 2][:].rearrange("p t h w -> p t (h w)")).then_inc(v_stored[c % 2], 16)
                for n, (ready, piece) in enumerate(((hi_ready, hi), (mid_ready, mid), (low_ready, low))):
                    sp.wait_ge(ready, QKG * done)
                    sp.dma_start(pieces_d[b, n, :, :, cols], piece[c % 2][:]).then_inc(pieces_stored[c % 2], 16)

            sp.dma_start(id_s[:], ident).then_inc(w_loaded, 16)
            sp.dma_start(xin[0][:], x[0, 0]).then_inc(x_loaded[0], 16)
            sp.dma_start(wqk_s[:], wqk).then_inc(w_loaded, 16)
            sp.dma_start(bqk_s[:], bqk).then_inc(w_loaded, 16)
            sp.dma_start(wv_s[:], wv).then_inc(w_loaded, 16)
            sp.dma_start(cos_s[:], rope_cos).then_inc(w_loaded, 16)
            sp.dma_start(sin_s[:], rope_sin).then_inc(w_loaded, 16)
            sp.dma_start(bv_s[:], bv2).then_inc(w_loaded, 16)
            sp.dma_start(slots_d, no_rows).then_inc(slots_filled, 16)
            with sp.Fori(0, B - 1) as b:
                for c in range(NCH):
                    if c < NCH - 1:
                        load_x(b, c + 1)
                    else:
                        load_x(b + 1, 0)
                    store(b, c)
            for c in range(NCH):
                if c < NCH - 1:
                    load_x(B - 1, c + 1)
                store(B - 1, c)
            sp.wait_ge(slots_filled, 16)
            for i in range(2):
                sp.wait_ge(pieces_stored[i], 16 * NPIECE * B * NCH // 2)
                sp.wait_ge(v_stored[i], 16 * B * NCH // 2)

        @block.tensor
        def _(pe):
            pe.wait_ge(w_loaded, 16 * n_w)
            with pe.Fori(0, B) as b:
                for c in range(NCH):
                    i, n = c % 2, NCH * b + c
                    pe.wait_ge(x_loaded[i], 16 * (2 * b + c // 2 + 1))
                    pe.wait_ge(xT_ready, KT * n)
                    for kt in range(KT):
                        for t in range(TPC):
                            last = nc.tensor.transpose(psT[:, kt, t * P:(t + 1) * P],
                                                       xin[i][:, t, kt * P:(kt + 1) * P], id_s[:])
                    last.then_inc(x_turned[i], 1)
                    pe.wait_ge(xT_ready, KT * (n + 1))
                    pe.wait_ge(raw_ready, QKG * n)
                    for g in range(QKG):
                        for kt in range(KT):
                            last = nc.tensor.matmul(psP[:, g, :], wqk_s[:, kt, g * P:(g + 1) * P], xT[i][:, kt, :],
                                                    start=(kt == 0), stop=(kt == KT - 1))
                        last.then_inc(qk_projected, 1)
                    pe.wait_ge(v_ready, 2 * n)
                    for t in range(TPC):
                        for kt in range(KT):
                            last = nc.tensor.matmul(psV[:, t, :], xT[i][:, kt, t * P:(t + 1) * P], wv_s[:, kt, :],
                                                    start=(kt == 0), stop=(kt == KT - 1))
                        if t % 2:
                            last.then_inc(v_projected, 1)

        @block.scalar
        def _(act):
            act.wait_ge(w_loaded, 16 * n_w)

            def turn(b, c):
                i = c % 2
                act.wait_ge(x_turned[i], 2 * b + c // 2 + 1)
                for kt in range(KT):
                    nc.scalar.activation(xT[i][:, kt, :], psT[:, kt, :], ACT.Copy).then_inc(xT_ready, 1)

            def evacuate(b, c, g):
                i, n = c % 2, NCH * b + c
                act.wait_ge(qk_projected, QKG * n + g + 1)
                nc.scalar.activation(raw[i][:, g, :], psP[:, g, :], ACT.Identity,
                                     bias=bqk_s[:, g:g + 1]).then_inc(raw_ready, 1)

            def cut_hi(b, c, g):
                i, n = c % 2, NCH * b + c
                if g == 0:
                    act.wait_ge(pieces_stored[i], 16 * NPIECE * (2 * b + c // 2))
                act.wait_ge(roped, QKG * n + g + 1)
                nc.scalar.activation(hi[i][:, g, :], raw[i][:, g, :], ACT.Copy).then_inc(hi_ready, 1)

            def cut_mid(b, c, g):
                i, n = c % 2, NCH * b + c
                act.wait_ge(rest_ready, QKG * n + g + 1)
                nc.scalar.activation(mid[i][:, g, :], rots[i][:, g, :], ACT.Copy).then_inc(mid_ready, 1)

            with act.Fori(0, B) as b:
                for c in range(NCH):
                    turn(b, c)
                    evacuate(b, c, 0)
                    for g in range(QKG):
                        if g + 1 < QKG:
                            evacuate(b, c, g + 1)
                        cut_hi(b, c, g)
                        if g:
                            cut_mid(b, c, g - 1)
                    cut_mid(b, c, QKG - 1)

        @block.vector
        def _(dve):
            for i in range(2):
                nc.vector.memset(vt[i][:], 1.0).then_inc(ones_set, 1)
            dve.wait_ge(ones_set, 2)
            dve.wait_ge(w_loaded, 16 * n_w)
            swap = [r ^ 1 for r in range(32)]

            def rope(b, c, g):
                i, n, cols = c % 2, NCH * b + c, slice(c * CHUNK, (c + 1) * CHUNK)
                done = QKG * n + g + 1
                done = in_register(dve, done)
                dve.wait_ge(w_loaded, 16 * n_w)
                dve.wait_ge(raw_ready, done)
                nc.vector.stream_shuffle(rot[i][:, g, :], raw[i][:, g, :], mask=swap).then_inc(rotated, 1)
                if g:
                    rest(b, c, g - 1)
                dve.wait_ge(rotated, done)
                nc.vector.tensor_tensor(rots[i][:, g, :], rot[i][:, g, :], sin_s[:, cols],
                                        ALU.mult).then_inc(rot_scaled, 1)
                dve.wait_ge(cos_scaled, done)
                dve.wait_ge(rot_scaled, done)
                nc.vector.tensor_tensor(raw[i][:, g, :], xcos[i][:, g, :], rots[i][:, g, :],
                                        ALU.add).then_inc(roped, 1)

            def rest(b, c, g):
                i, done = c % 2, QKG * (NCH * b + c) + g + 1
                dve.wait_ge(hi_ready, done)
                dve.wait_ge(roped, done)
                nc.vector.tensor_tensor(rots[i][:, g, :], raw[i][:, g, :], hi[i][:, g, :],
                                        ALU.subtract).then_inc(rest_ready, 1)

            with dve.Fori(0, B) as b:
                for c in range(NCH):
                    for g in range(QKG):
                        rope(b, c, g)
                    dve.wait_ge(v_stored[c % 2], 16 * (2 * b + c // 2))
                    for half in range(2):
                        dve.wait_ge(v_projected, 2 * (NCH * b + c) + half + 1)
                        tiles = slice(2 * half, 2 * half + 2)
                        nc.vector.tensor_tensor(vt[c % 2][:, tiles, :, 0:HS],
                                                psV[:, tiles, :].rearrange("p t (h d) -> p t h d", d=HS),
                                                bv_s[:].rearrange("p t (h d) -> p t h d", d=HS),
                                                ALU.add).then_inc(v_ready, 1)
                        if half == 0:
                            rest(b, c, QKG - 1)

        @block.gpsimd
        def _(pool):
            pool.wait_ge(w_loaded, 16 * n_w)

            def scale_cos(b, c, g):
                i, n, cols = c % 2, NCH * b + c, slice(c * CHUNK, (c + 1) * CHUNK)
                pool.wait_ge(raw_ready, QKG * n + g + 1)
                nc.gpsimd.tensor_tensor(xcos[i][:, g, :], raw[i][:, g, :], cos_s[:, cols],
                                        ALU.mult).then_inc(cos_scaled, 1)

            def cut_low(b, c, g):
                i, n = c % 2, NCH * b + c
                pool.wait_ge(mid_ready, QKG * n + g + 1)
                nc.gpsimd.tensor_tensor(low[i][:, g, :], rots[i][:, g, :], mid[i][:, g, :],
                                        ALU.subtract).then_inc(low_ready, 1)

            with pool.Fori(0, B) as b:
                for c in range(NCH):
                    pool.wait_ge(pieces_stored[c % 2], 16 * NPIECE * (2 * b + c // 2))
                    for g in range(QKG):
                        scale_cos(b, c, g)
                        if g >= 2:
                            cut_low(b, c, g - 2)
                    for g in range(QKG - 2, QKG):
                        cut_low(b, c, g)


STEPS = [(c, kb, max(0, kb * P - c * CHUNK)) for c in range(NCH) for kb in range(TPC * (c + 1))]
NSTEP = len(STEPS)
LAST = [max(n for n, s in enumerate(STEPS) if s[0] == c) for c in range(NCH)]
DIAG = [n for n, (c, kb, _) in enumerate(STEPS) if kb >= TPC * c]
NQT = T // P
MAXJOBS = [(i, t, j, min(CHUNK, (i + 1) * P - t * CHUNK), t == i // TPC)
           for i in range(NQT) for t in range(i // TPC + 1) for j in range(HPU)]
NMAX = len(MAXJOBS)
NRING = NMAX + 2
assert NRING % 3 == 0 and NSTEP % 2 == 0
FIRST_MAX, END_MAX, TURN_AT = 4, 36, 37


def max_plan():
    steps = range(FIRST_MAX, END_MAX)
    width = [CHUNK - STEPS[n][2] for n in steps]
    total, jobs = sum(width), [w for *_, w, _ in MAXJOBS]
    plan, m, seen = {}, 0, 0
    for n, w in zip(steps, width):
        seen += w
        start = m
        while m < NMAX and sum(jobs[:m + 1]) <= seen / total * sum(jobs) + 1e-6:
            m += 1
        plan[n] = range(start, m)
    assert m == NMAX
    return plan


PLAN = max_plan()


def attention(nc, pieces_d, v_d, causal, ident16, o_d):
    with ExitStack() as ctx:
        def sb(name, shape, dt=F32):
            return ctx.enter_context(nc.sbuf_tensor(name, shape, dt))

        def sem(name):
            return ctx.enter_context(nc.semaphore(name))

        q_stack = [sb(f"q_stack{i}", [P, HPU, T], BF16) for i in range(2)]
        k_stack = [sb(f"k_stack{i}", [P, HPU, T], BF16) for i in range(2)]
        v_s = [sb(f"v_s{i}", [P, NQT, HPU * VW]) for i in range(2)]
        probs = [sb(f"probs{i}", [P, HPU, CHUNK]) for i in range(2)]
        o_s = [sb(f"o_s{i}", [P, CHUNK]) for i in range(2)]
        mask_s = sb("mask_s", [P, CHUNK])
        id16 = sb("id16", [P, P], BF16)
        scratch = sb("scratch", [P, HPU, CHUNK])
        part_max = sb("part_max", [P, NQT, HPU, NCH])
        row_max = sb("row_max", [P, HPU, NQT])
        max_rest = sb("max_rest", [P, HPU, NQT])
        max_pieces = sb("max_pieces", [P, HPU, NPIECE, NQT], BF16)
        max_rows = sb("max_rows", [P, 2, P], BF16)
        scores = [ctx.enter_context(nc.psum_tensor(f"scores{p}", [P, 2, CHUNK], F32)) for p in range(2)]
        ring = [ctx.enter_context(nc.psum_tensor(f"ring{i}", [P, CHUNK], F32)) for i in range(3)]
        out_p = ctx.enter_context(nc.psum_tensor("out_p", [P, CHUNK], F32))

        const_loaded = sem("const_loaded")
        ones_set = sem("ones_row_set")
        stack_a = [sem(f"stack_a{i}") for i in range(2)]
        stack_b = [sem(f"stack_b{i}") for i in range(2)]
        v_loaded = [sem(f"v_loaded{i}") for i in range(2)]
        scores_ready = [sem(f"scores_ready{p}") for p in range(2)]
        exp_done = [sem(f"exp_done{p}") for p in range(2)]
        masked = sem("masked")
        pv_done = [sem(f"pv_done{i}") for i in range(2)]
        o_copied = sem("o_copied")
        o_stored = [sem(f"o_stored{i}") for i in range(2)]
        ring_full = sem("ring_full")
        ring_read = sem("ring_read")
        fold = sem("fold")
        pieces_ready = sem("pieces_ready")
        max_loaded = [sem(f"max_loaded{i}") for i in range(2)]
        N_FOLD = 4

        block = ctx.enter_context(nc.Block())

        @block.sync
        def _(sp):
            def load(b, g, i):
                for ready, cols in ((stack_a, slice(0, CHUNK)), (stack_b, slice(CHUNK, T))):
                    for r, (qp, kp) in enumerate(TERMS):
                        rows = slice(r * HS, (r + 1) * HS)
                        for stack, side, piece in ((q_stack, 0, qp), (k_stack, 1, kp)):
                            sp.dma_start(stack[i][rows, :, cols],
                                         pieces_d[b, piece, side, g, :, :, cols]).then_inc(ready[i], 16)
                    if ready is stack_a:
                        sp.dma_start(v_s[i][:], v_d[b, :, :, :, g]).then_inc(v_loaded[i], 16)

            def load_max(i):
                for j in range(HPU):
                    for pc in range(NPIECE):
                        at = (j % 2) * NPIECE * NQT + pc * NQT
                        sp.dma_start(q_stack[i][SROWS + pc:SROWS + pc + 1, j, :],
                                     max_rows[at:at + NQT, j // 2, :]).then_inc(max_loaded[i], 16)

            def store_o(u, b, g, c):
                sp.wait_ge(o_copied, NCH * u + c + 1)
                sp.dma_start(o_d[b, g, :, c * CHUNK:(c + 1) * CHUNK], o_s[c % 2][:]).then_inc(o_stored[c % 2], 16)

            def unit(u, b, g, i, ahead, two_ahead):
                for c in range(NCH - 1):
                    store_o(u, b, g, c)
                if ahead:
                    sp.wait_ge(ring_read, NRING * (u + 2))
                    load_max(1 - i)
                store_o(u, b, g, NCH - 1)
                if two_ahead:
                    done = in_register(sp, (NSTEP // 2) * (u + 1))
                    sp.wait_ge(const_loaded, 32)
                    sp.wait_ge(pv_done[1], done)
                    load(two_ahead[0], two_ahead[1], i)

            sp.dma_start(mask_s[:], causal).then_inc(const_loaded, 16)
            sp.dma_start(id16[:], ident16).then_inc(const_loaded, 16)
            load(0, 0, 0)
            load(0, 1, 1)
            sp.wait_ge(ring_read, NRING)
            load_max(0)
            half = NG // 2
            with sp.Fori(0, half) as k:
                for i in range(2):
                    u = 2 * k + i
                    unit(u, 0, u, i, True, (k, 2 - 2 * k + i))
            with sp.Fori(0, half - 1) as k:
                for i in range(2):
                    unit(2 * k + NG + i, 1, 2 * k + i, i, True, (1, 2 * k + 2 + i))
            unit(UNITS - 2, B - 1, NG - 2, 0, True, None)
            unit(UNITS - 1, B - 1, NG - 1, 1, False, None)
            for i in range(2):
                sp.wait_ge(o_stored[i], 16 * UNITS * NCH // 2)

        @block.tensor
        def _(pe):
            def score_step(u, i, n):
                c, kb, off = STEPS[n]
                for p in range(2):
                    pe.wait_ge(exp_done[p], NSTEP * u + n)
                    for hh in range(2):
                        j = 2 * p + hh
                        last = nc.tensor.matmul(scores[p][:, hh, off:CHUNK],
                                                k_stack[i][0:KROWS, j, kb * P:(kb + 1) * P],
                                                q_stack[i][0:KROWS, j, c * CHUNK + off:(c + 1) * CHUNK],
                                                start=True, stop=True)
                    last.then_inc(scores_ready[p], 1)

            def pv_step(u, i, n):
                c, kb, off = STEPS[n]
                for p in range(2):
                    pe.wait_ge(exp_done[p], NSTEP * u + n + 1)
                if n in DIAG:
                    pe.wait_ge(masked, len(DIAG) * u + DIAG.index(n) + 1)
                if kb == 0:
                    pe.wait_ge(o_copied, NCH * u + c)
                for j in range(HPU):
                    last = nc.tensor.matmul(out_p[j * VW:(j + 1) * VW, off:CHUNK],
                                            v_s[i][:, kb, j * VW:(j + 1) * VW], probs[n % 2][:, j, off:CHUNK],
                                            start=(kb == 0), stop=(n == LAST[c]))
                last.then_inc(pv_done[n % 2], 1)

            def max_job(u, i, m):
                qt, t, j, w, _ = MAXJOBS[m]
                if not (isinstance(u, int) and u == 0 and m < 3):
                    pe.wait_ge(ring_read, NRING * u + m - 2)
                nc.tensor.matmul(ring[m % 3][:, 0:w], q_stack[i][0:SROWS, j, qt * P:(qt + 1) * P],
                                 k_stack[i][0:SROWS, j, t * CHUNK:t * CHUNK + w],
                                 start=True, stop=True).then_inc(ring_full, 1)

            def turn_maxima(u):
                pe.wait_ge(pieces_ready, u + 1)
                for s in range(2):
                    m = NMAX + s
                    pe.wait_ge(ring_read, NRING * u + m - 2)
                    nc.tensor.transpose(ring[m % 3][0:2 * NPIECE * NQT, 0:P // 2].bitcast(BF16),
                                        max_pieces[:, 2 * s:2 * s + 2].rearrange("p j c i -> p (j c i)"),
                                        id16[:]).then_inc(ring_full, 1)

            def unit(u, i, uses, ahead):
                for n in range(1, NSTEP):
                    score_step(u, i, n)
                    if n == 1:
                        pe.wait_ge(v_loaded[i], 16 * uses[0])
                    pv_step(u, i, n - 1)
                    if ahead and n in PLAN:
                        if n == FIRST_MAX:
                            pe.wait_ge(stack_a[1 - i], 16 * 2 * NTERM * uses[1])
                        for m in PLAN[n]:
                            if MAXJOBS[m][:3] == (TPC, 0, 0):
                                pe.wait_ge(stack_b[1 - i], 16 * 2 * NTERM * uses[1])
                            max_job(u + 1, 1 - i, m)
                    if ahead and n == TURN_AT:
                        turn_maxima(u + 1)
                if ahead:
                    pe.wait_ge(max_loaded[1 - i], 16 * HPU * NPIECE * uses[1])
                    score_step(u + 1, 1 - i, 0)
                pv_step(u, i, NSTEP - 1)

            pe.wait_ge(const_loaded, 32)
            pe.wait_ge(ones_set, 2)
            pe.wait_ge(stack_a[0], 16 * 2 * NTERM)
            pe.wait_ge(stack_b[0], 16 * 2 * NTERM)
            for m in range(NMAX):
                max_job(0, 0, m)
            turn_maxima(0)
            pe.wait_ge(max_loaded[0], 16 * HPU * NPIECE)
            score_step(0, 0, 0)
            with pe.Fori(0, UNITS // 2 - 1) as k:
                unit(2 * k, 0, (k + 1, k + 1), True)
                unit(2 * k + 1, 1, (k + 1, k + 2), True)
            unit(UNITS - 2, 0, (UNITS // 2, UNITS // 2), True)
            unit(UNITS - 1, 1, (UNITS // 2, None), False)

        @block.scalar
        def _(act):
            def exp_step(u, n):
                off = STEPS[n][2]
                for p in range(2):
                    act.wait_ge(scores_ready[p], NSTEP * u + n + 1)
                    if p == 0:
                        act.wait_ge(pv_done[n % 2], (NSTEP // 2) * u + n // 2)
                    nc.scalar.activation(probs[n % 2][:, 2 * p:2 * p + 2, off:CHUNK], scores[p][:, :, off:CHUNK],
                                         ACT.Exp, scale=SCALE).then_inc(exp_done[p], 1)

            def copy_o(u, c):
                n = LAST[c]
                act.wait_ge(pv_done[n % 2], (NSTEP // 2) * u + n // 2 + 1)
                act.wait_ge(o_stored[c % 2], 16 * (2 * u + c // 2))
                nc.scalar.activation(o_s[c % 2][:], out_p[:], ACT.Copy).then_inc(o_copied, 1)

            def unit(u, ahead):
                for n in range(1, NSTEP):
                    exp_step(u, n)
                    if n - 1 in LAST:
                        copy_o(u, LAST.index(n - 1))
                if ahead:
                    exp_step(u + 1, 0)
                copy_o(u, NCH - 1)

            exp_step(0, 0)
            with act.Fori(0, UNITS - 1) as u:
                unit(u, True)
            unit(UNITS - 1, False)

        @block.vector
        def _(dve):
            for i in range(2):
                nc.vector.memset(k_stack[i][SROWS:KROWS], 1.0).then_inc(ones_set, 1)
            nc.vector.memset(part_max[:], LOWEST).then_inc(ones_set, 1)
            dve.wait_ge(ones_set, 3)
            dve.wait_ge(const_loaded, 32)

            def read_max(u, m):
                qt, t, j, w, diag = MAXJOBS[m]
                out = part_max[:, qt, j, t:t + 1]
                if diag:
                    full = in_register(dve, NRING * u + m + 1)
                    read = in_register(dve, NRING * u + m - 3)
                    dve.wait_ge(const_loaded, 32)
                    dve.wait_ge(ring_full, full)
                    if not (isinstance(u, int) and u == 0 and m < 4):
                        dve.wait_ge(ring_read, read)
                    nc.vector.tensor_tensor_reduce(out=scratch[:, j, 0:w], in0=ring[m % 3][:, 0:w],
                                                   in1=mask_s[:, CHUNK - w:CHUNK], scale=1.0, scalar=LOWEST,
                                                   op0=ALU.add, op1=ALU.max, accum_out=out).then_inc(ring_read, 1)
                else:
                    dve.wait_ge(ring_full, NRING * u + m + 1)
                    nc.vector.tensor_reduce(out, ring[m % 3][:, 0:w], axis=AX.X, op=ALU.max).then_inc(ring_read, 1)

            def fold_maxima(u):
                dve.wait_ge(ring_read, NRING * u + NMAX)
                nc.vector.tensor_reduce(row_max[:].rearrange("p j i -> p i j"), part_max[:], axis=AX.X,
                                        op=ALU.max).then_inc(fold, 1)
                dve.wait_ge(fold, N_FOLD * u + 1)
                nc.vector.tensor_scalar(max_pieces[:, :, 0, :], row_max[:], -1.0, None, ALU.mult).then_inc(fold, 1)
                dve.wait_ge(fold, N_FOLD * u + 2)
                nc.vector.scalar_tensor_tensor(max_rest[:], row_max[:], -1.0, max_pieces[:, :, 0, :],
                                               ALU.mult, ALU.subtract).then_inc(fold, 1)
                dve.wait_ge(fold, N_FOLD * u + 3)
                nc.vector.tensor_copy(max_pieces[:, :, 1, :], max_rest[:]).then_inc(fold, 1)
                dve.wait_ge(fold, N_FOLD * u + 4)
                nc.vector.tensor_tensor(max_pieces[:, :, 2, :], max_rest[:], max_pieces[:, :, 1, :],
                                        ALU.subtract).then_inc(pieces_ready, 1)
                for s in range(2):
                    m = NMAX + s
                    dve.wait_ge(ring_full, NRING * u + m + 1)
                    n = 2 * NPIECE * NQT
                    nc.vector.tensor_copy(max_rows[0:n, s, :],
                                          ring[m % 3][0:n, 0:P // 2].bitcast(BF16)).then_inc(ring_read, 1)

            for m in range(NMAX):
                read_max(0, m)
            fold_maxima(0)
            with dve.Fori(1, UNITS) as u:
                for m in range(NMAX):
                    read_max(u, m)
                fold_maxima(u)

        @block.gpsimd
        def _(pool):
            with pool.Fori(0, UNITS) as u:
                for d, n in enumerate(DIAG):
                    off = STEPS[n][2]
                    done = in_register(pool, NSTEP * u + n + 1)
                    pool.wait_ge(const_loaded, 32)
                    for p in range(2):
                        pool.wait_ge(exp_done[p], done)
                    block_ = probs[n % 2][:, :, off:off + P]
                    nc.gpsimd.affine_select(out=block_, in_=block_, compare_op=ALU.is_ge, fill=0.0, base=0,
                                            pattern=[[0, HPU], [1, P]], channel_multiplier=-1).then_inc(masked, 1)


RW = C + 4
PROB, TOKEN = C, C + 1
NOWHERE = 1.0e6
TILES = B * T // P
NBLK = CAP // P
FT = DFF // P
assert CAP == NBLK * P


def project_and_gate(nc, x, o_d, wproj, bproj, gate, ident, before, ones, prefer, slot_base, tok0, slots_d, out_d):
    with ExitStack() as ctx:
        def sb(name, shape, dt=F32):
            return ctx.enter_context(nc.sbuf_tensor(name, shape, dt))

        def ps(name, shape, dt=F32):
            return ctx.enter_context(nc.psum_tensor(name, shape, dt))

        def sem(name):
            return ctx.enter_context(nc.semaphore(name))

        wproj_s = sb("wproj_s", [P, KT, C])
        bproj_s = sb("bproj_s", [P, C])
        gate_s = sb("gate_s", [P, KT, E])
        id_s = sb("p3_id", [P, P])
        before_s = sb("before_s", [P, P], BF16)
        ones_s = sb("ones_s", [P, P], BF16)
        prefer_s = sb("prefer_s", [P, TPC, E])
        slot_base_s = sb("slot_base_s", [P, TPC, E])
        token_s = sb("token_s", [P, TPC])
        eps_s = sb("eps_s", [P, 1])
        count_s = sb("count_s", [P, E])
        o_s = [sb(f"p3_o{i}", [P, NG, CHUNK]) for i in range(2)]
        x_s = [sb(f"p3_x{i}", [P, TPC, C]) for i in range(2)]
        xb = [sb(f"xb{i}", [P, TPC, C]) for i in range(2)]
        rden = [sb(f"rden{i}", [P, H]) for i in range(2)]
        y_s = [sb(f"y_s{i}", [P, H, HS]) for i in range(2)]
        yT = [sb(f"yT{i}", [P, KT, P]) for i in range(2)]
        res = [sb(f"res{i}", [P, TPC, C]) for i in range(2)]
        stats = [sb(f"stats{i}", [P, 6]) for i in range(2)]
        mv = [sb(f"mv{i}", [P, TPC, 2]) for i in range(2)]
        std = [sb(f"std{i}", [P, TPC]) for i in range(2)]
        rstd = [sb(f"rstd{i}", [P, TPC]) for i in range(2)]
        var1 = [sb(f"var1_{i}", [P, TPC]) for i in range(2)]
        var2 = [sb(f"var2_{i}", [P, TPC]) for i in range(2)]
        std2 = [sb(f"std2_{i}", [P, TPC]) for i in range(2)]
        rstd2 = [sb(f"rstd2_{i}", [P, TPC]) for i in range(2)]
        rows = [sb(f"rows{i}", [P, TPC, RW]) for i in range(2)]
        plain = [sb(f"plain{i}", [P, TPC, C]) for i in range(2)]
        x1T = sb("x1T", [P, KT, CHUNK])
        top = sb("top", [P, TPC])
        shifted = sb("shifted", [P, TPC, E])
        wanted = sb("wanted", [P, TPC, E])
        best = sb("best", [P, TPC])
        onehot = sb("onehot", [P, TPC, E], BF16)
        expd = sb("expd", [P, TPC, E])
        total = sb("total", [P, TPC])
        rank_all = sb("rank_all", [P, TPC, E])
        rank_own = sb("rank_own", [P, TPC, E])
        rank = sb("rank", [P, TPC])
        base_own = sb("base_own", [P, TPC, E])
        slot0 = sb("slot0", [P, TPC])
        dropped = sb("dropped", [P, TPC])
        slot1 = sb("slot1", [P, TPC])
        slot = [sb(f"slot_index{i}", [P, TPC], U32) for i in range(2)]
        psA = [ps(f"psA{i}", [P, CHUNK]) for i in range(2)]
        psB = ps("psB", [P, KT, P])
        psC = [ps(f"psC{i}", [P, CHUNK]) for i in range(2)]
        psD = ps("psD", [P, KT, CHUNK])
        psL = ps("psL", [P, CHUNK])
        logits = psL[:, 0:TPC * E].rearrange("p (t e) -> p t e", e=E)
        ranks = psL[:, 64:64 + TPC * E].rearrange("p (t e) -> p t e", e=E)
        counts = psL[:, 128:128 + E]

        w_loaded = sem("w3_loaded")
        set_up = sem("set_up")
        loaded = [sem(f"loaded{i}") for i in range(2)]
        o_turned = sem("o_turned")
        y_ready = sem("y_ready")
        y_turned = sem("y_turned")
        yT_ready = sem("yT_ready")
        projected = sem("projected")
        xb_ready = sem("xb_ready")
        res_ready = sem("res_ready")
        den_ready = sem("den_ready")
        stat_ready = sem("stat_ready")
        mv_ready = sem("mv_ready")
        std_ready = sem("std_ready")
        rstd_ready = sem("rstd_ready")
        var_step = sem("var_step")
        std2_ready = sem("std2_ready")
        rstd2_ready = sem("rstd2_ready")
        rows_ready = sem("rows_ready")
        plain_ready = sem("plain_ready")
        plain_stored = [sem(f"plain_stored{i}") for i in range(2)]
        x1_turned = sem("x1_turned")
        x1T_ready = sem("x1T_ready")
        logits_ready = sem("logits_ready")
        gate_step = sem("gate_step")
        shifted_ready = sem("shifted_ready")
        exp_ready = sem("exp_ready")
        onehot_ready = sem("onehot_ready")
        ranks_ready = sem("ranks_ready")
        slots_ready = sem("slots_ready")
        rows_sent = [sem(f"rows_sent{i}") for i in range(2)]
        NC3 = B * NCH
        n_w = 10
        N_GATE = 16

        block = ctx.enter_context(nc.Block())

        @block.sync
        def _(sp):
            for dst, src in ((id_s, ident), (wproj_s, wproj), (bproj_s, bproj), (gate_s, gate), (before_s, before),
                             (ones_s, ones), (prefer_s, prefer), (slot_base_s, slot_base), (token_s, tok0)):
                sp.dma_start(dst[:], src).then_inc(w_loaded, 16)

            def load(b, c):
                i = c % 2
                sp.dma_start(o_s[i][:], o_d[b, c]).then_inc(loaded[i], 16)
                sp.dma_start(x_s[i][:], x[b, c]).then_inc(loaded[i], 16)

            load(0, 0)
            load(0, 1)
            with sp.Fori(0, B) as b:
                for c in range(NCH):
                    n = NCH * b + c
                    sp.wait_ge(o_turned, TPC * (n + 1))
                    sp.wait_ge(xb_ready, n + 1)
                    if c + 2 < NCH:
                        load(b, c + 2)
                    else:
                        load((b + 1) % B, c + 2 - NCH)
                    done = in_register(sp, TPC * (n + 1))
                    sp.wait_ge(w_loaded, 16 * (n_w - 1))
                    sp.wait_ge(plain_ready, done)
                    sp.dma_start(out_d[b, c], plain[c % 2][:]).then_inc(plain_stored[c % 2], 16)
            for i in range(2):
                sp.wait_ge(plain_stored[i], 16 * NC3 // 2)
                sp.wait_ge(loaded[i], 16 * 2 * (NC3 // 2 + 1))

        @block.tensor
        def _(pe):
            pe.wait_ge(w_loaded, 16 * (n_w - 1))

            def turn_o(b, c, t):
                i, n = c % 2, TPC * (NCH * b + c) + t
                if t == 0:
                    pe.wait_ge(loaded[i], 32 * (2 * b + c // 2 + 1))
                pe.wait_ge(y_ready, n)
                for g in range(NG):
                    last = nc.tensor.transpose(psA[t % 2][:, g * P:(g + 1) * P], o_s[i][:, g, t * P:(t + 1) * P],
                                               id_s[:])
                last.then_inc(o_turned, 1)

            def project(b, c, t):
                n = TPC * (NCH * b + c) + t
                pe.wait_ge(y_ready, n + 1)
                pe.wait_ge(yT_ready, n)
                for kt in range(KT):
                    last = nc.tensor.transpose(psB[:, kt, :],
                                               y_s[t % 2][:].rearrange("p h d -> p (h d)")[:, kt * P:(kt + 1) * P],
                                               id_s[:])
                last.then_inc(y_turned, 1)
                pe.wait_ge(yT_ready, n + 1)
                pe.wait_ge(res_ready, n)
                for kt in range(KT):
                    last = nc.tensor.matmul(psC[t % 2][:, 0:C], yT[t % 2][:, kt, :], wproj_s[:, kt, :],
                                            start=(kt == 0), stop=(kt == KT - 1))
                last.then_inc(projected, 1)

            def gate_chunk(b, c):
                i, n = c % 2, NCH * b + c
                pe.wait_ge(rows_ready, TPC * (n + 1))
                for kt in range(KT):
                    for t in range(TPC):
                        last = nc.tensor.transpose(psD[:, kt, t * P:(t + 1) * P],
                                                   rows[i][:, t, kt * P:(kt + 1) * P], id_s[:])
                last.then_inc(x1_turned, 1)
                pe.wait_ge(x1T_ready, KT * (n + 1))
                pe.wait_ge(slots_ready, n)
                for t in range(TPC):
                    for kt in range(KT):
                        last = nc.tensor.matmul(logits[:, t, :], x1T[:, kt, t * P:(t + 1) * P], gate_s[:, kt, :],
                                                start=(kt == 0), stop=(kt == KT - 1))
                last.then_inc(logits_ready, 1)

            def rank_chunk(b, c):
                n = NCH * b + c
                pe.wait_ge(onehot_ready, n + 1)
                nc.tensor.matmul(ranks[:], before_s[:], onehot[:], start=True, stop=False)
                for t in range(TPC - 1):
                    later = TPC - 1 - t
                    nc.tensor.matmul(ranks[:, t + 1:TPC, :], ones_s[:],
                                     onehot[:, t:t + 1, :].to_broadcast([P, later, E]),
                                     start=False, stop=(t == TPC - 2))
                for t in range(TPC):
                    last = nc.tensor.matmul(counts, ones_s[:], onehot[:, t, :], start=(t == 0), stop=(t == TPC - 1))
                last.then_inc(ranks_ready, 1)

            def chunk(b, c):
                turn_o(b, c, 0)
                for t in range(TPC):
                    if t + 1 < TPC:
                        turn_o(b, c, t + 1)
                    project(b, c, t)

            with pe.Fori(0, B) as b:
                for c in range(NCH):
                    chunk(b, c)
                    gate_chunk(b, c)
                    rank_chunk(b, c)

        @block.scalar
        def _(act):
            act.wait_ge(w_loaded, 16 * (n_w - 1))
            act.wait_ge(set_up, 2)

            with act.Fori(0, B) as b:
                for c in range(NCH):
                    i, n = c % 2, NCH * b + c
                    for t in range(TPC):
                        act.wait_ge(y_turned, TPC * n + t + 1)
                        nc.scalar.activation(yT[t % 2][:], psB[:], ACT.Copy).then_inc(yT_ready, 1)
                    act.wait_ge(mv_ready, TPC * (n + 1))
                    nc.scalar.activation(std[i][:], mv[i][:, :, 1], ACT.Sqrt, bias=eps_s[:]).then_inc(std_ready, 1)
                    act.wait_ge(var_step, 2 * (n + 1))
                    nc.scalar.activation(std2[i][:], var2[i][:], ACT.Sqrt, bias=eps_s[:]).then_inc(std2_ready, 1)
                    act.wait_ge(x1_turned, n + 1)
                    for kt in range(KT):
                        nc.scalar.activation(x1T[:, kt, :], psD[:, kt, :], ACT.Copy).then_inc(x1T_ready, 1)
                    act.wait_ge(rstd2_ready, n + 1)
                    act.wait_ge(plain_stored[i], 16 * (2 * b + c // 2))
                    for t in range(TPC):
                        nc.scalar.activation(plain[i][:, t, :], rows[i][:, t, 0:C], ACT.Copy,
                                             scale=rstd2[i][:, t:t + 1]).then_inc(plain_ready, 1)
                    act.wait_ge(shifted_ready, n + 1)
                    nc.scalar.activation(expd[:], shifted[:], ACT.Exp).then_inc(exp_ready, 1)

        @block.vector
        def _(dve):
            nc.vector.memset(eps_s[:], EPS).then_inc(set_up, 1)
            nc.vector.memset(count_s[:], 0.0).then_inc(set_up, 1)
            for i in range(2):
                nc.vector.memset(rows[i][:, :, C:RW], 0.0).then_inc(set_up, 1)
            dve.wait_ge(set_up, 4)
            dve.wait_ge(w_loaded, 16 * (n_w - 1))

            def normalise(b, c, t):
                n = TPC * (NCH * b + c) + t
                heads = psA[t % 2][:].rearrange("p (h w) -> p h w", w=VW)
                dve.wait_ge(o_turned, n + 1)
                nc.vector.reciprocal(rden[t % 2][:], heads[:, :, HS]).then_inc(den_ready, 1)
                dve.wait_ge(den_ready, n + 1)
                nc.vector.tensor_tensor(y_s[t % 2][:], heads[:, :, 0:HS],
                                        rden[t % 2][:].unsqueeze(2).to_broadcast([P, H, HS]),
                                        ALU.mult).then_inc(y_ready, 1)

            def residual(b, c, t):
                i, n = c % 2, TPC * (NCH * b + c) + t
                dve.wait_ge(projected, n + 1)
                if t == 0:
                    dve.wait_ge(xb_ready, NCH * b + c + 1)
                nc.vector.tensor_tensor(res[i][:, t, :], psC[t % 2][:, 0:C], xb[i][:, t, :],
                                        ALU.add).then_inc(res_ready, 1)
                dve.wait_ge(res_ready, n + 1)
                nc.vector.bn_stats(stats[t % 2][:], res[i][:, t, :]).then_inc(stat_ready, 1)
                done = in_register(dve, n + 1)
                dve.wait_ge(set_up, 4)
                dve.wait_ge(stat_ready, done)
                nc.vector.bn_aggr(mv[i][:, t, :], stats[t % 2][:]).then_inc(mv_ready, 1)

            def norm_chunk(b, c):
                i, n = c % 2, NCH * b + c
                dve.wait_ge(std_ready, n + 1)
                dve.wait_ge(mv_ready, TPC * (n + 1))
                nc.vector.reciprocal(rstd[i][:], std[i][:]).then_inc(rstd_ready, 1)
                dve.wait_ge(rstd_ready, n + 1)
                dve.wait_ge(rows_sent[i], 16 * TPC * (2 * b + c // 2))
                dve.wait_ge(plain_ready, TPC * n)
                for t in range(TPC):
                    nc.vector.tensor_scalar(rows[i][:, t, 0:C], res[i][:, t, :], mv[i][:, t, 0:1],
                                            rstd[i][:, t:t + 1], ALU.subtract, ALU.mult).then_inc(rows_ready, 1)
                nc.vector.tensor_tensor(var1[i][:], mv[i][:, :, 1], rstd[i][:], ALU.mult).then_inc(var_step, 1)
                dve.wait_ge(var_step, 2 * n + 1)
                nc.vector.tensor_tensor(var2[i][:], var1[i][:], rstd[i][:], ALU.mult).then_inc(var_step, 1)
                dve.wait_ge(std2_ready, n + 1)
                nc.vector.reciprocal(rstd2[i][:], std2[i][:]).then_inc(rstd2_ready, 1)

            def gate(b, c):
                i, n = c % 2, NCH * b + c
                step = [N_GATE * n]

                def then(instruction):
                    instruction.then_inc(gate_step, 1)
                    step[0] = step[0] + 1
                    dve.wait_ge(gate_step, step[0])

                def per_tile(ap):
                    return ap.unsqueeze(2).to_broadcast([P, TPC, E])

                dve.wait_ge(logits_ready, n + 1)
                then(nc.vector.tensor_reduce(top[:], logits, axis=AX.X, op=ALU.max))
                nc.vector.tensor_tensor(shifted[:], logits, per_tile(top[:]), ALU.subtract).then_inc(shifted_ready, 1)
                dve.wait_ge(shifted_ready, n + 1)
                then(nc.vector.scalar_tensor_tensor(wanted[:], shifted[:], 0.0, prefer_s[:], ALU.is_equal, ALU.mult))
                then(nc.vector.tensor_reduce(best[:], wanted[:], axis=AX.X, op=ALU.max))
                nc.vector.tensor_tensor(onehot[:], wanted[:], per_tile(best[:]), ALU.is_equal).then_inc(onehot_ready, 1)
                dve.wait_ge(exp_ready, n + 1)
                then(nc.vector.tensor_reduce(total[:], expd[:], axis=AX.X, op=ALU.add))
                then(nc.vector.reciprocal(rows[i][:, :, PROB], total[:]))
                then(nc.vector.tensor_copy(rows[i][:, :, TOKEN], token_s[:]))
                then(nc.vector.tensor_scalar(token_s[:], token_s[:], float(CHUNK), None, ALU.add))
                dve.wait_ge(onehot_ready, n + 1)
                then(nc.vector.tensor_tensor(base_own[:], onehot[:], slot_base_s[:], ALU.mult))
                then(nc.vector.tensor_reduce(slot0[:], base_own[:], axis=AX.X, op=ALU.add))
                dve.wait_ge(ranks_ready, n + 1)
                then(nc.vector.tensor_tensor(rank_all[:], ranks, count_s[:].unsqueeze(1).to_broadcast([P, TPC, E]),
                                             ALU.add))
                then(nc.vector.tensor_tensor(count_s[:], counts, count_s[:], ALU.add))
                then(nc.vector.tensor_tensor(rank_own[:], rank_all[:], onehot[:], ALU.mult))
                then(nc.vector.tensor_reduce(rank[:], rank_own[:], axis=AX.X, op=ALU.add))
                then(nc.vector.tensor_scalar(dropped[:], rank[:], float(CAP), NOWHERE, ALU.is_ge, ALU.mult))
                then(nc.vector.tensor_tensor(slot1[:], slot0[:], rank[:], ALU.add))
                then(nc.vector.tensor_tensor(slot1[:], slot1[:], dropped[:], ALU.add))
                nc.vector.tensor_copy(slot[i][:], slot1[:]).then_inc(slots_ready, 1)

            with dve.Fori(0, B) as b:
                for c in range(NCH):
                    normalise(b, c, 0)
                    for t in range(TPC):
                        if t + 1 < TPC:
                            normalise(b, c, t + 1)
                        residual(b, c, t)
                    norm_chunk(b, c)
                    gate(b, c)

        @block.gpsimd
        def _(pool):
            pool.wait_ge(w_loaded, 16 * (n_w - 1))

            with pool.Fori(0, B) as b:
                for c in range(NCH):
                    i, n = c % 2, NCH * b + c
                    pool.wait_ge(loaded[i], 32 * (2 * b + c // 2 + 1))
                    pool.wait_ge(res_ready, TPC * n)
                    nc.gpsimd.tensor_tensor(xb[i][:], x_s[i][:], bproj_s[:].unsqueeze(1).to_broadcast([P, TPC, C]),
                                            ALU.add).then_inc(xb_ready, 1)
                    done = in_register(pool, n + 1)
                    pool.wait_ge(w_loaded, 16 * (n_w - 1))
                    pool.wait_ge(slots_ready, done)
                    for t in range(TPC):
                        nc.gpsimd.indirect_dma_start(
                            slots_d, bass.IndirectOffsetOnAxis(ap=slot[i][:, t:t + 1], axis=0),
                            rows[i][:, t, :], None, bounds_check=E * CAP - 1, oob_is_err=False,
                        ).then_inc(rows_sent[i], 16)
            for i in range(2):
                pool.wait_ge(rows_sent[i], 16 * TPC * NC3 // 2)


def experts(nc, slots_d, w1, b1, w2, b2, ident, out_d):
    with ExitStack() as ctx:
        def sb(name, shape, dt=F32):
            return ctx.enter_context(nc.sbuf_tensor(name, shape, dt))

        def ps(name, shape, dt=F32):
            return ctx.enter_context(nc.psum_tensor(name, shape, dt))

        def sem(name):
            return ctx.enter_context(nc.semaphore(name))

        id_s = sb("p4_id", [P, P])
        eps_s = sb("p4_eps", [P, 1])
        w1_s = [sb(f"w1_s{i}", [P, KT, DFF]) for i in range(2)]
        w2_s = [sb(f"w2_s{i}", [P, FT, C]) for i in range(2)]
        b1_s = [sb(f"b1_s{i}", [P, FT]) for i in range(2)]
        b2_s = [sb(f"b2_s{i}", [P, C]) for i in range(2)]
        xe = [sb(f"xe{i}", [P, NBLK, RW]) for i in range(2)]
        token = [sb(f"token{i}", [P, NBLK], U32) for i in range(2)]
        xeT = [sb(f"xeT{i}", [P, NBLK * KT, P]) for i in range(2)]
        hT = sb("hT", [P, FT, CAP])
        eo = [sb(f"eo{i}", [P, C]) for i in range(2)]
        z = [sb(f"z{i}", [P, C]) for i in range(2)]
        stats = [sb(f"p4_stats{i}", [P, 6]) for i in range(2)]
        mv = [sb(f"p4_mv{i}", [P, 2]) for i in range(2)]
        std = [sb(f"p4_std{i}", [P, 1]) for i in range(2)]
        rstd = [sb(f"p4_rstd{i}", [P, 1]) for i in range(2)]
        fin = [sb(f"fin{i}", [P, NBLK, C]) for i in range(2)]
        psX = [ps(f"psX{i}", [P, CHUNK]) for i in range(2)]
        psH = [ps(f"psH{i}", [P, CHUNK]) for i in range(4)]
        psY = [ps(f"psY{i}", [P, CHUNK]) for i in range(2)]
        PARTS = [(0, 3), (3, NBLK)]
        PAIRS = [(blk, kt) for blk in range(NBLK) for kt in range(KT)]
        TURNS = [PAIRS[k:k + 4] for k in range(0, len(PAIRS), 4)]
        NT = len(TURNS)

        const_loaded = sem("p4_const")
        eps_set = sem("p4_eps_set")
        w_loaded = [sem(f"p4_w{i}") for i in range(2)]
        xe_loaded = [sem(f"p4_xe{i}") for i in range(2)]
        turned = sem("turned")
        xeT_ready = sem("xeT_ready")
        h_ready = sem("h_ready")
        relu_done = sem("relu_done")
        y_done = sem("y_done")
        eo_ready = sem("eo_ready")
        z_ready = sem("z_ready")
        stat_ready = sem("p4_stat")
        mv_ready = sem("p4_mvr")
        std_ready = sem("p4_stdr")
        rstd_ready = sem("p4_rstdr")
        fin_ready = sem("fin_ready")
        token_ready = sem("token_ready")
        sent = [sem(f"sent{i}") for i in range(2)]

        block = ctx.enter_context(nc.Block())

        @block.sync
        def _(sp):
            def load_weights(e, i):
                for dst, src in ((w1_s, w1), (b1_s, b1), (w2_s, w2)):
                    sp.dma_start(dst[i][:], src[e]).then_inc(w_loaded[i], 16)

            def load_rows(e, i):
                sp.dma_start(xe[i][:], slots_d[e]).then_inc(xe_loaded[i], 16)
                sp.dma_start(b2_s[i][:], b2[e]).then_inc(xe_loaded[i], 16)

            sp.dma_start(id_s[:], ident).then_inc(const_loaded, 16)
            for e in range(2):
                load_rows(e, e)
                load_weights(e, e)
            with sp.Fori(0, E // 2 - 1) as k:
                for i in range(2):
                    e = 2 * k + i
                    sp.wait_ge(y_done, NBLK * (e + 1))
                    load_weights(e + 2, i)
                    sp.wait_ge(z_ready, NBLK * (e + 1))
                    load_rows(e + 2, i)

        @block.tensor
        def _(pe):
            def turn(e, i, uses):
                pe.wait_ge(xe_loaded[i], 32 * uses)
                for s, group in enumerate(TURNS):
                    if not (isinstance(e, int) and e == 0 and s < 2):
                        pe.wait_ge(xeT_ready, NT * e + s - 1)
                    for at, (blk, kt) in enumerate(group):
                        last = nc.tensor.transpose(psX[s % 2][:, at * P:(at + 1) * P],
                                                   xe[i][:, blk, kt * P:(kt + 1) * P], id_s[:])
                    last.then_inc(turned, 1)

            def up(e, i, uses):
                xv = xeT[i][:].rearrange("p (b k) q -> p b k q", k=KT)
                pe.wait_ge(w_loaded[i], 48 * uses)
                pe.wait_ge(xeT_ready, NT * (e + 1))
                for ft in range(FT):
                    if ft < 2:
                        pe.wait_ge(relu_done, 2 * FT * e)
                    else:
                        pe.wait_ge(relu_done, 2 * FT * e + 2 * (ft - 1))
                    for part, (b0, b1_) in enumerate(PARTS):
                        for kt in range(KT):
                            last = nc.tensor.matmul(psH[2 * (ft % 2) + part][:, 0:(b1_ - b0) * P],
                                                    w1_s[i][:, kt, ft * P:(ft + 1) * P], xv[:, b0:b1_, kt, :],
                                                    start=(kt == 0), stop=(kt == KT - 1))
                        last.then_inc(h_ready, 1)

            def down(e, i):
                pe.wait_ge(relu_done, 2 * FT * (e + 1))
                for blk in range(NBLK):
                    n = NBLK * e + blk
                    if not (isinstance(e, int) and e == 0 and blk < 1):
                        pe.wait_ge(eo_ready, n - 1)
                    for ft in range(FT):
                        last = nc.tensor.matmul(psY[blk % 2][:, 0:C], hT[:, ft, blk * P:(blk + 1) * P],
                                                w2_s[i][:, ft, :], start=(ft == 0), stop=(ft == FT - 1))
                    last.then_inc(y_done, 1)

            pe.wait_ge(const_loaded, 16)
            turn(0, 0, 1)
            up(0, 0, 1)
            turn(1, 1, 1)
            down(0, 0)
            with pe.Fori(0, E // 2 - 1) as k:
                for i in range(2):
                    e = 2 * k + 1 + i
                    up(e, 1 - i, k + 1 + i)
                    turn(e + 1, i, k + 2)
                    down(e, 1 - i)
            up(E - 1, 1, E // 2)
            down(E - 1, 1)

        @block.scalar
        def _(act):
            def take_turn(e, i):
                for s, group in enumerate(TURNS):
                    act.wait_ge(turned, NT * e + s + 1)
                    nc.scalar.activation(xeT[i][:, 4 * s:4 * s + len(group), :].rearrange("p a q -> p (a q)"),
                                         psX[s % 2][:, 0:len(group) * P], ACT.Copy).then_inc(xeT_ready, 1)

            def relu(e, i):
                for ft in range(FT):
                    for part, (b0, b1_) in enumerate(PARTS):
                        act.wait_ge(h_ready, 2 * (FT * e + ft) + part + 1)
                        nc.scalar.activation(hT[:, ft, b0 * P:b1_ * P], psH[2 * (ft % 2) + part][:, 0:(b1_ - b0) * P],
                                             ACT.Relu, bias=b1_s[i][:, ft:ft + 1]).then_inc(relu_done, 1)

            def deviation(e):
                for blk in range(NBLK):
                    act.wait_ge(mv_ready, NBLK * e + blk + 1)
                    nc.scalar.activation(std[blk % 2][:], mv[blk % 2][:, 1:2], ACT.Sqrt,
                                         bias=eps_s[:]).then_inc(std_ready, 1)

            act.wait_ge(eps_set, 1)
            take_turn(0, 0)
            relu(0, 0)
            take_turn(1, 1)
            deviation(0)
            with act.Fori(0, E // 2 - 1) as k:
                for i in range(2):
                    e = 2 * k + 1 + i
                    relu(e, 1 - i)
                    take_turn(e + 1, i)
                    deviation(e)
            relu(E - 1, 1)
            deviation(E - 1)

        @block.vector
        def _(dve):
            nc.vector.memset(eps_s[:], EPS).then_inc(eps_set, 1)

            def combine(e, i, blk, uses):
                n, h = NBLK * e + blk, blk % 2
                dve.wait_ge(y_done, n + 1)
                nc.vector.tensor_tensor(eo[h][:], psY[h][:, 0:C], b2_s[i][:], ALU.add).then_inc(eo_ready, 1)
                dve.wait_ge(eo_ready, n + 1)
                nc.vector.scalar_tensor_tensor(z[h][:], eo[h][:], xe[i][:, blk, PROB:PROB + 1],
                                               xe[i][:, blk, 0:C], ALU.mult, ALU.add).then_inc(z_ready, 1)
                dve.wait_ge(z_ready, n + 1)
                nc.vector.bn_stats(stats[h][:], z[h][:]).then_inc(stat_ready, 1)
                done = in_register(dve, n + 1)
                dve.wait_ge(eps_set, 1)
                dve.wait_ge(stat_ready, done)
                nc.vector.bn_aggr(mv[h][:], stats[h][:]).then_inc(mv_ready, 1)

            def norm(e, i, blk):
                n, h = NBLK * e + blk, blk % 2
                dve.wait_ge(std_ready, n + 1)
                nc.vector.reciprocal(rstd[h][:], std[h][:]).then_inc(rstd_ready, 1)
                dve.wait_ge(rstd_ready, n + 1)
                nc.vector.tensor_scalar(fin[i][:, blk, :], z[h][:], mv[h][:, 0:1], rstd[h][:, 0:1],
                                        ALU.subtract, ALU.mult).then_inc(fin_ready, 1)

            def expert(e, i, uses):
                dve.wait_ge(xe_loaded[i], 32 * uses)
                dve.wait_ge(sent[i], 16 * NBLK * (uses - 1))
                nc.vector.tensor_copy(token[i][:], xe[i][:, :, TOKEN]).then_inc(token_ready, 1)
                for blk in range(NBLK):
                    if blk:
                        combine(e, i, blk, uses)
                        norm(e, i, blk - 1)
                    else:
                        combine(e, i, blk, uses)
                norm(e, i, NBLK - 1)

            with dve.Fori(0, E // 2) as k:
                for i in range(2):
                    expert(2 * k + i, i, k + 1)

        @block.gpsimd
        def _(pool):
            with pool.Fori(0, E // 2) as k:
                for i in range(2):
                    e = 2 * k + i
                    pool.wait_ge(token_ready, e + 1)
                    for blk in range(NBLK):
                        done = in_register(pool, NBLK * e + blk + 1)
                        pool.wait_ge(eps_set, 1)
                        pool.wait_ge(fin_ready, done)
                        nc.gpsimd.indirect_dma_start(
                            out_d, bass.IndirectOffsetOnAxis(ap=token[i][:, blk:blk + 1], axis=0),
                            fin[i][:, blk, :], None, bounds_check=B * T - 1, oob_is_err=False,
                        ).then_inc(sent[i], 16)
            for i in range(2):
                pool.wait_ge(sent[i], 16 * NBLK * (E // 2))


def constants():
    bf = mybir.dt.np(BF16)
    row = np.arange(P)
    pos = np.arange(T, dtype=np.float32)[None]
    theta = (1.0 / np.float32(10000.0) ** (2.0 * (row % HS // 2).astype(np.float32) / HS)).astype(np.float32)
    angle = pos * theta[:, None]
    sign = np.where(row % 2 == 0, -1.0, 1.0).astype(np.float32)[:, None]
    causal = np.zeros((P, CHUNK), np.float32)
    causal[:, CHUNK - P:] = np.where(row[:, None] >= row[None], 0.0, LOWEST)
    no_row = np.zeros((P, RW), np.float32)
    no_row[:, TOKEN] = NOWHERE
    eye = np.eye(P, dtype=np.float32)
    return {
        "rope_cos": np.cos(angle).astype(np.float32),
        "rope_sin": (np.sin(angle) * sign).astype(np.float32),
        "causal": causal,
        "no_row": no_row,
        "ident": eye,
        "ident16": eye.astype(bf),
        "before": (row[:, None] < row[None]).astype(bf),
        "ones16": np.ones((P, P), bf),
        "prefer": np.broadcast_to((E - np.arange(E)).astype(np.float32), (P, TPC, E)).copy(),
        "slot_base": np.broadcast_to((CAP * np.arange(E)).astype(np.float32), (P, TPC, E)).copy(),
        "tok0": (row[:, None] + P * np.arange(TPC)[None]).astype(np.float32),
    }


def program(nc, a, out, scratch):
    x = a["x"].rearrange("b (c t p) d -> b c p t d", t=TPC, p=P)
    pieces, v, o, slots = scratch
    project_qkv(nc, x, a["wqk"].rearrange("(k p) n -> p k n", p=P), a["wv"].rearrange("(k p) n -> p k n", p=P),
                a["bqk"], a["bv2"], a["rope_cos"], a["rope_sin"], a["ident"],
                a["no_row"].unsqueeze(1).to_broadcast([P, E * NBLK, RW]),
                pieces.rearrange("b n (g p) t -> b n p g t", p=P),
                v.rearrange("b (c t p) w -> b c p t w", t=TPC, p=P),
                slots.rearrange("(n p) w -> p n w", p=P))
    attention(nc, pieces.rearrange("b n (s g j d) t -> b n s g d j t", s=2, g=NG, j=HPU),
              v.rearrange("b (t p) (g w) -> b p t w g", p=P, g=NG), a["causal"], a["ident16"], o)
    project_and_gate(nc, x, o.rearrange("b g p (c q) -> b c p g q", c=NCH),
                     a["wproj"].rearrange("(k p) n -> p k n", p=P), a["bproj"],
                     a["gate"].rearrange("(k p) e -> p k e", p=P), a["ident"], a["before"], a["ones16"],
                     a["prefer"], a["slot_base"], a["tok0"], slots,
                     out.rearrange("b (c t p) d -> b c p t d", t=TPC, p=P))
    experts(nc, slots.rearrange("(e n p) w -> e p n w", e=E, p=P), a["w1"].rearrange("e (k p) n -> e p k n", p=P),
            a["b1"], a["w2"].rearrange("e (f p) n -> e p f n", p=P),
            a["b2"], a["ident"], out.rearrange("b t d -> (b t) d"))


def kernel(L0_attn_x, L0_attn_W_qkv, L0_attn_b_qkv, L0_attn_W_proj, L0_attn_b_proj, L0_ffn_gate_w,
           L0_ffn_w1, L0_ffn_b1, L0_ffn_w2, L0_ffn_b2):
    import concourse.bacc as bacc
    from concourse.bass_utils import run_bass_kernel_spmd

    w = np.asarray(L0_attn_W_qkv).reshape(C, H, 3, HS)
    bias = np.asarray(L0_attn_b_qkv).reshape(H, 3, HS)
    arrays = {
        "x": np.asarray(L0_attn_x),
        "wqk": w[:, :, 0:2].transpose(0, 2, 1, 3).reshape(C, 2 * C),
        "wv": w[:, :, 2].reshape(C, C),
        "bqk": bias[:, 0:2].transpose(1, 0, 2).reshape(QKG, P).T,
        "bv2": np.broadcast_to(bias[:, 2].reshape(C), (P, 2, C)),
        "wproj": np.asarray(L0_attn_W_proj),
        "bproj": np.broadcast_to(np.asarray(L0_attn_b_proj), (P, C)),
        "gate": np.asarray(L0_ffn_gate_w).T,
        "w1": np.asarray(L0_ffn_w1), "b1": np.asarray(L0_ffn_b1).reshape(E, FT, P).transpose(0, 2, 1), "w2": np.asarray(L0_ffn_w2),
        "b2": np.broadcast_to(np.asarray(L0_ffn_b2)[:, None, :], (E, P, C)),
        **constants(),
    }
    arrays = {k: np.ascontiguousarray(a) for k, a in arrays.items()}
    nc = bacc.Bacc("TRN2", target_bir_lowering=False, num_devices=1)
    a = {k: nc.dram_tensor(k, v.shape, mybir.dt.from_np(v.dtype), kind="ExternalInput").ap() for k, v in arrays.items()}
    out = nc.dram_tensor("out", [B, T, C], F32, kind="ExternalOutput").ap()
    scratch = [nc.dram_tensor(n, s, dt, kind="Internal").ap() for n, s, dt in (
        ("pieces_d", [B, NPIECE, 2 * C, T], BF16), ("v_d", [B, T, H * VW], F32),
        ("o_d", [B, NG, P, T], F32), ("slots_d", [E * CAP, RW], F32))]
    program(nc, a, out, scratch)
    return run_bass_kernel_spmd(nc, [arrays], core_ids=[0]).results[0]["out"]
```

```python
import math
from contextlib import ExitStack

import numpy as np

import concourse.bass as bass
from concourse import mybir

F32 = mybir.dt.float32
BF16 = mybir.dt.bfloat16
I32 = mybir.dt.int32
U32 = mybir.dt.uint32
ALU = mybir.AluOpType
ACT = mybir.ActivationFunctionType
AX = mybir.AxisListType

P = 128
B, T, C, H = 2, 2048, 256, 16
HS = C // H
KT = C // P
E, DFF = 8, 1024
CAP = math.ceil(1.25 * B * T / E)
CHUNK = 512
NCH = T // CHUNK
TPC = CHUNK // P
QKG = 2 * C // P
SCALE = 1.0 / math.sqrt(HS)
EPS = 1e-5

TERMS = [(0, 0), (0, 1), (1, 0), (1, 1), (0, 2), (2, 0)]
NTERM = len(TERMS)
SROWS = NTERM * HS
NPIECE = 3
KROWS = SROWS + NPIECE
HPU = 4
NG = H // HPU
UNITS = B * NG
VW = 2 * HS
LOWEST = -3.0e38


def in_register(engine, value):
    return value if isinstance(value, int) else engine.to_reg(value)


def project_qkv(nc, x, wqk, wv, bqk, bv2, rope_cos, rope_sin, ident, no_rows, pieces_d, v_d, slots_d):
    with ExitStack() as ctx:
        def sb(name, shape, dt=F32):
            return ctx.enter_context(nc.sbuf_tensor(name, shape, dt))

        def ps(name, shape, dt=F32):
            return ctx.enter_context(nc.psum_tensor(name, shape, dt))

        def sem(name):
            return ctx.enter_context(nc.semaphore(name))

        wqk_s = sb("wqk_s", [P, KT, 2 * C])
        wv_s = sb("wv_s", [P, KT, C])
        bqk_s = sb("bqk_s", [P, QKG])
        bv_s = sb("bv_s", [P, 2, C])
        cos_s = sb("cos_s", [P, T])
        sin_s = sb("sin_s", [P, T])
        id_s = sb("p1_id", [P, P])
        xin = [sb(f"xin{i}", [P, TPC, C]) for i in range(2)]
        xT = [sb(f"xT{i}", [P, KT, CHUNK]) for i in range(2)]
        raw = [sb(f"raw{i}", [P, QKG, CHUNK]) for i in range(2)]
        rot = [sb(f"rot{i}", [P, QKG, CHUNK]) for i in range(2)]
        rots = [sb(f"rots{i}", [P, QKG, CHUNK]) for i in range(2)]
        xcos = [sb(f"xcos{i}", [P, QKG, CHUNK]) for i in range(2)]
        hi = [sb(f"hi{i}", [P, QKG, CHUNK], BF16) for i in range(2)]
        mid = [sb(f"mid{i}", [P, QKG, CHUNK], BF16) for i in range(2)]
        low = [sb(f"low{i}", [P, QKG, CHUNK], BF16) for i in range(2)]
        vt = [sb(f"vt{i}", [P, TPC, H, VW]) for i in range(2)]
        psT = ps("psT", [P, KT, CHUNK])
        psP = ps("psP", [P, QKG, CHUNK])
        psV = ps("psV", [P, TPC, C])

        id_loaded = sem("id_loaded")
        wqk_loaded = sem("wqk_loaded")
        wv_loaded = sem("wv_loaded")
        rope_loaded = [sem(f"rope_loaded_{part}") for part in ("first", "rest")]
        x_loaded = [sem(f"x_loaded{i}") for i in range(2)]
        x_turned = [sem(f"x_turned{i}") for i in range(2)]
        xT_ready = sem("xT_ready")
        qk_projected = sem("qk_projected")
        v_projected = sem("v_projected")
        raw_ready = sem("raw_ready")
        rotated = sem("rotated")
        rot_scaled = sem("rot_scaled")
        cos_scaled = sem("cos_scaled")
        roped = sem("roped")
        hi_ready = sem("hi_ready")
        rest_ready = sem("rest_ready")
        mid_ready = sem("mid_ready")
        low_ready = sem("low_ready")
        ones_set = sem("ones_set")
        v_ready = sem("v_ready")
        slots_filled = sem("slots_filled")
        pieces_stored = [sem(f"pieces_stored{i}") for i in range(2)]
        v_stored = [sem(f"v_stored{i}") for i in range(2)]
        primed = (*pieces_stored, raw_ready, v_ready, xT_ready, *v_stored, *x_turned)

        block = ctx.enter_context(nc.Block())

        @block.sync
        def _(sp):
            for semaphore in primed:
                sp.sem_inc(semaphore, 1)

            def load_x(b, c):
                k = 2 * b + c // 2
                sp.wait_ge(x_turned[c % 2], 1 + k)
                sp.dma_start(xin[c % 2][:], x[b, c]).then_inc(x_loaded[c % 2], 16)

            def store(b, c):
                done = (NCH * b + c + 1)
                cols = slice(c * CHUNK, (c + 1) * CHUNK)
                sp.wait_ge(v_ready, 1 + 2 * done)
                sp.dma_start(v_d[b, c], vt[c % 2][:].rearrange("p t h w -> p t (h w)")).then_inc(v_stored[c % 2], 16)
                for n, (ready, piece) in enumerate(((hi_ready, hi), (mid_ready, mid), (low_ready, low))):
                    sp.wait_ge(ready, QKG * done)
                    sp.dma_start(pieces_d[b, n, :, :, cols], piece[c % 2][:]).then_inc(pieces_stored[c % 2], 16)

            sp.dma_start(id_s[:], ident).then_inc(id_loaded, 16)
            sp.dma_start(xin[0][:], x[0, 0]).then_inc(x_loaded[0], 16)
            sp.dma_start(wqk_s[:], wqk).then_inc(wqk_loaded, 16)
            sp.dma_start(bqk_s[:], bqk).then_inc(wqk_loaded, 16)
            for part, cols in enumerate((slice(0, CHUNK), slice(CHUNK, T))):
                sp.dma_start(cos_s[:, cols], rope_cos[:, cols]).then_inc(rope_loaded[part], 16)
                sp.dma_start(sin_s[:, cols], rope_sin[:, cols]).then_inc(rope_loaded[part], 16)
                if part == 0:
                    sp.dma_start(wv_s[:], wv).then_inc(wv_loaded, 16)
                    sp.dma_start(bv_s[:], bv2).then_inc(wv_loaded, 16)
                    sp.dma_start(xin[1][:], x[0, 1]).then_inc(x_loaded[1], 16)
            with sp.Fori(0, B - 1) as b:
                for c in range(NCH):
                    if c + 2 < NCH:
                        load_x(b, c + 2)
                    else:
                        load_x(b + 1, c + 2 - NCH)
                    store(b, c)
            sp.dma_start(slots_d, no_rows).then_inc(slots_filled, 16)
            for c in range(NCH):
                if c + 2 < NCH:
                    load_x(B - 1, c + 2)
                store(B - 1, c)
            sp.wait_ge(slots_filled, 16)
            for i in range(2):
                sp.wait_ge(pieces_stored[i], 1 + 16 * NPIECE * B * NCH // 2)
                sp.wait_ge(v_stored[i], 1 + 16 * B * NCH // 2)

        @block.tensor
        def _(pe):
            pe.wait_ge(id_loaded, 16)

            def turn(b, c):
                i, n = c % 2, NCH * b + c
                pe.wait_ge(x_loaded[i], 16 * (2 * b + c // 2 + 1))
                pe.wait_ge(xT_ready, 1 + KT * n)
                for kt in range(KT):
                    for t in range(TPC):
                        last = nc.tensor.transpose(psT[:, kt, t * P:(t + 1) * P],
                                                   xin[i][:, t, kt * P:(kt + 1) * P], id_s[:])
                last.then_inc(x_turned[i], 1)

            def project_qk(b, c):
                i, n = c % 2, NCH * b + c
                pe.wait_ge(xT_ready, 1 + KT * (n + 1))
                pe.wait_ge(raw_ready, 1 + QKG * n)
                for g in range(QKG):
                    for kt in range(KT):
                        last = nc.tensor.matmul(psP[:, g, :], wqk_s[:, kt, g * P:(g + 1) * P], xT[i][:, kt, :],
                                                start=(kt == 0), stop=(kt == KT - 1))
                    last.then_inc(qk_projected, 1)

            def project_v(b, c):
                i, n = c % 2, NCH * b + c
                pe.wait_ge(v_ready, 1 + 2 * n)
                for t in range(TPC):
                    for kt in range(KT):
                        last = nc.tensor.matmul(psV[:, t, :], xT[i][:, kt, t * P:(t + 1) * P], wv_s[:, kt, :],
                                                start=(kt == 0), stop=(kt == KT - 1))
                    if t % 2:
                        last.then_inc(v_projected, 1)

            def batch(b, last_one):
                for c in range(NCH):
                    project_qk(b, c)
                    if c + 1 < NCH:
                        turn(b, c + 1)
                    elif not last_one:
                        turn(b + 1, 0)
                    project_v(b, c)

            turn(0, 0)
            pe.wait_ge(wqk_loaded, 32)
            pe.wait_ge(wv_loaded, 32)
            with pe.Fori(0, B - 1) as b:
                batch(b, False)
            batch(B - 1, True)

        @block.scalar
        def _(act):
            def turn(b, c):
                i = c % 2
                act.wait_ge(x_turned[i], 1 + 2 * b + c // 2 + 1)
                for kt in range(KT):
                    nc.scalar.activation(xT[i][:, kt, :], psT[:, kt, :], ACT.Copy).then_inc(xT_ready, 1)

            def evacuate(b, c, g):
                i, n = c % 2, NCH * b + c
                act.wait_ge(qk_projected, QKG * n + g + 1)
                nc.scalar.activation(raw[i][:, g, :], psP[:, g, :], ACT.Identity,
                                     bias=bqk_s[:, g:g + 1]).then_inc(raw_ready, 1)

            def cut_hi(b, c, g):
                i, n = c % 2, NCH * b + c
                if g == 0:
                    act.wait_ge(pieces_stored[i], 1 + 16 * NPIECE * (2 * b + c // 2))
                act.wait_ge(roped, QKG * n + g + 1)
                nc.scalar.activation(hi[i][:, g, :], raw[i][:, g, :], ACT.Copy).then_inc(hi_ready, 1)

            def cut_mid(b, c, g):
                i, n = c % 2, NCH * b + c
                act.wait_ge(rest_ready, QKG * n + g + 1)
                nc.scalar.activation(mid[i][:, g, :], rots[i][:, g, :], ACT.Copy).then_inc(mid_ready, 1)

            def batch(b, last_one):
                for c in range(NCH):
                    evacuate(b, c, 0)
                    for g in range(QKG):
                        if g + 1 < QKG:
                            evacuate(b, c, g + 1)
                        elif c + 1 < NCH:
                            turn(b, c + 1)
                        elif not last_one:
                            turn(b + 1, 0)
                        cut_hi(b, c, g)
                        if g:
                            cut_mid(b, c, g - 1)
                    cut_mid(b, c, QKG - 1)

            turn(0, 0)
            act.wait_ge(wqk_loaded, 32)
            with act.Fori(0, B - 1) as b:
                batch(b, False)
            batch(B - 1, True)

        @block.vector
        def _(dve):
            for i in range(2):
                nc.vector.memset(vt[i][:], 1.0).then_inc(ones_set, 1)
            dve.wait_ge(ones_set, 2)
            dve.wait_ge(wv_loaded, 32)
            swap = [r ^ 1 for r in range(32)]

            def rope(b, c, g):
                i, n, cols = c % 2, NCH * b + c, slice(c * CHUNK, (c + 1) * CHUNK)
                done = QKG * n + g + 1
                raws = in_register(dve, 1 + done)
                dve.wait_ge(rope_loaded[min(c, 1)], 32)
                dve.wait_ge(raw_ready, raws)
                nc.vector.stream_shuffle(rot[i][:, g, :], raw[i][:, g, :], mask=swap).then_inc(rotated, 1)
                if g:
                    rest(b, c, g - 1)
                dve.wait_ge(rotated, done)
                nc.vector.tensor_tensor(rots[i][:, g, :], rot[i][:, g, :], sin_s[:, cols],
                                        ALU.mult).then_inc(rot_scaled, 1)
                dve.wait_ge(cos_scaled, done)
                dve.wait_ge(rot_scaled, done)
                nc.vector.tensor_tensor(raw[i][:, g, :], xcos[i][:, g, :], rots[i][:, g, :],
                                        ALU.add).then_inc(roped, 1)

            def rest(b, c, g):
                i, done = c % 2, QKG * (NCH * b + c) + g + 1
                dve.wait_ge(hi_ready, done)
                dve.wait_ge(roped, done)
                nc.vector.tensor_tensor(rots[i][:, g, :], raw[i][:, g, :], hi[i][:, g, :],
                                        ALU.subtract).then_inc(rest_ready, 1)

            with dve.Fori(0, B) as b:
                for c in range(NCH):
                    for g in range(QKG):
                        rope(b, c, g)
                    dve.wait_ge(v_stored[c % 2], 1 + 16 * (2 * b + c // 2))
                    for half in range(2):
                        dve.wait_ge(v_projected, 2 * (NCH * b + c) + half + 1)
                        tiles = slice(2 * half, 2 * half + 2)
                        nc.vector.tensor_tensor(vt[c % 2][:, tiles, :, 0:HS],
                                                psV[:, tiles, :].rearrange("p t (h d) -> p t h d", d=HS),
                                                bv_s[:].rearrange("p t (h d) -> p t h d", d=HS),
                                                ALU.add).then_inc(v_ready, 1)
                        if half == 0:
                            rest(b, c, QKG - 1)

        @block.gpsimd
        def _(pool):
            def scale_cos(b, c, g):
                i, n, cols = c % 2, NCH * b + c, slice(c * CHUNK, (c + 1) * CHUNK)
                done = in_register(pool, 1 + QKG * n + g + 1)
                pool.wait_ge(rope_loaded[min(c, 1)], 32)
                pool.wait_ge(raw_ready, done)
                nc.gpsimd.tensor_tensor(xcos[i][:, g, :], raw[i][:, g, :], cos_s[:, cols],
                                        ALU.mult).then_inc(cos_scaled, 1)

            def cut_low(b, c, g):
                i, n = c % 2, NCH * b + c
                pool.wait_ge(mid_ready, QKG * n + g + 1)
                nc.gpsimd.tensor_tensor(low[i][:, g, :], rots[i][:, g, :], mid[i][:, g, :],
                                        ALU.subtract).then_inc(low_ready, 1)

            with pool.Fori(0, B) as b:
                for c in range(NCH):
                    pool.wait_ge(pieces_stored[c % 2], 1 + 16 * NPIECE * (2 * b + c // 2))
                    for g in range(QKG):
                        scale_cos(b, c, g)
                        if g >= 2:
                            cut_low(b, c, g - 2)
                    for g in range(QKG - 2, QKG):
                        cut_low(b, c, g)


ORDER = range(NCH - 1, -1, -1)
STEPS = [(c, kb, max(0, kb * P - c * CHUNK)) for c in ORDER for kb in range(TPC * (c + 1))]
NSTEP = len(STEPS)
LAST = [max(n for n, s in enumerate(STEPS) if s[0] == c) for c in range(NCH)]
DIAG = [n for n, (c, kb, _) in enumerate(STEPS) if kb >= TPC * c]
NQT = T // P
MAXJOBS = [(i, t, j, min(CHUNK, (i + 1) * P - t * CHUNK), t == i // TPC)
           for t in ORDER for i in range(TPC * t, NQT) for j in range(HPU)]
NMAX = len(MAXJOBS)
NRING = NMAX + 2
assert NRING % 3 == 0 and NSTEP % 2 == 0
FIRST_MAX, END_MAX, TURN_AT = 1, 32, 34


def max_plan():
    steps = range(FIRST_MAX, END_MAX)
    width = [CHUNK - STEPS[n][2] for n in steps]
    total, jobs = sum(width), [w for *_, w, _ in MAXJOBS]
    plan, m, seen = {}, 0, 0
    for n, w in zip(steps, width):
        seen += w
        start = m
        while m < NMAX and sum(jobs[:m + 1]) <= seen / total * sum(jobs) + 1e-6:
            m += 1
        plan[n] = range(start, m)
    assert m == NMAX
    return plan


PLAN = max_plan()


def attention(nc, pieces_d, v_d, causal, ident16, o_d):
    with ExitStack() as ctx:
        def sb(name, shape, dt=F32):
            return ctx.enter_context(nc.sbuf_tensor(name, shape, dt))

        def sem(name):
            return ctx.enter_context(nc.semaphore(name))

        q_stack = [sb(f"q_stack{i}", [P, HPU, T], BF16) for i in range(2)]
        k_stack = [sb(f"k_stack{i}", [P, HPU, T], BF16) for i in range(2)]
        v_s = [sb(f"v_s{i}", [P, NQT, HPU * VW]) for i in range(2)]
        probs = [sb(f"probs{i}", [P, HPU, CHUNK]) for i in range(2)]
        o_s = [sb(f"o_s{i}", [P, CHUNK]) for i in range(2)]
        mask_s = sb("mask_s", [P, CHUNK])
        id16 = sb("id16", [P, P], BF16)
        scratch = sb("scratch", [P, HPU, CHUNK])
        part_max = sb("part_max", [P, NQT, HPU, NCH])
        row_max = sb("row_max", [P, HPU, NQT])
        max_rest = sb("max_rest", [P, HPU, NQT])
        max_pieces = sb("max_pieces", [P, HPU, NPIECE, NQT], BF16)
        max_rows = sb("max_rows", [P, 2, P], BF16)
        scores = [ctx.enter_context(nc.psum_tensor(f"scores{p}", [P, 2, CHUNK], F32)) for p in range(2)]
        ring = [ctx.enter_context(nc.psum_tensor(f"ring{i}", [P, CHUNK], F32)) for i in range(3)]
        out_p = ctx.enter_context(nc.psum_tensor("out_p", [P, CHUNK], F32))

        const_loaded = sem("const_loaded")
        ones_set = sem("ones_row_set")
        part_max_set = sem("part_max_set")
        stack_loaded = [[sem(f"stack{i}_loaded{c}") for c in range(NCH)] for i in range(2)]
        v_loaded = [sem(f"v_loaded{i}") for i in range(2)]
        scores_ready = [sem(f"scores_ready{p}") for p in range(2)]
        exp_done = [sem(f"exp_done{p}") for p in range(2)]
        masked = sem("masked")
        pv_done = [sem(f"pv_done{i}") for i in range(2)]
        o_copied = sem("o_copied")
        o_stored = [sem(f"o_stored{i}") for i in range(2)]
        ring_full = sem("ring_full")
        ring_read = sem("ring_read")
        fold = sem("fold")
        pieces_ready = sem("pieces_ready")
        max_loaded = [sem(f"max_loaded{i}") for i in range(2)]
        N_FOLD = 4

        primed = (o_copied, *o_stored, *pv_done)

        block = ctx.enter_context(nc.Block())

        @block.sync
        def _(sp):
            for semaphore in primed:
                sp.sem_inc(semaphore, 1)

            def load_chunk(b, g, i, c):
                cols = slice(c * CHUNK, (c + 1) * CHUNK)
                for r, (qp, kp) in enumerate(TERMS):
                    rows = slice(r * HS, (r + 1) * HS)
                    for stack, side, piece in ((q_stack, 0, qp), (k_stack, 1, kp)):
                        sp.dma_start(stack[i][rows, :, cols],
                                     pieces_d[b, piece, side, g, :, :, cols]).then_inc(stack_loaded[i][c], 16)

            def load_v(b, g, i):
                sp.dma_start(v_s[i][:], v_d[b, :, :, :, g]).then_inc(v_loaded[i], 16)

            def load_max(i):
                for j in range(HPU):
                    for pc in range(NPIECE):
                        at = (j % 2) * NPIECE * NQT + pc * NQT
                        sp.dma_start(q_stack[i][SROWS + pc:SROWS + pc + 1, j, :],
                                     max_rows[at:at + NQT, j // 2, :]).then_inc(max_loaded[i], 16)

            def store_o(u, b, g, c):
                copied = in_register(sp, 1 + NCH * u + NCH - c)
                sp.wait_ge(const_loaded, 32)
                sp.wait_ge(o_copied, copied)
                sp.dma_start(o_d[NCH * b + c, g], o_s[c % 2][:]).then_inc(o_stored[c % 2], 16)

            def unit(u, b, g, i, ahead, two_ahead):
                for c in ORDER:
                    if c == 1 and ahead:
                        sp.wait_ge(ring_read, NRING * (u + 2))
                        load_max(1 - i)
                    store_o(u, b, g, c)
                    if two_ahead:
                        load_chunk(two_ahead[0], two_ahead[1], i, c)
                if two_ahead:
                    load_v(two_ahead[0], two_ahead[1], i)

            sp.dma_start(mask_s[:], causal).then_inc(const_loaded, 16)
            sp.dma_start(id16[:], ident16).then_inc(const_loaded, 16)
            for i in range(2):
                for c in ORDER:
                    load_chunk(0, i, i, c)
                load_v(0, i, i)
            sp.wait_ge(ring_read, NRING)
            load_max(0)
            half = NG // 2
            with sp.Fori(0, half) as k:
                for i in range(2):
                    u = 2 * k + i
                    unit(u, 0, u, i, True, (k, 2 - 2 * k + i))
            with sp.Fori(0, half - 1) as k:
                for i in range(2):
                    unit(2 * k + NG + i, 1, 2 * k + i, i, True, (1, 2 * k + 2 + i))
            unit(UNITS - 2, B - 1, NG - 2, 0, True, None)
            unit(UNITS - 1, B - 1, NG - 1, 1, False, None)
            for i in range(2):
                sp.wait_ge(o_stored[i], 1 + 16 * UNITS * NCH // 2)

        @block.tensor
        def _(pe):
            def score_step(u, i, n, after=()):
                c, kb, off = STEPS[n]
                for p in range(2):
                    pe.wait_ge(exp_done[p], NSTEP * u + n)
                    for hh in range(2):
                        j = 2 * p + hh
                        last = nc.tensor.matmul(scores[p][:, hh, off:CHUNK],
                                                k_stack[i][0:KROWS, j, kb * P:(kb + 1) * P],
                                                q_stack[i][0:KROWS, j, c * CHUNK + off:(c + 1) * CHUNK],
                                                start=True, stop=True)
                    last.then_inc(scores_ready[p], 1)
                    if after:
                        after[p]()

            def pv_step(u, i, n):
                c, kb, off = STEPS[n]
                for p in range(2):
                    pe.wait_ge(exp_done[p], NSTEP * u + n + 1)
                if n in DIAG:
                    pe.wait_ge(masked, len(DIAG) * u + DIAG.index(n) + 1)
                if kb == 0:
                    pe.wait_ge(o_copied, 1 + NCH * u + NCH - 1 - c)
                for j in range(HPU):
                    last = nc.tensor.matmul(out_p[j * VW:(j + 1) * VW, off:CHUNK],
                                            v_s[i][:, kb, j * VW:(j + 1) * VW], probs[n % 2][:, j, off:CHUNK],
                                            start=(kb == 0), stop=(n == LAST[c]))
                last.then_inc(pv_done[n % 2], 1)

            def max_job(u, i, m):
                qt, t, j, w, _ = MAXJOBS[m]
                if not (isinstance(u, int) and u == 0 and m < 3):
                    pe.wait_ge(ring_read, NRING * u + m - 2)
                nc.tensor.matmul(ring[m % 3][:, 0:w], q_stack[i][0:SROWS, j, qt * P:(qt + 1) * P],
                                 k_stack[i][0:SROWS, j, t * CHUNK:t * CHUNK + w],
                                 start=True, stop=True).then_inc(ring_full, 1)

            def wait_chunk(i, m, uses):
                qt, t, j, _, _ = MAXJOBS[m]
                if (qt, j) == (TPC * t, 0):
                    pe.wait_ge(stack_loaded[i][t], 16 * 2 * NTERM * uses)

            def turn_maxima(u):
                pe.wait_ge(pieces_ready, u + 1)
                for s in range(2):
                    m = NMAX + s
                    pe.wait_ge(ring_read, NRING * u + m - 2)
                    nc.tensor.transpose(ring[m % 3][0:2 * NPIECE * NQT, 0:P // 2].bitcast(BF16),
                                        max_pieces[:, 2 * s:2 * s + 2].rearrange("p j c i -> p (j c i)"),
                                        id16[:]).then_inc(ring_full, 1)

            def unit(u, i, uses, ahead):
                def maxima(jobs):
                    for m in jobs:
                        wait_chunk(1 - i, m, uses[1])
                        max_job(u + 1, 1 - i, m)

                for n in range(1, NSTEP):
                    jobs = PLAN[n] if ahead and n in PLAN else range(0)
                    score_step(u, i, n, (lambda: maxima(jobs[0:1]), lambda: maxima(jobs[1:3])))
                    if n == 1:
                        pe.wait_ge(v_loaded[i], 16 * uses[0])
                    pv_step(u, i, n - 1)
                    maxima(jobs[3:])
                    if ahead and n == TURN_AT:
                        turn_maxima(u + 1)
                if ahead:
                    pe.wait_ge(max_loaded[1 - i], 16 * HPU * NPIECE * uses[1])
                    score_step(u + 1, 1 - i, 0)
                pv_step(u, i, NSTEP - 1)

            pe.wait_ge(const_loaded, 32)
            for m in range(NMAX):
                wait_chunk(0, m, 1)
                max_job(0, 0, m)
            turn_maxima(0)
            pe.wait_ge(ones_set, 2)
            pe.wait_ge(max_loaded[0], 16 * HPU * NPIECE)
            score_step(0, 0, 0)
            with pe.Fori(0, UNITS // 2 - 1) as k:
                unit(2 * k, 0, (k + 1, k + 1), True)
                unit(2 * k + 1, 1, (k + 1, k + 2), True)
            unit(UNITS - 2, 0, (UNITS // 2, UNITS // 2), True)
            unit(UNITS - 1, 1, (UNITS // 2, None), False)

        @block.scalar
        def _(act):
            def exp_step(u, n):
                off = STEPS[n][2]
                for p in range(2):
                    act.wait_ge(scores_ready[p], NSTEP * u + n + 1)
                    if p == 0:
                        act.wait_ge(pv_done[n % 2], 1 + (NSTEP // 2) * u + n // 2)
                    nc.scalar.activation(probs[n % 2][:, 2 * p:2 * p + 2, off:CHUNK], scores[p][:, :, off:CHUNK],
                                         ACT.Exp, scale=SCALE).then_inc(exp_done[p], 1)

            def copy_o(u, c):
                n = LAST[c]
                act.wait_ge(pv_done[n % 2], 1 + (NSTEP // 2) * u + n // 2 + 1)
                act.wait_ge(o_stored[c % 2], 1 + 16 * (2 * u + (NCH - 1 - c) // 2))
                nc.scalar.activation(o_s[c % 2][:], out_p[:], ACT.Copy).then_inc(o_copied, 1)

            def unit(u, ahead):
                for n in range(1, NSTEP):
                    exp_step(u, n)
                    for c in ORDER:
                        if n - 1 == LAST[c]:
                            copy_o(u, c)
                if ahead:
                    exp_step(u + 1, 0)
                copy_o(u, 0)

            exp_step(0, 0)
            with act.Fori(0, UNITS - 1) as u:
                unit(u, True)
            unit(UNITS - 1, False)

        @block.vector
        def _(dve):
            nc.vector.memset(part_max[:], LOWEST).then_inc(part_max_set, 1)
            dve.wait_ge(part_max_set, 1)
            dve.wait_ge(const_loaded, 32)

            def read_max(u, m):
                qt, t, j, w, diag = MAXJOBS[m]
                out = part_max[:, qt, j, t:t + 1]
                if diag:
                    full = in_register(dve, NRING * u + m + 1)
                    read = in_register(dve, NRING * u + m - 3)
                    dve.wait_ge(const_loaded, 32)
                    dve.wait_ge(ring_full, full)
                    if not (isinstance(u, int) and u == 0 and m < 4):
                        dve.wait_ge(ring_read, read)
                    nc.vector.tensor_tensor_reduce(out=scratch[:, j, 0:w], in0=ring[m % 3][:, 0:w],
                                                   in1=mask_s[:, CHUNK - w:CHUNK], scale=1.0, scalar=LOWEST,
                                                   op0=ALU.add, op1=ALU.max, accum_out=out).then_inc(ring_read, 1)
                else:
                    dve.wait_ge(ring_full, NRING * u + m + 1)
                    nc.vector.tensor_reduce(out, ring[m % 3][:, 0:w], axis=AX.X, op=ALU.max).then_inc(ring_read, 1)

            def fold_maxima(u):
                dve.wait_ge(ring_read, NRING * u + NMAX)
                nc.vector.tensor_reduce(row_max[:].rearrange("p j i -> p i j"), part_max[:], axis=AX.X,
                                        op=ALU.max).then_inc(fold, 1)
                dve.wait_ge(fold, N_FOLD * u + 1)
                nc.vector.tensor_scalar(max_pieces[:, :, 0, :], row_max[:], -1.0, None, ALU.mult).then_inc(fold, 1)
                dve.wait_ge(fold, N_FOLD * u + 2)
                nc.vector.scalar_tensor_tensor(max_rest[:], row_max[:], -1.0, max_pieces[:, :, 0, :],
                                               ALU.mult, ALU.subtract).then_inc(fold, 1)
                dve.wait_ge(fold, N_FOLD * u + 3)
                nc.vector.tensor_copy(max_pieces[:, :, 1, :], max_rest[:]).then_inc(fold, 1)
                dve.wait_ge(fold, N_FOLD * u + 4)
                nc.vector.tensor_tensor(max_pieces[:, :, 2, :], max_rest[:], max_pieces[:, :, 1, :],
                                        ALU.subtract).then_inc(pieces_ready, 1)
                for s in range(2):
                    m = NMAX + s
                    dve.wait_ge(ring_full, NRING * u + m + 1)
                    n = 2 * NPIECE * NQT
                    nc.vector.tensor_copy(max_rows[0:n, s, :],
                                          ring[m % 3][0:n, 0:P // 2].bitcast(BF16)).then_inc(ring_read, 1)

            for m in range(NMAX):
                read_max(0, m)
            fold_maxima(0)
            with dve.Fori(1, UNITS) as u:
                for m in range(NMAX):
                    read_max(u, m)
                fold_maxima(u)

        @block.gpsimd
        def _(pool):
            for i in range(2):
                nc.gpsimd.memset(k_stack[i][SROWS:KROWS], 1.0).then_inc(ones_set, 1)
            with pool.Fori(0, UNITS) as u:
                for d, n in enumerate(DIAG):
                    off = STEPS[n][2]
                    done = in_register(pool, NSTEP * u + n + 1)
                    pool.wait_ge(const_loaded, 32)
                    for p in range(2):
                        pool.wait_ge(exp_done[p], done)
                    block_ = probs[n % 2][:, :, off:off + P]
                    nc.gpsimd.affine_select(out=block_, in_=block_, compare_op=ALU.is_ge, fill=0.0, base=0,
                                            pattern=[[0, HPU], [1, P]], channel_multiplier=-1).then_inc(masked, 1)


RW = C + 4
PROB, TOKEN = C, C + 1
NOWHERE = 1.0e6
TILES = B * T // P
NBLK = CAP // P
FT = DFF // P
assert CAP == NBLK * P


def project_and_gate(nc, x, o_d, wproj, bproj, gate, ident, before, ones, prefer, slot_base, tok0, slots_d, out_d):
    with ExitStack() as ctx:
        def sb(name, shape, dt=F32):
            return ctx.enter_context(nc.sbuf_tensor(name, shape, dt))

        def ps(name, shape, dt=F32):
            return ctx.enter_context(nc.psum_tensor(name, shape, dt))

        def sem(name):
            return ctx.enter_context(nc.semaphore(name))

        wproj_s = sb("wproj_s", [P, KT, C])
        bproj_s = sb("bproj_s", [P, C])
        gate_s = sb("gate_s", [P, KT, E])
        id_s = sb("p3_id", [P, P])
        before_s = sb("before_s", [P, P], BF16)
        ones_s = sb("ones_s", [P, P], BF16)
        prefer_s = sb("prefer_s", [P, TPC, E])
        slot_base_s = sb("slot_base_s", [P, TPC, E])
        token_s = sb("token_s", [P, TPC])
        eps_s = sb("eps_s", [P, 1])
        primer = sb("p3_primer", [2, P])
        count_s = sb("count_s", [P, E])
        o_s = [sb(f"p3_o{i}", [P, NG, CHUNK]) for i in range(2)]
        x_s = [sb(f"p3_x{i}", [P, TPC, C]) for i in range(2)]
        xb = [sb(f"xb{i}", [P, TPC, C]) for i in range(2)]
        rden = [sb(f"rden{i}", [P, H]) for i in range(2)]
        y_s = [sb(f"y_s{i}", [P, H, HS]) for i in range(2)]
        yT = [sb(f"yT{i}", [P, KT, P]) for i in range(2)]
        res = [sb(f"res{i}", [P, TPC, C]) for i in range(2)]
        stats = [sb(f"stats{i}", [P, 6]) for i in range(2)]
        mv = [sb(f"mv{i}", [P, TPC, 2]) for i in range(2)]
        std = [sb(f"std{i}", [P, TPC]) for i in range(2)]
        rstd = [sb(f"rstd{i}", [P, TPC]) for i in range(2)]
        var1 = [sb(f"var1_{i}", [P, TPC]) for i in range(2)]
        var2 = [sb(f"var2_{i}", [P, TPC]) for i in range(2)]
        std2 = [sb(f"std2_{i}", [P, TPC]) for i in range(2)]
        rstd2 = [sb(f"rstd2_{i}", [P, TPC]) for i in range(2)]
        rows = [sb(f"rows{i}", [P, TPC, RW]) for i in range(2)]
        plain = [sb(f"plain{i}", [P, TPC, C]) for i in range(2)]
        x1T = sb("x1T", [P, KT, CHUNK])
        top = sb("top", [P, TPC])
        shifted = sb("shifted", [P, TPC, E])
        wanted = sb("wanted", [P, TPC, E])
        best = sb("best", [P, TPC])
        onehot = sb("onehot", [P, TPC, E], BF16)
        expd = sb("expd", [P, TPC, E])
        total = sb("total", [P, TPC])
        rank_all = sb("rank_all", [P, TPC, E])
        rank_own = sb("rank_own", [P, TPC, E])
        rank = sb("rank", [P, TPC])
        base_own = sb("base_own", [P, TPC, E])
        slot0 = sb("slot0", [P, TPC])
        dropped = sb("dropped", [P, TPC])
        slot1 = sb("slot1", [P, TPC])
        slot = [sb(f"slot_index{i}", [P, TPC], U32) for i in range(2)]
        psA = [ps(f"psA{i}", [P, CHUNK]) for i in range(2)]
        psB = ps("psB", [P, KT, P])
        psC = [ps(f"psC{i}", [P, CHUNK]) for i in range(2)]
        psD = ps("psD", [P, KT, CHUNK])
        psL = ps("psL", [P, CHUNK])
        logits = psL[:, 0:TPC * E].rearrange("p (t e) -> p t e", e=E)
        ranks = psL[:, 64:64 + TPC * E].rearrange("p (t e) -> p t e", e=E)
        counts = psL[:, 128:128 + E]

        w_loaded = sem("w3_loaded")
        set_up = sem("set_up")
        loaded = [sem(f"loaded{i}") for i in range(2)]
        o_turned = sem("o_turned")
        y_ready = sem("y_ready")
        y_turned = sem("y_turned")
        yT_ready = sem("yT_ready")
        projected = sem("projected")
        xb_ready = sem("xb_ready")
        res_ready = sem("res_ready")
        den_ready = sem("den_ready")
        stat_ready = sem("stat_ready")
        mv_ready = sem("mv_ready")
        std_ready = sem("std_ready")
        rstd_ready = sem("rstd_ready")
        var_step = sem("var_step")
        std2_ready = sem("std2_ready")
        rstd2_ready = sem("rstd2_ready")
        rows_ready = sem("rows_ready")
        plain_ready = sem("plain_ready")
        plain_stored = [sem(f"plain_stored{i}") for i in range(2)]
        x1_turned = sem("x1_turned")
        x1T_ready = sem("x1T_ready")
        logits_ready = sem("logits_ready")
        gate_step = sem("gate_step")
        shifted_ready = sem("shifted_ready")
        exp_ready = sem("exp_ready")
        onehot_ready = sem("onehot_ready")
        ranks_ready = sem("ranks_ready")
        slots_ready = sem("slots_ready")
        rows_sent = [sem(f"rows_sent{i}") for i in range(2)]
        NC3 = B * NCH
        n_w = 10
        N_GATE = 16

        primed = (plain_ready, *plain_stored, res_ready, slots_ready, yT_ready, y_ready)

        block = ctx.enter_context(nc.Block())

        @block.sync
        def _(sp):
            for semaphore in primed:
                sp.sem_inc(semaphore, 1)

            for dst, src in ((id_s, ident), (wproj_s, wproj), (bproj_s, bproj), (gate_s, gate), (before_s, before),
                             (ones_s, ones), (prefer_s, prefer), (slot_base_s, slot_base), (token_s, tok0)):
                sp.dma_start(dst[:], src).then_inc(w_loaded, 16)

            def load(n, i):
                sp.dma_start(o_s[i][:], o_d[n]).then_inc(loaded[i], 16)
                sp.dma_start(x_s[i][:], x[n]).then_inc(loaded[i], 16)

            def load_two_ahead(n, i):
                turned, summed = in_register(sp, TPC * (n + 1)), in_register(sp, n + 1)
                sp.wait_ge(w_loaded, 16 * (n_w - 1))
                sp.wait_ge(o_turned, turned)
                sp.wait_ge(xb_ready, summed)
                load(n + 2, i)

            def store(n, i):
                done = in_register(sp, 1 + TPC * (n + 1))
                sp.wait_ge(w_loaded, 16 * (n_w - 1))
                sp.wait_ge(plain_ready, done)
                sp.dma_start(out_d[n], plain[i][:]).then_inc(plain_stored[i], 16)

            load(0, 0)
            load(1, 1)
            load_two_ahead(0, 0)
            with sp.Fori(0, NC3 // 2 - 2) as k:
                for i in (1, 0):
                    n = 2 * k + 2 - i
                    load_two_ahead(n, i)
                    store(n - 1, 1 - i)
            load_two_ahead(NC3 - 3, 1)
            for n in range(NC3 - 4, NC3):
                store(n, n % 2)
            for i in range(2):
                sp.wait_ge(plain_stored[i], 1 + 16 * NC3 // 2)

        @block.tensor
        def _(pe):
            pe.wait_ge(w_loaded, 16 * (n_w - 1))

            def turn_o(n, i, h, t):
                if t == 0:
                    pe.wait_ge(loaded[i], 32 * (h + 1))
                pe.wait_ge(y_ready, 1 + TPC * n + t)
                for g in range(NG):
                    last = nc.tensor.transpose(psA[t % 2][:, g * P:(g + 1) * P], o_s[i][:, g, t * P:(t + 1) * P],
                                               id_s[:])
                last.then_inc(o_turned, 1)

            def project(n, t):
                m = TPC * n + t
                pe.wait_ge(y_ready, 1 + m + 1)
                pe.wait_ge(yT_ready, 1 + m)
                for kt in range(KT):
                    last = nc.tensor.transpose(psB[:, kt, :],
                                               y_s[t % 2][:].rearrange("p h d -> p (h d)")[:, kt * P:(kt + 1) * P],
                                               id_s[:])
                last.then_inc(y_turned, 1)
                pe.wait_ge(yT_ready, 1 + m + 1)
                pe.wait_ge(res_ready, 1 + m)
                for kt in range(KT):
                    last = nc.tensor.matmul(psC[t % 2][:, 0:C], yT[t % 2][:, kt, :], wproj_s[:, kt, :],
                                            start=(kt == 0), stop=(kt == KT - 1))
                last.then_inc(projected, 1)

            def turn_x1(n, i):
                pe.wait_ge(rows_ready, TPC * (n + 1))
                for kt in range(KT):
                    for t in range(TPC):
                        last = nc.tensor.transpose(psD[:, kt, t * P:(t + 1) * P],
                                                   rows[i][:, t, kt * P:(kt + 1) * P], id_s[:])
                last.then_inc(x1_turned, 1)

            def gate_logits(n):
                pe.wait_ge(x1T_ready, KT * (n + 1))
                pe.wait_ge(slots_ready, 1 + n)
                for t in range(TPC):
                    for kt in range(KT):
                        last = nc.tensor.matmul(logits[:, t, :], x1T[:, kt, t * P:(t + 1) * P], gate_s[:, kt, :],
                                                start=(kt == 0), stop=(kt == KT - 1))
                last.then_inc(logits_ready, 1)

            def rank_chunk(n):
                pe.wait_ge(onehot_ready, n + 1)
                nc.tensor.matmul(ranks[:], before_s[:], onehot[:], start=True, stop=False)
                for t in range(TPC - 1):
                    later = TPC - 1 - t
                    nc.tensor.matmul(ranks[:, t + 1:TPC, :], ones_s[:],
                                     onehot[:, t:t + 1, :].to_broadcast([P, later, E]),
                                     start=False, stop=(t == TPC - 2))
                for t in range(TPC):
                    last = nc.tensor.matmul(counts, ones_s[:], onehot[:, t, :], start=(t == 0), stop=(t == TPC - 1))
                last.then_inc(ranks_ready, 1)

            def both(n, i, h):
                turn_o(n, i, h, 0)
                turn_o(n, i, h, 1)
                project(n, 0)
                turn_x1(n - 1, 1 - i)
                turn_o(n, i, h, 2)
                project(n, 1)
                gate_logits(n - 1)
                turn_o(n, i, h, 3)
                project(n, 2)
                rank_chunk(n - 1)
                project(n, 3)

            turn_o(0, 0, 0, 0)
            for t in range(TPC):
                if t + 1 < TPC:
                    turn_o(0, 0, 0, t + 1)
                project(0, t)
            with pe.Fori(0, NC3 // 2 - 1) as k:
                both(2 * k + 1, 1, k)
                both(2 * k + 2, 0, k + 1)
            both(NC3 - 1, 1, NC3 // 2 - 1)
            turn_x1(NC3 - 1, 1)
            gate_logits(NC3 - 1)
            rank_chunk(NC3 - 1)

        @block.scalar
        def _(act):
            act.wait_ge(w_loaded, 16 * (n_w - 1))
            act.wait_ge(set_up, 2)

            def copy_yT(n, t):
                act.wait_ge(y_turned, TPC * n + t + 1)
                nc.scalar.activation(yT[t % 2][:], psB[:], ACT.Copy).then_inc(yT_ready, 1)

            def deviations(n, i):
                act.wait_ge(mv_ready, TPC * (n + 1))
                nc.scalar.activation(std[i][:], mv[i][:, :, 1], ACT.Sqrt, bias=eps_s[:]).then_inc(std_ready, 1)
                act.wait_ge(var_step, 2 * (n + 1))
                nc.scalar.activation(std2[i][:], var2[i][:], ACT.Sqrt, bias=eps_s[:]).then_inc(std2_ready, 1)

            def copy_x1T(n):
                act.wait_ge(x1_turned, n + 1)
                for kt in range(KT):
                    nc.scalar.activation(x1T[:, kt, :], psD[:, kt, :], ACT.Copy).then_inc(x1T_ready, 1)

            def exponentials(n):
                act.wait_ge(shifted_ready, n + 1)
                nc.scalar.activation(expd[:], shifted[:], ACT.Exp).then_inc(exp_ready, 1)

            def plain_rows(n, i, h):
                act.wait_ge(rstd2_ready, n + 1)
                act.wait_ge(plain_stored[i], 1 + 16 * h)
                for t in range(TPC):
                    nc.scalar.activation(plain[i][:, t, :], rows[i][:, t, 0:C], ACT.Copy,
                                         scale=rstd2[i][:, t:t + 1]).then_inc(plain_ready, 1)

            def both(n, i, h_before):
                copy_yT(n, 0)
                copy_x1T(n - 1)
                copy_yT(n, 1)
                copy_yT(n, 2)
                exponentials(n - 1)
                copy_yT(n, 3)
                plain_rows(n - 1, 1 - i, h_before)
                deviations(n, i)

            for t in range(TPC):
                copy_yT(0, t)
            deviations(0, 0)
            with act.Fori(0, NC3 // 2 - 1) as k:
                both(2 * k + 1, 1, k)
                both(2 * k + 2, 0, k)
            both(NC3 - 1, 1, NC3 // 2 - 1)
            copy_x1T(NC3 - 1)
            plain_rows(NC3 - 1, 1, NC3 // 2 - 1)
            exponentials(NC3 - 1)

        @block.vector
        def _(dve):
            nc.vector.memset(eps_s[:], EPS).then_inc(set_up, 1)
            nc.vector.memset(count_s[:], 0.0).then_inc(set_up, 1)
            for i in range(2):
                nc.vector.memset(rows[i][:, :, C:RW], 0.0).then_inc(set_up, 1)
            dve.wait_ge(set_up, 4)
            dve.wait_ge(w_loaded, 16 * (n_w - 1))

            def normalise(n, t):
                m = TPC * n + t
                heads = psA[t % 2][:].rearrange("p (h w) -> p h w", w=VW)
                dve.wait_ge(o_turned, m + 1)
                nc.vector.reciprocal(rden[t % 2][:], heads[:, :, HS]).then_inc(den_ready, 1)
                dve.wait_ge(den_ready, m + 1)
                nc.vector.tensor_tensor(y_s[t % 2][:], heads[:, :, 0:HS],
                                        rden[t % 2][:].unsqueeze(2).to_broadcast([P, H, HS]),
                                        ALU.mult).then_inc(y_ready, 1)

            def residual(n, i, t):
                m = TPC * n + t
                dve.wait_ge(projected, m + 1)
                if t == 0:
                    dve.wait_ge(xb_ready, n + 1)
                nc.vector.tensor_tensor(res[i][:, t, :], psC[t % 2][:, 0:C], xb[i][:, t, :],
                                        ALU.add).then_inc(res_ready, 1)
                dve.wait_ge(res_ready, 1 + m + 1)
                nc.vector.bn_stats(stats[t % 2][:], res[i][:, t, :]).then_inc(stat_ready, 1)
                done = in_register(dve, m + 1)
                dve.wait_ge(set_up, 4)
                dve.wait_ge(stat_ready, done)
                nc.vector.bn_aggr(mv[i][:, t, :], stats[t % 2][:]).then_inc(mv_ready, 1)

            def norm_chunk(n, i, h):
                dve.wait_ge(std_ready, n + 1)
                dve.wait_ge(mv_ready, TPC * (n + 1))
                nc.vector.reciprocal(rstd[i][:], std[i][:]).then_inc(rstd_ready, 1)
                dve.wait_ge(rstd_ready, n + 1)
                nc.vector.tensor_tensor(var1[i][:], mv[i][:, :, 1], rstd[i][:], ALU.mult).then_inc(var_step, 1)
                dve.wait_ge(var_step, 2 * n + 1)
                nc.vector.tensor_tensor(var2[i][:], var1[i][:], rstd[i][:], ALU.mult).then_inc(var_step, 1)
                dve.wait_ge(rows_sent[i], 16 + 16 * TPC * h)
                if not (isinstance(n, int) and n == 0):
                    dve.wait_ge(plain_ready, 1 + TPC * (n - 1))
                for t in range(TPC):
                    nc.vector.tensor_scalar(rows[i][:, t, 0:C], res[i][:, t, :], mv[i][:, t, 0:1],
                                            rstd[i][:, t:t + 1], ALU.subtract, ALU.mult).then_inc(rows_ready, 1)

            def norm_plain(n, i):
                dve.wait_ge(std2_ready, n + 1)
                nc.vector.reciprocal(rstd2[i][:], std2[i][:]).then_inc(rstd2_ready, 1)

            def then(n, step, instruction):
                instruction.then_inc(gate_step, 1)
                dve.wait_ge(gate_step, N_GATE * n + step)

            def per_tile(ap):
                return ap.unsqueeze(2).to_broadcast([P, TPC, E])

            def choose(n):
                dve.wait_ge(logits_ready, n + 1)
                then(n, 1, nc.vector.tensor_reduce(top[:], logits, axis=AX.X, op=ALU.max))
                nc.vector.tensor_tensor(shifted[:], logits, per_tile(top[:]), ALU.subtract).then_inc(shifted_ready, 1)
                dve.wait_ge(shifted_ready, n + 1)
                then(n, 2, nc.vector.scalar_tensor_tensor(wanted[:], shifted[:], 0.0, prefer_s[:],
                                                          ALU.is_equal, ALU.mult))
                then(n, 3, nc.vector.tensor_reduce(best[:], wanted[:], axis=AX.X, op=ALU.max))
                nc.vector.tensor_tensor(onehot[:], wanted[:], per_tile(best[:]), ALU.is_equal).then_inc(onehot_ready, 1)

            def place(n, i):
                dve.wait_ge(exp_ready, n + 1)
                then(n, 4, nc.vector.tensor_reduce(total[:], expd[:], axis=AX.X, op=ALU.add))
                then(n, 5, nc.vector.reciprocal(rows[i][:, :, PROB], total[:]))
                then(n, 6, nc.vector.tensor_copy(rows[i][:, :, TOKEN], token_s[:]))
                then(n, 7, nc.vector.tensor_scalar(token_s[:], token_s[:], float(CHUNK), None, ALU.add))
                dve.wait_ge(onehot_ready, n + 1)
                then(n, 8, nc.vector.tensor_tensor(base_own[:], onehot[:], slot_base_s[:], ALU.mult))
                then(n, 9, nc.vector.tensor_reduce(slot0[:], base_own[:], axis=AX.X, op=ALU.add))
                dve.wait_ge(ranks_ready, n + 1)
                then(n, 10, nc.vector.tensor_tensor(rank_all[:], ranks, count_s[:].unsqueeze(1).to_broadcast([P, TPC, E]),
                                                    ALU.add))
                then(n, 11, nc.vector.tensor_tensor(count_s[:], counts, count_s[:], ALU.add))
                then(n, 12, nc.vector.tensor_tensor(rank_own[:], rank_all[:], onehot[:], ALU.mult))
                then(n, 13, nc.vector.tensor_reduce(rank[:], rank_own[:], axis=AX.X, op=ALU.add))
                then(n, 14, nc.vector.tensor_scalar(dropped[:], rank[:], float(CAP), NOWHERE, ALU.is_ge, ALU.mult))
                then(n, 15, nc.vector.tensor_tensor(slot1[:], slot0[:], rank[:], ALU.add))
                then(n, 16, nc.vector.tensor_tensor(slot1[:], slot1[:], dropped[:], ALU.add))
                nc.vector.tensor_copy(slot[i][:], slot1[:]).then_inc(slots_ready, 1)

            def both(n, i, h):
                normalise(n, 0)
                norm_plain(n - 1, 1 - i)
                normalise(n, 1)
                residual(n, i, 0)
                normalise(n, 2)
                residual(n, i, 1)
                choose(n - 1)
                normalise(n, 3)
                residual(n, i, 2)
                residual(n, i, 3)
                place(n - 1, 1 - i)
                norm_chunk(n, i, h)

            normalise(0, 0)
            for t in range(TPC):
                if t + 1 < TPC:
                    normalise(0, t + 1)
                residual(0, 0, t)
            norm_chunk(0, 0, 0)
            with dve.Fori(0, NC3 // 2 - 1) as k:
                both(2 * k + 1, 1, k)
                both(2 * k + 2, 0, k + 1)
            both(NC3 - 1, 1, NC3 // 2 - 1)
            norm_plain(NC3 - 1, 1)
            choose(NC3 - 1)
            place(NC3 - 1, 1)

        @block.gpsimd
        def _(pool):
            for i in range(2):
                nc.gpsimd.dma_start(primer[i:i + 1, :], ident[i:i + 1, :]).then_inc(rows_sent[i], 16)
            pool.wait_ge(w_loaded, 16 * (n_w - 1))

            def add_bias(n, i, h):
                pool.wait_ge(loaded[i], 32 * (h + 1))
                if not (isinstance(n, int) and n == 0):
                    pool.wait_ge(res_ready, 1 + TPC * (n - 1))
                nc.gpsimd.tensor_tensor(xb[i][:], x_s[i][:], bproj_s[:].unsqueeze(1).to_broadcast([P, TPC, C]),
                                        ALU.add).then_inc(xb_ready, 1)

            def send(n, i):
                done = in_register(pool, 1 + (n + 1))
                pool.wait_ge(w_loaded, 16 * (n_w - 1))
                pool.wait_ge(slots_ready, done)
                for t in range(TPC):
                    nc.gpsimd.indirect_dma_start(
                        slots_d, bass.IndirectOffsetOnAxis(ap=slot[i][:, t:t + 1], axis=0),
                        rows[i][:, t, :], None, bounds_check=E * CAP - 1, oob_is_err=False,
                    ).then_inc(rows_sent[i], 16)

            add_bias(0, 0, 0)
            add_bias(1, 1, 0)
            with pool.Fori(0, NC3 // 2 - 1) as k:
                add_bias(2 * k + 2, 0, k + 1)
                send(2 * k, 0)
                add_bias(2 * k + 3, 1, k + 1)
                send(2 * k + 1, 1)
            for n in (NC3 - 2, NC3 - 1):
                send(n, n % 2)
            for i in range(2):
                pool.wait_ge(rows_sent[i], 16 + 16 * TPC * NC3 // 2)


def experts(nc, slots_d, w1, b1, w2, b2, ident, out_d):
    with ExitStack() as ctx:
        def sb(name, shape, dt=F32):
            return ctx.enter_context(nc.sbuf_tensor(name, shape, dt))

        def ps(name, shape, dt=F32):
            return ctx.enter_context(nc.psum_tensor(name, shape, dt))

        def sem(name):
            return ctx.enter_context(nc.semaphore(name))

        id_s = sb("p4_id", [P, P])
        eps_s = sb("p4_eps", [P, 1])
        primer = sb("p4_primer", [2, P])
        w1_s = [sb(f"w1_s{i}", [P, KT, DFF]) for i in range(2)]
        w2_s = [sb(f"w2_s{i}", [P, FT, C]) for i in range(2)]
        b1_s = [sb(f"b1_s{i}", [P, FT]) for i in range(2)]
        b2_s = [sb(f"b2_s{i}", [P, C]) for i in range(2)]
        xe = [sb(f"xe{i}", [P, NBLK, RW]) for i in range(2)]
        token = [sb(f"token{i}", [P, NBLK], U32) for i in range(2)]
        xeT = [sb(f"xeT{i}", [P, NBLK * KT, P]) for i in range(2)]
        hT = sb("hT", [P, FT, CAP])
        eo = [sb(f"eo{i}", [P, C]) for i in range(2)]
        z = [sb(f"z{i}", [P, C]) for i in range(2)]
        stats = [sb(f"p4_stats{i}", [P, 6]) for i in range(2)]
        mv = [sb(f"p4_mv{i}", [P, 2]) for i in range(2)]
        std = [sb(f"p4_std{i}", [P, 1]) for i in range(2)]
        rstd = [sb(f"p4_rstd{i}", [P, 1]) for i in range(2)]
        fin = [sb(f"fin{i}", [P, NBLK, C]) for i in range(2)]
        psX = [ps(f"psX{i}", [P, CHUNK]) for i in range(2)]
        psH = [ps(f"psH{i}", [P, CHUNK]) for i in range(4)]
        psY = [ps(f"psY{i}", [P, CHUNK]) for i in range(2)]
        PARTS = [(0, 3), (3, NBLK)]
        PAIRS = [(blk, kt) for blk in range(NBLK) for kt in range(KT)]
        TURNS = [PAIRS[k:k + 4] for k in range(0, len(PAIRS), 4)]
        NT = len(TURNS)

        const_loaded = sem("p4_const")
        eps_set = sem("p4_eps_set")
        w_loaded = [sem(f"p4_w{i}") for i in range(2)]
        xe_loaded = [sem(f"p4_xe{i}") for i in range(2)]
        turned = sem("turned")
        xeT_ready = sem("xeT_ready")
        h_ready = sem("h_ready")
        relu_done = sem("relu_done")
        y_done = sem("y_done")
        eo_ready = sem("eo_ready")
        z_ready = sem("z_ready")
        stat_ready = sem("p4_stat")
        mv_ready = sem("p4_mvr")
        std_ready = sem("p4_stdr")
        rstd_ready = sem("p4_rstdr")
        fin_ready = sem("fin_ready")
        token_ready = sem("token_ready")
        sent = [sem(f"sent{i}") for i in range(2)]

        block = ctx.enter_context(nc.Block())

        @block.sync
        def _(sp):
            def load_weights(e, i):
                for dst, src in ((w1_s, w1), (b1_s, b1), (w2_s, w2)):
                    sp.dma_start(dst[i][:], src[e]).then_inc(w_loaded[i], 16)

            def load_rows(e, i):
                sp.dma_start(xe[i][:], slots_d[e]).then_inc(xe_loaded[i], 16)
                sp.dma_start(b2_s[i][:], b2[e]).then_inc(xe_loaded[i], 16)

            sp.dma_start(id_s[:], ident).then_inc(const_loaded, 16)
            for e in range(2):
                load_rows(e, e)
                load_weights(e, e)
            with sp.Fori(0, E // 2 - 1) as k:
                for i in range(2):
                    e = 2 * k + i
                    sp.wait_ge(y_done, NBLK * (e + 1))
                    load_weights(e + 2, i)
                    sp.wait_ge(z_ready, NBLK * (e + 1))
                    load_rows(e + 2, i)

        @block.tensor
        def _(pe):
            def turn(e, i, uses):
                pe.wait_ge(xe_loaded[i], 32 * uses)
                for s, group in enumerate(TURNS):
                    if not (isinstance(e, int) and e == 0 and s < 2):
                        pe.wait_ge(xeT_ready, NT * e + s - 1)
                    for at, (blk, kt) in enumerate(group):
                        last = nc.tensor.transpose(psX[s % 2][:, at * P:(at + 1) * P],
                                                   xe[i][:, blk, kt * P:(kt + 1) * P], id_s[:])
                    last.then_inc(turned, 1)

            def up(e, i, uses):
                xv = xeT[i][:].rearrange("p (b k) q -> p b k q", k=KT)
                pe.wait_ge(w_loaded[i], 48 * uses)
                pe.wait_ge(xeT_ready, NT * (e + 1))
                for ft in range(FT):
                    if ft < 2:
                        pe.wait_ge(relu_done, 2 * FT * e)
                    else:
                        pe.wait_ge(relu_done, 2 * FT * e + 2 * (ft - 1))
                    for part, (b0, b1_) in enumerate(PARTS):
                        for kt in range(KT):
                            last = nc.tensor.matmul(psH[2 * (ft % 2) + part][:, 0:(b1_ - b0) * P],
                                                    w1_s[i][:, kt, ft * P:(ft + 1) * P], xv[:, b0:b1_, kt, :],
                                                    start=(kt == 0), stop=(kt == KT - 1))
                        last.then_inc(h_ready, 1)

            def down(e, i):
                pe.wait_ge(relu_done, 2 * FT * (e + 1))
                for blk in range(NBLK):
                    n = NBLK * e + blk
                    if not (isinstance(e, int) and e == 0 and blk < 1):
                        pe.wait_ge(eo_ready, n - 1)
                    for ft in range(FT):
                        last = nc.tensor.matmul(psY[blk % 2][:, 0:C], hT[:, ft, blk * P:(blk + 1) * P],
                                                w2_s[i][:, ft, :], start=(ft == 0), stop=(ft == FT - 1))
                    last.then_inc(y_done, 1)

            pe.wait_ge(const_loaded, 16)
            turn(0, 0, 1)
            up(0, 0, 1)
            turn(1, 1, 1)
            down(0, 0)
            with pe.Fori(0, E // 2 - 1) as k:
                for i in range(2):
                    e = 2 * k + 1 + i
                    up(e, 1 - i, k + 1 + i)
                    turn(e + 1, i, k + 2)
                    down(e, 1 - i)
            up(E - 1, 1, E // 2)
            down(E - 1, 1)

        @block.scalar
        def _(act):
            def take_turn(e, i):
                for s, group in enumerate(TURNS):
                    act.wait_ge(turned, NT * e + s + 1)
                    nc.scalar.activation(xeT[i][:, 4 * s:4 * s + len(group), :].rearrange("p a q -> p (a q)"),
                                         psX[s % 2][:, 0:len(group) * P], ACT.Copy).then_inc(xeT_ready, 1)

            def relu(e, i):
                for ft in range(FT):
                    for part, (b0, b1_) in enumerate(PARTS):
                        act.wait_ge(h_ready, 2 * (FT * e + ft) + part + 1)
                        nc.scalar.activation(hT[:, ft, b0 * P:b1_ * P], psH[2 * (ft % 2) + part][:, 0:(b1_ - b0) * P],
                                             ACT.Relu, bias=b1_s[i][:, ft:ft + 1]).then_inc(relu_done, 1)

            def deviation(e):
                for blk in range(NBLK):
                    act.wait_ge(mv_ready, NBLK * e + blk + 1)
                    nc.scalar.activation(std[blk % 2][:], mv[blk % 2][:, 1:2], ACT.Sqrt,
                                         bias=eps_s[:]).then_inc(std_ready, 1)

            act.wait_ge(eps_set, 1)
            take_turn(0, 0)
            relu(0, 0)
            take_turn(1, 1)
            deviation(0)
            with act.Fori(0, E // 2 - 1) as k:
                for i in range(2):
                    e = 2 * k + 1 + i
                    relu(e, 1 - i)
                    take_turn(e + 1, i)
                    deviation(e)
            relu(E - 1, 1)
            deviation(E - 1)

        @block.vector
        def _(dve):
            nc.vector.memset(eps_s[:], EPS).then_inc(eps_set, 1)

            def combine(e, i, blk, uses):
                n, h = NBLK * e + blk, blk % 2
                dve.wait_ge(y_done, n + 1)
                nc.vector.tensor_tensor(eo[h][:], psY[h][:, 0:C], b2_s[i][:], ALU.add).then_inc(eo_ready, 1)
                dve.wait_ge(eo_ready, n + 1)
                nc.vector.scalar_tensor_tensor(z[h][:], eo[h][:], xe[i][:, blk, PROB:PROB + 1],
                                               xe[i][:, blk, 0:C], ALU.mult, ALU.add).then_inc(z_ready, 1)
                dve.wait_ge(z_ready, n + 1)
                nc.vector.bn_stats(stats[h][:], z[h][:]).then_inc(stat_ready, 1)
                done = in_register(dve, n + 1)
                dve.wait_ge(eps_set, 1)
                dve.wait_ge(stat_ready, done)
                nc.vector.bn_aggr(mv[h][:], stats[h][:]).then_inc(mv_ready, 1)

            def norm(e, i, blk):
                n, h = NBLK * e + blk, blk % 2
                dve.wait_ge(std_ready, n + 1)
                nc.vector.reciprocal(rstd[h][:], std[h][:]).then_inc(rstd_ready, 1)
                dve.wait_ge(rstd_ready, n + 1)
                nc.vector.tensor_scalar(fin[i][:, blk, :], z[h][:], mv[h][:, 0:1], rstd[h][:, 0:1],
                                        ALU.subtract, ALU.mult).then_inc(fin_ready, 1)

            def expert(e, i, uses):
                dve.wait_ge(xe_loaded[i], 32 * uses)
                dve.wait_ge(sent[i], 16 + 16 * NBLK * (uses - 1))
                nc.vector.tensor_copy(token[i][:], xe[i][:, :, TOKEN]).then_inc(token_ready, 1)
                for blk in range(NBLK):
                    if blk:
                        combine(e, i, blk, uses)
                        norm(e, i, blk - 1)
                    else:
                        combine(e, i, blk, uses)
                norm(e, i, NBLK - 1)

            with dve.Fori(0, E // 2) as k:
                for i in range(2):
                    expert(2 * k + i, i, k + 1)

        @block.gpsimd
        def _(pool):
            for i in range(2):
                nc.gpsimd.dma_start(primer[i:i + 1, :], ident[i:i + 1, :]).then_inc(sent[i], 16)
            with pool.Fori(0, E // 2) as k:
                for i in range(2):
                    e = 2 * k + i
                    pool.wait_ge(token_ready, e + 1)
                    for blk in range(NBLK):
                        done = in_register(pool, NBLK * e + blk + 1)
                        pool.wait_ge(eps_set, 1)
                        pool.wait_ge(fin_ready, done)
                        nc.gpsimd.indirect_dma_start(
                            out_d, bass.IndirectOffsetOnAxis(ap=token[i][:, blk:blk + 1], axis=0),
                            fin[i][:, blk, :], None, bounds_check=B * T - 1, oob_is_err=False,
                        ).then_inc(sent[i], 16)
            for i in range(2):
                pool.wait_ge(sent[i], 16 + 16 * NBLK * (E // 2))


def constants():
    bf = mybir.dt.np(BF16)
    row = np.arange(P)
    pos = np.arange(T, dtype=np.float32)[None]
    theta = (1.0 / np.float32(10000.0) ** (2.0 * (row % HS // 2).astype(np.float32) / HS)).astype(np.float32)
    angle = pos * theta[:, None]
    sign = np.where(row % 2 == 0, -1.0, 1.0).astype(np.float32)[:, None]
    causal = np.zeros((P, CHUNK), np.float32)
    causal[:, CHUNK - P:] = np.where(row[:, None] >= row[None], 0.0, LOWEST)
    no_row = np.zeros((P, RW), np.float32)
    no_row[:, TOKEN] = NOWHERE
    eye = np.eye(P, dtype=np.float32)
    return {
        "rope_cos": np.cos(angle).astype(np.float32),
        "rope_sin": (np.sin(angle) * sign).astype(np.float32),
        "causal": causal,
        "no_row": no_row,
        "ident": eye,
        "ident16": eye.astype(bf),
        "before": (row[:, None] < row[None]).astype(bf),
        "ones16": np.ones((P, P), bf),
        "prefer": np.broadcast_to((E - np.arange(E)).astype(np.float32), (P, TPC, E)).copy(),
        "slot_base": np.broadcast_to((CAP * np.arange(E)).astype(np.float32), (P, TPC, E)).copy(),
        "tok0": (row[:, None] + P * np.arange(TPC)[None]).astype(np.float32),
    }


def program(nc, a, out, scratch):
    x = a["x"].rearrange("b (c t p) d -> b c p t d", t=TPC, p=P)
    pieces, v, o, slots = scratch
    project_qkv(nc, x, a["wqk"].rearrange("(k p) n -> p k n", p=P), a["wv"].rearrange("(k p) n -> p k n", p=P),
                a["bqk"], a["bv2"], a["rope_cos"], a["rope_sin"], a["ident"],
                a["no_row"].unsqueeze(1).to_broadcast([P, E * NBLK, RW]),
                pieces.rearrange("b n (g p) t -> b n p g t", p=P),
                v.rearrange("b (c t p) w -> b c p t w", t=TPC, p=P),
                slots.rearrange("(n p) w -> p n w", p=P))
    attention(nc, pieces.rearrange("b n (s g j d) t -> b n s g d j t", s=2, g=NG, j=HPU),
              v.rearrange("b (t p) (g w) -> b p t w g", p=P, g=NG), a["causal"], a["ident16"], o)
    project_and_gate(nc, x.rearrange("b c p t d -> (b c) p t d"), o.rearrange("n g p q -> n p g q"),
                     a["wproj"].rearrange("(k p) n -> p k n", p=P), a["bproj"],
                     a["gate"].rearrange("(k p) e -> p k e", p=P), a["ident"], a["before"], a["ones16"],
                     a["prefer"], a["slot_base"], a["tok0"], slots,
                     out.rearrange("b (c t p) d -> (b c) p t d", t=TPC, p=P))
    experts(nc, slots.rearrange("(e n p) w -> e p n w", e=E, p=P), a["w1"].rearrange("e (k p) n -> e p k n", p=P),
            a["b1"], a["w2"].rearrange("e (f p) n -> e p f n", p=P),
            a["b2"], a["ident"], out.rearrange("b t d -> (b t) d"))


def kernel(L0_attn_x, L0_attn_W_qkv, L0_attn_b_qkv, L0_attn_W_proj, L0_attn_b_proj, L0_ffn_gate_w,
           L0_ffn_w1, L0_ffn_b1, L0_ffn_w2, L0_ffn_b2):
    import concourse.bacc as bacc
    from concourse.bass_utils import run_bass_kernel_spmd

    w = np.asarray(L0_attn_W_qkv).reshape(C, H, 3, HS)
    bias = np.asarray(L0_attn_b_qkv).reshape(H, 3, HS)
    arrays = {
        "x": np.asarray(L0_attn_x),
        "wqk": w[:, :, 0:2].transpose(0, 2, 1, 3).reshape(C, 2 * C),
        "wv": w[:, :, 2].reshape(C, C),
        "bqk": bias[:, 0:2].transpose(1, 0, 2).reshape(QKG, P).T,
        "bv2": np.broadcast_to(bias[:, 2].reshape(C), (P, 2, C)),
        "wproj": np.asarray(L0_attn_W_proj),
        "bproj": np.broadcast_to(np.asarray(L0_attn_b_proj), (P, C)),
        "gate": np.asarray(L0_ffn_gate_w).T,
        "w1": np.asarray(L0_ffn_w1), "b1": np.asarray(L0_ffn_b1).reshape(E, FT, P).transpose(0, 2, 1), "w2": np.asarray(L0_ffn_w2),
        "b2": np.broadcast_to(np.asarray(L0_ffn_b2)[:, None, :], (E, P, C)),
        **constants(),
    }
    arrays = {k: np.ascontiguousarray(a) for k, a in arrays.items()}
    nc = bacc.Bacc("TRN2", target_bir_lowering=False, num_devices=1)
    a = {k: nc.dram_tensor(k, v.shape, mybir.dt.from_np(v.dtype), kind="ExternalInput").ap() for k, v in arrays.items()}
    out = nc.dram_tensor("out", [B, T, C], F32, kind="ExternalOutput").ap()
    scratch = [nc.dram_tensor(n, s, dt, kind="Internal").ap() for n, s, dt in (
        ("pieces_d", [B, NPIECE, 2 * C, T], BF16), ("v_d", [B, T, H * VW], F32),
        ("o_d", [B * NCH, NG, P, CHUNK], F32), ("slots_d", [E * CAP, RW], F32))]
    program(nc, a, out, scratch)
    return run_bass_kernel_spmd(nc, [arrays], core_ids=[0]).results[0]["out"]
```

```python
import math
from contextlib import ExitStack

import numpy as np

import concourse.bass as bass
from concourse import mybir

F32 = mybir.dt.float32
BF16 = mybir.dt.bfloat16
F32R = mybir.dt.float32r
U32 = mybir.dt.uint32
ALU = mybir.AluOpType
ACT = mybir.ActivationFunctionType
AX = mybir.AxisListType

P = 128
B, T, C, H = 2, 2048, 256, 16
HS = C // H
KT = C // P
E, DFF = 8, 1024
CAP = math.ceil(1.25 * B * T / E)
CHUNK = 512
NCH = T // CHUNK
TPC = CHUNK // P
QKG = 2 * C // P
SCALE = 1.0 / math.sqrt(HS)
EPS = 1e-5

TERMS = [(0, 0), (0, 1), (1, 0), (1, 1), (0, 2), (2, 0)]
NTERM = len(TERMS)
SROWS = NTERM * HS
NPIECE = 3
KROWS = SROWS + NPIECE
HPU = 4
NG = H // HPU
UNITS = B * NG
VW = 2 * HS
LOWEST = -3.0e38


def in_register(engine, value):
    return value if isinstance(value, int) else engine.to_reg(value)


def project_qkv(nc, x, wqk, wv, bqk, bv2, rope_cos, rope_sin, ident, no_rows, pieces_d, v_d, slots_d):
    with ExitStack() as ctx:
        def sb(name, shape, dt=F32):
            return ctx.enter_context(nc.sbuf_tensor(name, shape, dt))

        def ps(name, shape, dt=F32):
            return ctx.enter_context(nc.psum_tensor(name, shape, dt))

        def sem(name):
            return ctx.enter_context(nc.semaphore(name))

        wqk_s = sb("wqk_s", [P, KT, 2 * C])
        wv_s = sb("wv_s", [P, KT, C])
        bqk_s = sb("bqk_s", [P, QKG])
        bv_s = sb("bv_s", [P, 2, C])
        cos_s = sb("cos_s", [P, T])
        sin_s = sb("sin_s", [P, T])
        id_s = sb("p1_id", [P, P])
        xin = [sb(f"xin{i}", [P, TPC, C]) for i in range(2)]
        xT = [sb(f"xT{i}", [P, KT, CHUNK]) for i in range(2)]
        raw = [sb(f"raw{i}", [P, QKG, CHUNK]) for i in range(2)]
        rot = [sb(f"rot{i}", [P, QKG, CHUNK]) for i in range(2)]
        rots = [sb(f"rots{i}", [P, QKG, CHUNK]) for i in range(2)]
        xcos = [sb(f"xcos{i}", [P, QKG, CHUNK]) for i in range(2)]
        hi = [sb(f"hi{i}", [P, QKG, CHUNK], BF16) for i in range(2)]
        mid = [sb(f"mid{i}", [P, QKG, CHUNK], BF16) for i in range(2)]
        low = [sb(f"low{i}", [P, QKG, CHUNK], BF16) for i in range(2)]
        vt = [sb(f"vt{i}", [P, TPC, H, VW]) for i in range(2)]
        psT = ps("psT", [P, KT, CHUNK])
        psP = ps("psP", [P, QKG, CHUNK])
        psV = ps("psV", [P, TPC, C])

        id_loaded = sem("id_loaded")
        wqk_loaded = sem("wqk_loaded")
        wv_loaded = sem("wv_loaded")
        rope_loaded = [sem(f"rope_loaded_{part}") for part in ("first", "rest")]
        x_loaded = [sem(f"x_loaded{i}") for i in range(2)]
        x_turned = [sem(f"x_turned{i}") for i in range(2)]
        xT_ready = sem("xT_ready")
        qk_projected = sem("qk_projected")
        v_projected = sem("v_projected")
        raw_ready = sem("raw_ready")
        rotated = sem("rotated")
        rot_scaled = sem("rot_scaled")
        cos_scaled = sem("cos_scaled")
        roped = sem("roped")
        hi_ready = sem("hi_ready")
        rest_ready = sem("rest_ready")
        mid_ready = sem("mid_ready")
        low_ready = sem("low_ready")
        ones_set = sem("ones_set")
        v_ready = sem("v_ready")
        slots_filled = sem("slots_filled")
        pieces_stored = [sem(f"pieces_stored{i}") for i in range(2)]
        v_stored = [sem(f"v_stored{i}") for i in range(2)]
        primed = (*pieces_stored, raw_ready, v_ready, xT_ready, *v_stored, *x_turned)

        block = ctx.enter_context(nc.Block())

        @block.sync
        def _(sp):
            for semaphore in primed:
                sp.sem_inc(semaphore, 1)

            def load_x(b, c):
                k = 2 * b + c // 2
                sp.wait_ge(x_turned[c % 2], 1 + k)
                sp.dma_start(xin[c % 2][:], x[b, c]).then_inc(x_loaded[c % 2], 16)

            def store(b, c):
                done = (NCH * b + c + 1)
                cols = slice(c * CHUNK, (c + 1) * CHUNK)
                sp.wait_ge(v_ready, 1 + 2 * done)
                sp.dma_start(v_d[b, c], vt[c % 2][:].rearrange("p t h w -> p t (h w)")).then_inc(v_stored[c % 2], 16)
                for n, (ready, piece) in enumerate(((hi_ready, hi), (mid_ready, mid), (low_ready, low))):
                    sp.wait_ge(ready, QKG * done)
                    sp.dma_start(pieces_d[b, n, :, :, cols], piece[c % 2][:]).then_inc(pieces_stored[c % 2], 16)

            sp.dma_start(id_s[:], ident).then_inc(id_loaded, 16)
            sp.dma_start(xin[0][:], x[0, 0]).then_inc(x_loaded[0], 16)
            sp.dma_start(wqk_s[:], wqk).then_inc(wqk_loaded, 16)
            sp.dma_start(bqk_s[:], bqk).then_inc(wqk_loaded, 16)
            for part, cols in enumerate((slice(0, CHUNK), slice(CHUNK, T))):
                sp.dma_start(cos_s[:, cols], rope_cos[:, cols]).then_inc(rope_loaded[part], 16)
                sp.dma_start(sin_s[:, cols], rope_sin[:, cols]).then_inc(rope_loaded[part], 16)
                if part == 0:
                    sp.dma_start(wv_s[:], wv).then_inc(wv_loaded, 16)
                    sp.dma_start(bv_s[:], bv2).then_inc(wv_loaded, 16)
                    sp.dma_start(xin[1][:], x[0, 1]).then_inc(x_loaded[1], 16)
            with sp.Fori(0, B - 1) as b:
                for c in range(NCH):
                    if c + 2 < NCH:
                        load_x(b, c + 2)
                    else:
                        load_x(b + 1, c + 2 - NCH)
                    store(b, c)
            sp.dma_start(slots_d, no_rows).then_inc(slots_filled, 16)
            for c in range(NCH):
                if c + 2 < NCH:
                    load_x(B - 1, c + 2)
                store(B - 1, c)
            sp.wait_ge(slots_filled, 16)
            for i in range(2):
                sp.wait_ge(pieces_stored[i], 1 + 16 * NPIECE * B * NCH // 2)
                sp.wait_ge(v_stored[i], 1 + 16 * B * NCH // 2)

        @block.tensor
        def _(pe):
            pe.wait_ge(id_loaded, 16)

            def turn(b, c):
                i, n = c % 2, NCH * b + c
                pe.wait_ge(x_loaded[i], 16 * (2 * b + c // 2 + 1))
                pe.wait_ge(xT_ready, 1 + KT * n)
                for kt in range(KT):
                    for t in range(TPC):
                        last = nc.tensor.transpose(psT[:, kt, t * P:(t + 1) * P],
                                                   xin[i][:, t, kt * P:(kt + 1) * P], id_s[:])
                last.then_inc(x_turned[i], 1)

            def project_qk(b, c):
                i, n = c % 2, NCH * b + c
                pe.wait_ge(xT_ready, 1 + KT * (n + 1))
                pe.wait_ge(raw_ready, 1 + QKG * n)
                for g in range(QKG):
                    for kt in range(KT):
                        last = nc.tensor.matmul(psP[:, g, :], wqk_s[:, kt, g * P:(g + 1) * P], xT[i][:, kt, :],
                                                start=(kt == 0), stop=(kt == KT - 1))
                    last.then_inc(qk_projected, 1)

            def project_v(b, c):
                i, n = c % 2, NCH * b + c
                pe.wait_ge(v_ready, 1 + 2 * n)
                for t in range(TPC):
                    for kt in range(KT):
                        last = nc.tensor.matmul(psV[:, t, :], xT[i][:, kt, t * P:(t + 1) * P], wv_s[:, kt, :],
                                                start=(kt == 0), stop=(kt == KT - 1))
                    if t % 2:
                        last.then_inc(v_projected, 1)

            def batch(b, last_one):
                for c in range(NCH):
                    project_qk(b, c)
                    if c + 1 < NCH:
                        turn(b, c + 1)
                    elif not last_one:
                        turn(b + 1, 0)
                    project_v(b, c)

            turn(0, 0)
            pe.wait_ge(wqk_loaded, 32)
            pe.wait_ge(wv_loaded, 32)
            with pe.Fori(0, B - 1) as b:
                batch(b, False)
            batch(B - 1, True)

        @block.scalar
        def _(act):
            def turn(b, c):
                i = c % 2
                act.wait_ge(x_turned[i], 1 + 2 * b + c // 2 + 1)
                for kt in range(KT):
                    nc.scalar.activation(xT[i][:, kt, :], psT[:, kt, :], ACT.Copy).then_inc(xT_ready, 1)

            def evacuate(b, c, g):
                i, n = c % 2, NCH * b + c
                act.wait_ge(qk_projected, QKG * n + g + 1)
                nc.scalar.activation(raw[i][:, g, :], psP[:, g, :], ACT.Identity,
                                     bias=bqk_s[:, g:g + 1]).then_inc(raw_ready, 1)

            def cut_hi(b, c, g):
                i, n = c % 2, NCH * b + c
                if g == 0:
                    act.wait_ge(pieces_stored[i], 1 + 16 * NPIECE * (2 * b + c // 2))
                act.wait_ge(roped, QKG * n + g + 1)
                nc.scalar.activation(hi[i][:, g, :], raw[i][:, g, :], ACT.Copy).then_inc(hi_ready, 1)

            def cut_mid(b, c, g):
                i, n = c % 2, NCH * b + c
                act.wait_ge(rest_ready, QKG * n + g + 1)
                nc.scalar.activation(mid[i][:, g, :], rots[i][:, g, :], ACT.Copy).then_inc(mid_ready, 1)

            def batch(b, last_one):
                for c in range(NCH):
                    evacuate(b, c, 0)
                    for g in range(QKG):
                        if g + 1 < QKG:
                            evacuate(b, c, g + 1)
                        elif c + 1 < NCH:
                            turn(b, c + 1)
                        elif not last_one:
                            turn(b + 1, 0)
                        cut_hi(b, c, g)
                        if g:
                            cut_mid(b, c, g - 1)
                    cut_mid(b, c, QKG - 1)

            turn(0, 0)
            act.wait_ge(wqk_loaded, 32)
            with act.Fori(0, B - 1) as b:
                batch(b, False)
            batch(B - 1, True)

        @block.vector
        def _(dve):
            for i in range(2):
                nc.vector.memset(vt[i][:], 1.0).then_inc(ones_set, 1)
            dve.wait_ge(ones_set, 2)
            dve.wait_ge(wv_loaded, 32)
            swap = [r ^ 1 for r in range(32)]

            def rope(b, c, g):
                i, n, cols = c % 2, NCH * b + c, slice(c * CHUNK, (c + 1) * CHUNK)
                done = QKG * n + g + 1
                raws = in_register(dve, 1 + done)
                dve.wait_ge(rope_loaded[min(c, 1)], 32)
                dve.wait_ge(raw_ready, raws)
                nc.vector.stream_shuffle(rot[i][:, g, :], raw[i][:, g, :], mask=swap).then_inc(rotated, 1)
                if g:
                    rest(b, c, g - 1)
                dve.wait_ge(rotated, done)
                nc.vector.tensor_tensor(rots[i][:, g, :], rot[i][:, g, :], sin_s[:, cols],
                                        ALU.mult).then_inc(rot_scaled, 1)
                dve.wait_ge(cos_scaled, done)
                dve.wait_ge(rot_scaled, done)
                nc.vector.tensor_tensor(raw[i][:, g, :], xcos[i][:, g, :], rots[i][:, g, :],
                                        ALU.add).then_inc(roped, 1)

            def rest(b, c, g):
                i, done = c % 2, QKG * (NCH * b + c) + g + 1
                dve.wait_ge(hi_ready, done)
                dve.wait_ge(roped, done)
                nc.vector.tensor_tensor(rots[i][:, g, :], raw[i][:, g, :], hi[i][:, g, :],
                                        ALU.subtract).then_inc(rest_ready, 1)

            with dve.Fori(0, B) as b:
                for c in range(NCH):
                    for g in range(QKG):
                        rope(b, c, g)
                    dve.wait_ge(v_stored[c % 2], 1 + 16 * (2 * b + c // 2))
                    for half in range(2):
                        dve.wait_ge(v_projected, 2 * (NCH * b + c) + half + 1)
                        tiles = slice(2 * half, 2 * half + 2)
                        nc.vector.tensor_tensor(vt[c % 2][:, tiles, :, 0:HS],
                                                psV[:, tiles, :].rearrange("p t (h d) -> p t h d", d=HS),
                                                bv_s[:].rearrange("p t (h d) -> p t h d", d=HS),
                                                ALU.add).then_inc(v_ready, 1)
                        if half == 0:
                            rest(b, c, QKG - 1)

        @block.gpsimd
        def _(pool):
            def scale_cos(b, c, g):
                i, n, cols = c % 2, NCH * b + c, slice(c * CHUNK, (c + 1) * CHUNK)
                done = in_register(pool, 1 + QKG * n + g + 1)
                pool.wait_ge(rope_loaded[min(c, 1)], 32)
                pool.wait_ge(raw_ready, done)
                nc.gpsimd.tensor_tensor(xcos[i][:, g, :], raw[i][:, g, :], cos_s[:, cols],
                                        ALU.mult).then_inc(cos_scaled, 1)

            def cut_low(b, c, g):
                i, n = c % 2, NCH * b + c
                pool.wait_ge(mid_ready, QKG * n + g + 1)
                nc.gpsimd.tensor_tensor(low[i][:, g, :], rots[i][:, g, :], mid[i][:, g, :],
                                        ALU.subtract).then_inc(low_ready, 1)

            with pool.Fori(0, B) as b:
                for c in range(NCH):
                    pool.wait_ge(pieces_stored[c % 2], 1 + 16 * NPIECE * (2 * b + c // 2))
                    for g in range(QKG):
                        scale_cos(b, c, g)
                        if g >= 2:
                            cut_low(b, c, g - 2)
                    for g in range(QKG - 2, QKG):
                        cut_low(b, c, g)


ORDER = range(NCH - 1, -1, -1)
STEPS = [(c, kb, max(0, kb * P - c * CHUNK)) for c in ORDER for kb in range(TPC * (c + 1))]
NSTEP = len(STEPS)
LAST = [max(n for n, s in enumerate(STEPS) if s[0] == c) for c in range(NCH)]
DIAG = [n for n, (c, kb, _) in enumerate(STEPS) if kb >= TPC * c]
NQT = T // P
MAXJOBS = [(i, t, j, min(CHUNK, (i + 1) * P - t * CHUNK), t == i // TPC)
           for t in ORDER for i in range(TPC * t, NQT) for j in range(HPU)]
NMAX = len(MAXJOBS)
TURNED = (slice(0, 2), slice(2, 4))
NRING = NMAX + 2
assert NRING % 3 == 0 and NSTEP % 2 == 0
EARLY, FIRST_MAX, END_MAX, TURN_AT = 20, 1, 33, 35
EARLY_EACH = 4


def max_plan():
    steps = range(FIRST_MAX, END_MAX)
    width = [CHUNK - STEPS[n][2] for n in steps]
    total, jobs = sum(width), [w for *_, w, _ in MAXJOBS]
    plan, m, seen, early = {}, EARLY, 0, sum(jobs[:EARLY])
    for n, w in zip(steps, width):
        seen += w
        start = m
        while m < NMAX and sum(jobs[:m + 1]) - early <= seen / total * (sum(jobs) - early) + 1e-6:
            m += 1
        plan[n] = range(start, m)
    assert m == NMAX
    return plan


PLAN = max_plan()
EARLY_PLAN = {n: range(min(EARLY, EARLY_EACH * k), min(EARLY, EARLY_EACH * (k + 1)))
              for k, n in enumerate(range(TURN_AT, NSTEP))}
EARLY_REST = range(min(EARLY, EARLY_EACH * (NSTEP - TURN_AT)), EARLY)


def attention(nc, pieces_d, v_d, causal, ident16, o_d):
    with ExitStack() as ctx:
        def sb(name, shape, dt=F32):
            return ctx.enter_context(nc.sbuf_tensor(name, shape, dt))

        def sem(name):
            return ctx.enter_context(nc.semaphore(name))

        q_stack = [sb(f"q_stack{i}", [P, HPU, T], BF16) for i in range(2)]
        k_stack = [sb(f"k_stack{i}", [P, HPU, T], BF16) for i in range(2)]
        v_s = [sb(f"v_s{i}", [P, NQT, HPU * VW]) for i in range(2)]
        probs = [sb(f"probs{i}", [P, HPU, CHUNK]) for i in range(2)]
        o_s = [sb(f"o_s{i}", [P, CHUNK]) for i in range(2)]
        mask_s = sb("mask_s", [P, CHUNK])
        id16 = sb("id16", [P, P], BF16)
        scratch = sb("scratch", [P, HPU, CHUNK])
        part_max = sb("part_max", [P, NQT, HPU, NCH])
        row_max = sb("row_max", [P, HPU, NQT])
        max_rest = sb("max_rest", [P, HPU, NQT])
        max_pieces = sb("max_pieces", [P, NPIECE + 1, HPU, NQT], BF16)
        max_rows = sb("max_rows", [P, 2, P], BF16)
        scores = [ctx.enter_context(nc.psum_tensor(f"scores{p}", [P, 2, CHUNK], F32)) for p in range(2)]
        ring = [ctx.enter_context(nc.psum_tensor(f"ring{i}", [P, CHUNK], F32)) for i in range(3)]
        out_p = ctx.enter_context(nc.psum_tensor("out_p", [P, CHUNK], F32))

        const_loaded = sem("const_loaded")
        ones_set = sem("ones_row_set")
        maxima_set = sem("maxima_set")
        stack_loaded = [[sem(f"stack{i}_loaded{c}") for c in range(NCH)] for i in range(2)]
        v_loaded = [sem(f"v_loaded{i}") for i in range(2)]
        scores_ready = [sem(f"scores_ready{p}") for p in range(2)]
        exp_done = [sem(f"exp_done{p}") for p in range(2)]
        masked = sem("masked")
        pv_done = [sem(f"pv_done{i}") for i in range(2)]
        o_copied = sem("o_copied")
        o_stored = [sem(f"o_stored{i}") for i in range(2)]
        ring_full = sem("ring_full")
        ring_read = sem("ring_read")
        fold = sem("fold")
        pieces_ready = sem("pieces_ready")
        max_loaded = [sem(f"max_loaded{i}") for i in range(2)]
        N_FOLD = 4

        primed = (o_copied, *o_stored, *pv_done)

        block = ctx.enter_context(nc.Block())

        @block.sync
        def _(sp):
            for semaphore in primed:
                sp.sem_inc(semaphore, 1)

            def load_chunk(b, g, i, c):
                cols = slice(c * CHUNK, (c + 1) * CHUNK)
                for r, (qp, kp) in enumerate(TERMS):
                    rows = slice(r * HS, (r + 1) * HS)
                    for stack, side, piece in ((q_stack, 0, qp), (k_stack, 1, kp)):
                        sp.dma_start(stack[i][rows, :, cols],
                                     pieces_d[b, piece, side, g, :, :, cols]).then_inc(stack_loaded[i][c], 16)

            def load_v(b, g, i):
                sp.dma_start(v_s[i][:], v_d[b, :, :, :, g]).then_inc(v_loaded[i], 16)

            def load_max(i):
                for pc in range(NPIECE):
                    at = (pc % 2) * HPU * NQT
                    sp.dma_start(q_stack[i][SROWS + pc:SROWS + pc + 1],
                                 max_rows[at:at + HPU * NQT, pc // 2, :]).then_inc(max_loaded[i], 16)

            def store_o(u, b, g, c):
                copied = in_register(sp, 1 + NCH * u + NCH - c)
                sp.wait_ge(const_loaded, 32)
                sp.wait_ge(o_copied, copied)
                sp.dma_start(o_d[NCH * b + c, g], o_s[c % 2][:]).then_inc(o_stored[c % 2], 16)

            def unit(u, b, g, i, ahead, two_ahead):
                for c in ORDER:
                    if c == 1 and ahead:
                        sp.wait_ge(ring_read, NRING * (u + 2))
                        load_max(1 - i)
                    store_o(u, b, g, c)
                    if two_ahead:
                        load_chunk(two_ahead[0], two_ahead[1], i, c)
                if two_ahead:
                    load_v(two_ahead[0], two_ahead[1], i)

            sp.dma_start(mask_s[:], causal).then_inc(const_loaded, 16)
            sp.dma_start(id16[:], ident16).then_inc(const_loaded, 16)
            for i in range(2):
                for c in ORDER:
                    load_chunk(0, i, i, c)
                load_v(0, i, i)
            sp.wait_ge(ring_read, NRING)
            load_max(0)
            half = NG // 2
            with sp.Fori(0, half) as k:
                for i in range(2):
                    u = 2 * k + i
                    unit(u, 0, u, i, True, (k, 2 - 2 * k + i))
            with sp.Fori(0, half - 1) as k:
                for i in range(2):
                    unit(2 * k + NG + i, 1, 2 * k + i, i, True, (1, 2 * k + 2 + i))
            unit(UNITS - 2, B - 1, NG - 2, 0, True, None)
            unit(UNITS - 1, B - 1, NG - 1, 1, False, None)
            for i in range(2):
                sp.wait_ge(o_stored[i], 1 + 16 * UNITS * NCH // 2)

        @block.tensor
        def _(pe):
            def score_step(u, i, n, after=()):
                c, kb, off = STEPS[n]
                for p in range(2):
                    pe.wait_ge(exp_done[p], NSTEP * u + n)
                    for hh in range(2):
                        j = 2 * p + hh
                        last = nc.tensor.matmul(scores[p][:, hh, off:CHUNK],
                                                k_stack[i][0:KROWS, j, kb * P:(kb + 1) * P],
                                                q_stack[i][0:KROWS, j, c * CHUNK + off:(c + 1) * CHUNK],
                                                start=True, stop=True)
                    last.then_inc(scores_ready[p], 1)
                    if after:
                        after[p]()

            def pv_step(u, i, n):
                c, kb, off = STEPS[n]
                for p in range(2):
                    pe.wait_ge(exp_done[p], NSTEP * u + n + 1)
                if n in DIAG:
                    pe.wait_ge(masked, len(DIAG) * u + DIAG.index(n) + 1)
                if kb == 0:
                    pe.wait_ge(o_copied, 1 + NCH * u + NCH - 1 - c)
                for j in range(HPU):
                    last = nc.tensor.matmul(out_p[j * VW:(j + 1) * VW, off:CHUNK],
                                            v_s[i][:, kb, j * VW:(j + 1) * VW], probs[n % 2][:, j, off:CHUNK],
                                            start=(kb == 0), stop=(n == LAST[c]))
                last.then_inc(pv_done[n % 2], 1)

            def max_job(u, i, m):
                qt, t, j, w, _ = MAXJOBS[m]
                if not (isinstance(u, int) and u == 0 and m < 3):
                    pe.wait_ge(ring_read, NRING * u + m - 2)
                nc.tensor.matmul(ring[m % 3][:, 0:w], q_stack[i][0:SROWS, j, qt * P:(qt + 1) * P],
                                 k_stack[i][0:SROWS, j, t * CHUNK:t * CHUNK + w],
                                 start=True, stop=True).then_inc(ring_full, 1)

            def wait_chunk(i, m, uses):
                qt, t, j, _, _ = MAXJOBS[m]
                if (qt, j) == (TPC * t, 0):
                    pe.wait_ge(stack_loaded[i][t], 16 * 2 * NTERM * uses)

            def turn_maxima(u):
                pe.wait_ge(pieces_ready, u + 1)
                for s, pieces in enumerate(TURNED):
                    m = NMAX + s
                    pe.wait_ge(ring_read, NRING * u + m - 2)
                    nc.tensor.transpose(ring[m % 3][:, 0:P // 2].bitcast(BF16),
                                        max_pieces[:, pieces].rearrange("p c j i -> p (c j i)"),
                                        id16[:]).then_inc(ring_full, 1)

            def maxima(u, i, uses, jobs):
                for m in jobs:
                    wait_chunk(i, m, uses)
                    max_job(u, i, m)

            def unit(u, i, uses, ahead):
                for n in range(1, NSTEP):
                    if ahead and n == TURN_AT:
                        turn_maxima(u + 1)
                    if ahead == 2 and n in EARLY_PLAN:
                        unit_, i_, uses_, jobs = u + 2, i, uses[0] + 1, EARLY_PLAN[n]
                    else:
                        unit_, i_, uses_, jobs = u + 1, 1 - i, uses[1], PLAN[n] if ahead and n in PLAN else range(0)
                    score_step(u, i, n, (lambda: maxima(unit_, i_, uses_, jobs[0:1]),
                                         lambda: maxima(unit_, i_, uses_, jobs[1:3])))
                    if n == 1:
                        pe.wait_ge(v_loaded[i], 16 * uses[0])
                    pv_step(u, i, n - 1)
                    maxima(unit_, i_, uses_, jobs[3:])
                if ahead == 2:
                    maxima(u + 2, i, uses[0] + 1, EARLY_REST)
                if ahead:
                    pe.wait_ge(max_loaded[1 - i], 16 * NPIECE * uses[1])
                    score_step(u + 1, 1 - i, 0)
                pv_step(u, i, NSTEP - 1)

            pe.wait_ge(const_loaded, 32)
            maxima(0, 0, 1, range(NMAX))
            turn_maxima(0)
            maxima(1, 1, 1, range(EARLY))
            pe.wait_ge(ones_set, 2)
            pe.wait_ge(max_loaded[0], 16 * NPIECE)
            score_step(0, 0, 0)
            with pe.Fori(0, UNITS // 2 - 1) as k:
                unit(2 * k, 0, (k + 1, k + 1), 2)
                unit(2 * k + 1, 1, (k + 1, k + 2), 2)
            unit(UNITS - 2, 0, (UNITS // 2, UNITS // 2), 1)
            unit(UNITS - 1, 1, (UNITS // 2, None), 0)

        @block.scalar
        def _(act):
            def exp_step(u, n):
                off = STEPS[n][2]
                for p in range(2):
                    act.wait_ge(scores_ready[p], NSTEP * u + n + 1)
                    if p == 0:
                        act.wait_ge(pv_done[n % 2], 1 + (NSTEP // 2) * u + n // 2)
                    nc.scalar.activation(probs[n % 2][:, 2 * p:2 * p + 2, off:CHUNK], scores[p][:, :, off:CHUNK],
                                         ACT.Exp, scale=SCALE).then_inc(exp_done[p], 1)

            def copy_o(u, c):
                n = LAST[c]
                act.wait_ge(pv_done[n % 2], 1 + (NSTEP // 2) * u + n // 2 + 1)
                act.wait_ge(o_stored[c % 2], 1 + 16 * (2 * u + (NCH - 1 - c) // 2))
                nc.scalar.activation(o_s[c % 2][:], out_p[:], ACT.Copy).then_inc(o_copied, 1)

            def unit(u, ahead):
                for n in range(1, NSTEP):
                    exp_step(u, n)
                    for c in ORDER:
                        if n - 1 == LAST[c]:
                            copy_o(u, c)
                if ahead:
                    exp_step(u + 1, 0)
                copy_o(u, 0)

            exp_step(0, 0)
            with act.Fori(0, UNITS - 1) as u:
                unit(u, True)
            unit(UNITS - 1, False)

        @block.vector
        def _(dve):
            nc.vector.memset(part_max[:], LOWEST).then_inc(maxima_set, 1)
            nc.vector.memset(max_pieces[:], 0.0).then_inc(maxima_set, 1)
            dve.wait_ge(maxima_set, 2)
            dve.wait_ge(const_loaded, 32)

            def read_max(u, m):
                qt, t, j, w, diag = MAXJOBS[m]
                out = part_max[:, qt, j, t:t + 1]
                if diag:
                    full = in_register(dve, NRING * u + m + 1)
                    read = in_register(dve, NRING * u + m - 3)
                    dve.wait_ge(const_loaded, 32)
                    dve.wait_ge(ring_full, full)
                    if not (isinstance(u, int) and u == 0 and m < 4):
                        dve.wait_ge(ring_read, read)
                    nc.vector.tensor_tensor_reduce(out=scratch[:, j, 0:w], in0=ring[m % 3][:, 0:w],
                                                   in1=mask_s[:, CHUNK - w:CHUNK], scale=1.0, scalar=LOWEST,
                                                   op0=ALU.add, op1=ALU.max, accum_out=out).then_inc(ring_read, 1)
                else:
                    dve.wait_ge(ring_full, NRING * u + m + 1)
                    nc.vector.tensor_reduce(out, ring[m % 3][:, 0:w], axis=AX.X, op=ALU.max).then_inc(ring_read, 1)

            def fold_maxima(u):
                dve.wait_ge(ring_read, NRING * u + NMAX)
                nc.vector.tensor_reduce(row_max[:].rearrange("p j i -> p i j"), part_max[:], axis=AX.X,
                                        op=ALU.max).then_inc(fold, 1)
                dve.wait_ge(fold, N_FOLD * u + 1)
                nc.vector.tensor_scalar(max_pieces[:, 0], row_max[:], -1.0, None, ALU.mult).then_inc(fold, 1)
                dve.wait_ge(fold, N_FOLD * u + 2)
                nc.vector.scalar_tensor_tensor(max_rest[:], row_max[:], -1.0, max_pieces[:, 0],
                                               ALU.mult, ALU.subtract).then_inc(fold, 1)
                dve.wait_ge(fold, N_FOLD * u + 3)
                nc.vector.tensor_copy(max_pieces[:, 1], max_rest[:]).then_inc(fold, 1)
                dve.wait_ge(fold, N_FOLD * u + 4)
                nc.vector.tensor_tensor(max_pieces[:, 2], max_rest[:], max_pieces[:, 1],
                                        ALU.subtract).then_inc(pieces_ready, 1)
                for s in range(2):
                    m = NMAX + s
                    dve.wait_ge(ring_full, NRING * u + m + 1)
                    nc.vector.tensor_copy(max_rows[:, s, :],
                                          ring[m % 3][:, 0:P // 2].bitcast(BF16)).then_inc(ring_read, 1)

            for m in range(NMAX):
                read_max(0, m)
            fold_maxima(0)
            with dve.Fori(1, UNITS) as u:
                for m in range(NMAX):
                    read_max(u, m)
                fold_maxima(u)

        @block.gpsimd
        def _(pool):
            for i in range(2):
                nc.gpsimd.memset(k_stack[i][SROWS:KROWS], 1.0).then_inc(ones_set, 1)
            with pool.Fori(0, UNITS) as u:
                for d, n in enumerate(DIAG):
                    off = STEPS[n][2]
                    done = in_register(pool, NSTEP * u + n + 1)
                    pool.wait_ge(const_loaded, 32)
                    for p in range(2):
                        pool.wait_ge(exp_done[p], done)
                    block_ = probs[n % 2][:, :, off:off + P]
                    nc.gpsimd.affine_select(out=block_, in_=block_, compare_op=ALU.is_ge, fill=0.0, base=0,
                                            pattern=[[0, HPU], [1, P]], channel_multiplier=-1).then_inc(masked, 1)


RW = C + 4
PROB, TOKEN = C, C + 1
NOWHERE = 1.0e6
TILES = B * T // P
NBLK = CAP // P
FT = DFF // P
assert CAP == NBLK * P


def project_and_gate(nc, x, o_d, wproj, bproj, gate, ident, before, ones, prefer, slot_base, tok0, slots_d, out_d,
                     w_whole, w_first):
    with ExitStack() as ctx:
        def sb(name, shape, dt=F32):
            return ctx.enter_context(nc.sbuf_tensor(name, shape, dt))

        def ps(name, shape, dt=F32):
            return ctx.enter_context(nc.psum_tensor(name, shape, dt))

        def sem(name):
            return ctx.enter_context(nc.semaphore(name))

        wproj_s = sb("wproj_s", [P, KT, C])
        bproj_s = sb("bproj_s", [P, C])
        gate_s = sb("gate_s", [P, KT, E])
        id_s = sb("p3_id", [P, P])
        before_s = sb("before_s", [P, P], BF16)
        ones_s = sb("ones_s", [P, P], BF16)
        prefer_s = sb("prefer_s", [P, TPC, E])
        slot_base_s = sb("slot_base_s", [P, TPC, E])
        token_s = sb("token_s", [P, TPC])
        eps_s = sb("eps_s", [P, 1])
        primer = sb("p3_primer", [2, P])
        count_s = sb("count_s", [P, E])
        o_s = [sb(f"p3_o{i}", [P, NG, CHUNK]) for i in range(2)]
        x_s = [sb(f"p3_x{i}", [P, TPC, C]) for i in range(2)]
        xb = [sb(f"xb{i}", [P, TPC, C]) for i in range(2)]
        rden = [sb(f"rden{i}", [P, H]) for i in range(2)]
        y_s = [sb(f"y_s{i}", [P, H, HS]) for i in range(2)]
        yT = [sb(f"yT{i}", [P, KT, P]) for i in range(2)]
        res = [sb(f"res{i}", [P, TPC, C]) for i in range(2)]
        stats = [sb(f"stats{i}", [P, 6]) for i in range(2)]
        mv = [sb(f"mv{i}", [P, TPC, 2]) for i in range(2)]
        std = [sb(f"std{i}", [P, TPC]) for i in range(2)]
        rstd = [sb(f"rstd{i}", [P, TPC]) for i in range(2)]
        var1 = [sb(f"var1_{i}", [P, TPC]) for i in range(2)]
        var2 = [sb(f"var2_{i}", [P, TPC]) for i in range(2)]
        std2 = [sb(f"std2_{i}", [P, TPC]) for i in range(2)]
        rstd2 = [sb(f"rstd2_{i}", [P, TPC]) for i in range(2)]
        rows = [sb(f"rows{i}", [P, TPC, RW]) for i in range(2)]
        plain = [sb(f"plain{i}", [P, TPC, C]) for i in range(2)]
        x1T = sb("x1T", [P, KT, CHUNK])
        top = sb("top", [P, TPC])
        shifted = sb("shifted", [P, TPC, E])
        wanted = sb("wanted", [P, TPC, E])
        best = sb("best", [P, TPC])
        onehot = sb("onehot", [P, TPC, E], BF16)
        expd = sb("expd", [P, TPC, E])
        total = sb("total", [P, TPC])
        rank_all = sb("rank_all", [P, TPC, E])
        rank_own = sb("rank_own", [P, TPC, E])
        rank = sb("rank", [P, TPC])
        base_own = sb("base_own", [P, TPC, E])
        slot0 = sb("slot0", [P, TPC])
        dropped = sb("dropped", [P, TPC])
        slot1 = sb("slot1", [P, TPC])
        slot = [sb(f"slot_index{i}", [P, TPC], U32) for i in range(2)]
        psA = [ps(f"psA{i}", [P, CHUNK]) for i in range(2)]
        psB = ps("psB", [P, KT, P])
        psC = [ps(f"psC{i}", [P, CHUNK]) for i in range(2)]
        psD = ps("psD", [P, KT, CHUNK])
        psL = ps("psL", [P, CHUNK])
        logits = psL[:, 0:TPC * E].rearrange("p (t e) -> p t e", e=E)
        ranks = psL[:, 64:64 + TPC * E].rearrange("p (t e) -> p t e", e=E)
        counts = psL[:, 128:128 + E]

        w_loaded = sem("w3_loaded")
        w_first_loaded = sem("w_first_loaded")
        set_up = sem("set_up")
        loaded = [sem(f"loaded{i}") for i in range(2)]
        o_turned = sem("o_turned")
        y_ready = sem("y_ready")
        y_turned = sem("y_turned")
        yT_ready = sem("yT_ready")
        projected = sem("projected")
        xb_ready = sem("xb_ready")
        res_ready = sem("res_ready")
        den_ready = sem("den_ready")
        stat_ready = sem("stat_ready")
        mv_ready = sem("mv_ready")
        std_ready = sem("std_ready")
        rstd_ready = sem("rstd_ready")
        var_step = sem("var_step")
        std2_ready = sem("std2_ready")
        rstd2_ready = sem("rstd2_ready")
        rows_ready = sem("rows_ready")
        plain_ready = sem("plain_ready")
        plain_stored = [sem(f"plain_stored{i}") for i in range(2)]
        x1_turned = sem("x1_turned")
        x1T_ready = sem("x1T_ready")
        logits_ready = sem("logits_ready")
        gate_step = sem("gate_step")
        shifted_ready = sem("shifted_ready")
        exp_ready = sem("exp_ready")
        onehot_ready = sem("onehot_ready")
        ranks_ready = sem("ranks_ready")
        slots_ready = sem("slots_ready")
        rows_sent = [sem(f"rows_sent{i}") for i in range(2)]
        NC3 = B * NCH
        n_w = 10
        N_GATE = 15

        primed = (plain_ready, *plain_stored, res_ready, slots_ready, yT_ready, y_ready)

        block = ctx.enter_context(nc.Block())

        @block.sync
        def _(sp):
            for semaphore in primed:
                sp.sem_inc(semaphore, 1)

            def load(n, i):
                sp.dma_start(o_s[i][:], o_d[n]).then_inc(loaded[i], 16)
                sp.dma_start(x_s[i][:], x[n]).then_inc(loaded[i], 16)

            def load_two_ahead(n, i):
                turned, summed = in_register(sp, TPC * (n + 1)), in_register(sp, n + 1)
                sp.wait_ge(w_loaded, 16 * (n_w - 1))
                sp.wait_ge(o_turned, turned)
                sp.wait_ge(xb_ready, summed)
                load(n + 2, i)

            def store(n, i):
                done = in_register(sp, 1 + TPC * (n + 1))
                sp.wait_ge(w_loaded, 16 * (n_w - 1))
                sp.wait_ge(plain_ready, done)
                sp.dma_start(out_d[n], plain[i][:]).then_inc(plain_stored[i], 16)

            load(0, 0)
            for dst, src in ((id_s, ident), (bproj_s, bproj), (wproj_s, wproj), (gate_s, gate), (before_s, before),
                             (ones_s, ones), (prefer_s, prefer), (slot_base_s, slot_base), (token_s, tok0)):
                sp.dma_start(dst[:], src).then_inc(w_loaded, 16)
            load(1, 1)
            load_two_ahead(0, 0)
            with sp.Fori(0, NC3 // 2 - 2) as k:
                for i in (1, 0):
                    n = 2 * k + 2 - i
                    load_two_ahead(n, i)
                    store(n - 1, 1 - i)
            load_two_ahead(NC3 - 3, 1)
            for dst, src in zip(w_whole, w_first):
                sp.dma_start(dst[:], src).then_inc(w_first_loaded, 16)
            for n in range(NC3 - 4, NC3):
                store(n, n % 2)
            for i in range(2):
                sp.wait_ge(plain_stored[i], 1 + 16 * NC3 // 2)
            sp.wait_ge(w_first_loaded, 32)

        @block.tensor
        def _(pe):
            pe.wait_ge(w_loaded, 16 * (n_w - 1))

            def turn_o(n, i, h, t):
                if t == 0:
                    pe.wait_ge(loaded[i], 32 * (h + 1))
                if not (isinstance(n, int) and n == 0 and t < 2):
                    pe.wait_ge(y_ready, 1 + TPC * n + t - 1)
                for g in range(NG):
                    last = nc.tensor.transpose(psA[t % 2][:, g * P:(g + 1) * P], o_s[i][:, g, t * P:(t + 1) * P],
                                               id_s[:])
                last.then_inc(o_turned, 1)

            def turn_y(n, t):
                m = TPC * n + t
                pe.wait_ge(y_ready, 1 + m + 1)
                pe.wait_ge(yT_ready, 1 + m)
                for kt in range(KT):
                    last = nc.tensor.transpose(psB[:, kt, :],
                                               y_s[t % 2][:].rearrange("p h d -> p (h d)")[:, kt * P:(kt + 1) * P],
                                               id_s[:])
                last.then_inc(y_turned, 1)

            def project(n, t):
                m = TPC * n + t
                pe.wait_ge(yT_ready, 1 + m + 1)
                pe.wait_ge(res_ready, 1 + m)
                for kt in range(KT):
                    last = nc.tensor.matmul(psC[t % 2][:, 0:C], yT[t % 2][:, kt, :], wproj_s[:, kt, :],
                                            start=(kt == 0), stop=(kt == KT - 1))
                last.then_inc(projected, 1)

            def turn_x1(n, i):
                pe.wait_ge(rows_ready, TPC * (n + 1))
                for kt in range(KT):
                    for t in range(TPC):
                        last = nc.tensor.transpose(psD[:, kt, t * P:(t + 1) * P],
                                                   rows[i][:, t, kt * P:(kt + 1) * P], id_s[:])
                last.then_inc(x1_turned, 1)

            def gate_logits(n):
                pe.wait_ge(x1T_ready, KT * (n + 1))
                pe.wait_ge(slots_ready, 1 + n)
                for t in range(TPC):
                    for kt in range(KT):
                        last = nc.tensor.matmul(logits[:, t, :], x1T[:, kt, t * P:(t + 1) * P], gate_s[:, kt, :],
                                                start=(kt == 0), stop=(kt == KT - 1))
                last.then_inc(logits_ready, 1)

            def rank_chunk(n):
                pe.wait_ge(onehot_ready, n + 1)
                nc.tensor.matmul(ranks[:], before_s[:], onehot[:], start=True, stop=False)
                for t in range(TPC - 1):
                    later = TPC - 1 - t
                    nc.tensor.matmul(ranks[:, t + 1:TPC, :], ones_s[:],
                                     onehot[:, t:t + 1, :].to_broadcast([P, later, E]),
                                     start=False, stop=(t == TPC - 2))
                for t in range(TPC):
                    last = nc.tensor.matmul(counts, ones_s[:], onehot[:, t, :], start=(t == 0), stop=(t == TPC - 1))
                last.then_inc(ranks_ready, 1)

            def both(n, i, h, h_next):
                turn_y(n, 0)
                turn_o(n, i, h, 2)
                turn_y(n, 1)
                project(n, 0)
                turn_o(n, i, h, 3)
                turn_y(n, 2)
                project(n, 1)
                turn_x1(n - 1, 1 - i)
                turn_y(n, 3)
                project(n, 2)
                gate_logits(n - 1)
                project(n, 3)
                if h_next is not None:
                    turn_o(n + 1, 1 - i, h_next, 0)
                    turn_o(n + 1, 1 - i, h_next, 1)
                rank_chunk(n - 1)

            turn_o(0, 0, 0, 0)
            for t in range(TPC):
                if t + 1 < TPC:
                    turn_o(0, 0, 0, t + 1)
                turn_y(0, t)
                if t:
                    project(0, t - 1)
            project(0, TPC - 1)
            turn_o(1, 1, 0, 0)
            turn_o(1, 1, 0, 1)
            with pe.Fori(0, NC3 // 2 - 1) as k:
                both(2 * k + 1, 1, k, k + 1)
                both(2 * k + 2, 0, k + 1, k + 1)
            both(NC3 - 1, 1, NC3 // 2 - 1, None)
            turn_x1(NC3 - 1, 1)
            gate_logits(NC3 - 1)
            rank_chunk(NC3 - 1)

        @block.scalar
        def _(act):
            act.wait_ge(w_loaded, 16 * (n_w - 1))
            act.wait_ge(set_up, 2)

            def copy_yT(n, t):
                act.wait_ge(y_turned, TPC * n + t + 1)
                nc.scalar.activation(yT[t % 2][:], psB[:], ACT.Copy).then_inc(yT_ready, 1)

            def deviations(n, i):
                act.wait_ge(mv_ready, TPC * (n + 1))
                nc.scalar.activation(std[i][:], mv[i][:, :, 1], ACT.Sqrt, bias=eps_s[:]).then_inc(std_ready, 1)
                act.wait_ge(var_step, 2 * (n + 1))
                nc.scalar.activation(std2[i][:], var2[i][:], ACT.Sqrt, bias=eps_s[:]).then_inc(std2_ready, 1)

            def copy_x1T(n):
                act.wait_ge(x1_turned, n + 1)
                for kt in range(KT):
                    nc.scalar.activation(x1T[:, kt, :], psD[:, kt, :], ACT.Copy).then_inc(x1T_ready, 1)

            def exponentials(n):
                act.wait_ge(shifted_ready, n + 1)
                nc.scalar.activation(expd[:], shifted[:], ACT.Exp).then_inc(exp_ready, 1)

            def plain_rows(n, i, h, tiles):
                if tiles[0] == 0:
                    act.wait_ge(rstd2_ready, n + 1)
                    act.wait_ge(plain_stored[i], 1 + 16 * h)
                for t in tiles:
                    nc.scalar.activation(plain[i][:, t, :], rows[i][:, t, 0:C], ACT.Copy,
                                         scale=rstd2[i][:, t:t + 1]).then_inc(plain_ready, 1)

            def both(n, i, h_before):
                copy_yT(n, 0)
                plain_rows(n - 1, 1 - i, h_before, (0, 1))
                copy_yT(n, 1)
                plain_rows(n - 1, 1 - i, h_before, (2, 3))
                copy_yT(n, 2)
                copy_x1T(n - 1)
                copy_yT(n, 3)
                exponentials(n - 1)
                deviations(n, i)

            for t in range(TPC):
                copy_yT(0, t)
            deviations(0, 0)
            with act.Fori(0, NC3 // 2 - 1) as k:
                both(2 * k + 1, 1, k)
                both(2 * k + 2, 0, k)
            both(NC3 - 1, 1, NC3 // 2 - 1)
            copy_x1T(NC3 - 1)
            plain_rows(NC3 - 1, 1, NC3 // 2 - 1, range(TPC))
            exponentials(NC3 - 1)

        @block.vector
        def _(dve):
            nc.vector.memset(eps_s[:], EPS).then_inc(set_up, 1)
            nc.vector.memset(count_s[:], 0.0).then_inc(set_up, 1)
            for i in range(2):
                nc.vector.memset(rows[i][:, :, C:RW], 0.0).then_inc(set_up, 1)
            dve.wait_ge(set_up, 4)
            dve.wait_ge(w_loaded, 16 * (n_w - 1))

            def normalise(n, t):
                m = TPC * n + t
                heads = psA[t % 2][:].rearrange("p (h w) -> p h w", w=VW)
                dve.wait_ge(o_turned, m + 1)
                nc.vector.reciprocal(rden[t % 2][:], heads[:, :, HS]).then_inc(den_ready, 1)
                dve.wait_ge(den_ready, m + 1)
                nc.vector.tensor_tensor(y_s[t % 2][:], heads[:, :, 0:HS],
                                        rden[t % 2][:].unsqueeze(2).to_broadcast([P, H, HS]),
                                        ALU.mult).then_inc(y_ready, 1)

            def residual(n, i, t):
                m = TPC * n + t
                dve.wait_ge(projected, m + 1)
                if t == 0:
                    dve.wait_ge(xb_ready, n + 1)
                nc.vector.tensor_tensor(res[i][:, t, :], psC[t % 2][:, 0:C], xb[i][:, t, :],
                                        ALU.add).then_inc(res_ready, 1)
                dve.wait_ge(res_ready, 1 + m + 1)
                nc.vector.bn_stats(stats[t % 2][:], res[i][:, t, :]).then_inc(stat_ready, 1)
                done = in_register(dve, m + 1)
                dve.wait_ge(set_up, 4)
                dve.wait_ge(stat_ready, done)
                nc.vector.bn_aggr(mv[i][:, t, :], stats[t % 2][:]).then_inc(mv_ready, 1)

            def norm_chunk(n, i, h):
                dve.wait_ge(std_ready, n + 1)
                dve.wait_ge(mv_ready, TPC * (n + 1))
                nc.vector.reciprocal(rstd[i][:], std[i][:]).then_inc(rstd_ready, 1)
                dve.wait_ge(rstd_ready, n + 1)
                nc.vector.tensor_tensor(var1[i][:], mv[i][:, :, 1], rstd[i][:], ALU.mult).then_inc(var_step, 1)
                dve.wait_ge(var_step, 2 * n + 1)
                nc.vector.tensor_tensor(var2[i][:], var1[i][:], rstd[i][:], ALU.mult).then_inc(var_step, 1)
                dve.wait_ge(rows_sent[i], 16 + 16 * TPC * h)
                if not (isinstance(n, int) and n == 0):
                    dve.wait_ge(plain_ready, 1 + TPC * (n - 1))
                for t in range(TPC):
                    nc.vector.tensor_scalar(rows[i][:, t, 0:C], res[i][:, t, :], mv[i][:, t, 0:1],
                                            rstd[i][:, t:t + 1], ALU.subtract, ALU.mult).then_inc(rows_ready, 1)

            def norm_plain(n, i):
                dve.wait_ge(std2_ready, n + 1)
                nc.vector.reciprocal(rstd2[i][:], std2[i][:]).then_inc(rstd2_ready, 1)

            def step(n, k, instruction):
                instruction.then_inc(gate_step, 1)

            def wait_step(n, k):
                dve.wait_ge(gate_step, N_GATE * n + k)

            def per_tile(ap):
                return ap.unsqueeze(2).to_broadcast([P, TPC, E])

            def choose(n):
                dve.wait_ge(logits_ready, n + 1)
                step(n, 1, nc.vector.tensor_reduce(top[:], logits, axis=AX.X, op=ALU.max))
                wait_step(n, 1)
                nc.vector.tensor_tensor(shifted[:], logits, per_tile(top[:]), ALU.subtract).then_inc(shifted_ready, 1)
                dve.wait_ge(shifted_ready, n + 1)
                step(n, 2, nc.vector.scalar_tensor_tensor(wanted[:], shifted[:], 0.0, prefer_s[:],
                                                          ALU.is_equal, ALU.mult))
                wait_step(n, 2)
                step(n, 3, nc.vector.tensor_reduce(best[:], wanted[:], axis=AX.X, op=ALU.max))
                wait_step(n, 3)
                nc.vector.tensor_tensor(onehot[:], wanted[:], per_tile(best[:]), ALU.is_equal).then_inc(onehot_ready, 1)

            def place(n, i):
                dve.wait_ge(onehot_ready, n + 1)
                step(n, 4, nc.vector.tensor_tensor(base_own[:], onehot[:], slot_base_s[:], ALU.mult))
                dve.wait_ge(exp_ready, n + 1)
                step(n, 5, nc.vector.tensor_reduce(total[:], expd[:], axis=AX.X, op=ALU.add))
                wait_step(n, 4)
                step(n, 6, nc.vector.tensor_reduce(slot0[:], base_own[:], axis=AX.X, op=ALU.add))
                wait_step(n, 5)
                step(n, 7, nc.vector.reciprocal(rows[i][:, :, PROB], total[:]))
                dve.wait_ge(ranks_ready, n + 1)
                step(n, 8, nc.vector.tensor_tensor(rank_all[:], ranks, count_s[:].unsqueeze(1).to_broadcast([P, TPC, E]),
                                                   ALU.add))
                step(n, 9, nc.vector.tensor_copy(rows[i][:, :, TOKEN], token_s[:]))
                wait_step(n, 8)
                step(n, 10, nc.vector.tensor_tensor(rank_own[:], rank_all[:], onehot[:], ALU.mult))
                step(n, 11, nc.vector.tensor_tensor(count_s[:], counts, count_s[:], ALU.add))
                wait_step(n, 10)
                step(n, 12, nc.vector.tensor_reduce(rank[:], rank_own[:], axis=AX.X, op=ALU.add))
                wait_step(n, 12)
                step(n, 13, nc.vector.tensor_scalar(dropped[:], rank[:], float(CAP), NOWHERE, ALU.is_ge, ALU.mult))
                step(n, 14, nc.vector.tensor_tensor(slot1[:], slot0[:], rank[:], ALU.add))
                step(n, 15, nc.vector.tensor_scalar(token_s[:], token_s[:], float(CHUNK), None, ALU.add))
                wait_step(n, 15)
                nc.vector.tensor_tensor(slot[i][:], slot1[:], dropped[:], ALU.add).then_inc(slots_ready, 1)

            def both(n, i, h, last=False):
                norm_plain(n - 1, 1 - i)
                normalise(n, 2)
                residual(n, i, 0)
                normalise(n, 3)
                residual(n, i, 1)
                residual(n, i, 2)
                choose(n - 1)
                residual(n, i, 3)
                if not last:
                    normalise(n + 1, 0)
                    normalise(n + 1, 1)
                place(n - 1, 1 - i)
                norm_chunk(n, i, h)

            normalise(0, 0)
            normalise(0, 1)
            for t in range(TPC):
                if t + 2 < TPC:
                    normalise(0, t + 2)
                residual(0, 0, t)
            normalise(1, 0)
            normalise(1, 1)
            norm_chunk(0, 0, 0)
            with dve.Fori(0, NC3 // 2 - 1) as k:
                both(2 * k + 1, 1, k)
                both(2 * k + 2, 0, k + 1)
            both(NC3 - 1, 1, NC3 // 2 - 1, last=True)
            norm_plain(NC3 - 1, 1)
            choose(NC3 - 1)
            place(NC3 - 1, 1)

        @block.gpsimd
        def _(pool):
            for i in range(2):
                nc.gpsimd.dma_start(primer[i:i + 1, :], ident[i:i + 1, :]).then_inc(rows_sent[i], 16)
            pool.wait_ge(w_loaded, 16 * (n_w - 1))

            def add_bias(n, i, h):
                pool.wait_ge(loaded[i], 32 * (h + 1))
                if not (isinstance(n, int) and n == 0):
                    pool.wait_ge(res_ready, 1 + TPC * (n - 1))
                nc.gpsimd.tensor_tensor(xb[i][:], x_s[i][:], bproj_s[:].unsqueeze(1).to_broadcast([P, TPC, C]),
                                        ALU.add).then_inc(xb_ready, 1)

            def send(n, i):
                done = in_register(pool, 1 + (n + 1))
                pool.wait_ge(w_loaded, 16 * (n_w - 1))
                pool.wait_ge(slots_ready, done)
                for t in range(TPC):
                    nc.gpsimd.indirect_dma_start(
                        slots_d, bass.IndirectOffsetOnAxis(ap=slot[i][:, t:t + 1], axis=0),
                        rows[i][:, t, :], None, bounds_check=E * CAP - 1, oob_is_err=False,
                    ).then_inc(rows_sent[i], 16)

            add_bias(0, 0, 0)
            add_bias(1, 1, 0)
            with pool.Fori(0, NC3 // 2 - 1) as k:
                add_bias(2 * k + 2, 0, k + 1)
                send(2 * k, 0)
                add_bias(2 * k + 3, 1, k + 1)
                send(2 * k + 1, 1)
            for n in (NC3 - 2, NC3 - 1):
                send(n, n % 2)
            for i in range(2):
                pool.wait_ge(rows_sent[i], 16 + 16 * TPC * NC3 // 2)


def experts(nc, slots_d, w_whole, w1, b1, w2, b2, ident, out_d):
    with ExitStack() as ctx:
        def sb(name, shape, dt=F32):
            return ctx.enter_context(nc.sbuf_tensor(name, shape, dt))

        def ps(name, shape, dt=F32):
            return ctx.enter_context(nc.psum_tensor(name, shape, dt))

        def sem(name):
            return ctx.enter_context(nc.semaphore(name))

        id_s = sb("p4_id", [P, P])
        eps_s = sb("p4_eps", [P, 1])
        primer = sb("p4_primer", [2, P])
        w_hi = [[sb(f"w1_hi{i}", [P, KT, DFF], F32R), sb(f"w2_hi{i}", [P, FT, C], F32R)] for i in range(2)]
        w_lo = [[sb(f"w1_lo{i}", [P, KT, DFF], F32R), sb(f"w2_lo{i}", [P, FT, C], F32R)] for i in range(2)]
        b1_s = [sb(f"b1_s{i}", [P, FT]) for i in range(2)]
        b2_s = [sb(f"b2_s{i}", [P, C]) for i in range(2)]
        xe = [sb(f"xe{i}", [P, NBLK, RW]) for i in range(2)]
        token = [sb(f"token{i}", [P, NBLK], U32) for i in range(2)]
        x_hi = [sb(f"x_hi{i}", [P, NBLK * KT, P], F32R) for i in range(2)]
        x_lo = [sb(f"x_lo{i}", [P, NBLK * KT, P], F32R) for i in range(2)]
        h_whole = [sb(f"h_whole{i}", [P, CAP]) for i in range(2)]
        h_hi = sb("h_hi", [P, FT, CAP], F32R)
        h_lo = sb("h_lo", [P, FT, CAP], F32R)
        eo = [sb(f"eo{i}", [P, C]) for i in range(2)]
        z = [sb(f"z{i}", [P, C]) for i in range(2)]
        stats = [sb(f"p4_stats{i}", [P, 6]) for i in range(2)]
        mv = [sb(f"p4_mv{i}", [P, 2]) for i in range(2)]
        std = [sb(f"p4_std{i}", [P, 1]) for i in range(2)]
        rstd = [sb(f"p4_rstd{i}", [P, 1]) for i in range(2)]
        fin = [sb(f"fin{i}", [P, NBLK, C]) for i in range(2)]
        psX = [ps(f"psX{i}", [P, CHUNK]) for i in range(2)]
        psH = [ps(f"psH{i}", [P, CHUNK]) for i in range(4)]
        psY = [ps(f"psY{i}", [P, CHUNK]) for i in range(2)]
        PARTS = [(0, 3), (3, NBLK)]
        PAIRS = [(blk, kt) for blk in range(NBLK) for kt in range(KT)]
        TURNS = [PAIRS[k:k + 4] for k in range(0, len(PAIRS), 4)]
        NT = len(TURNS)
        ALL_TURNS = range(NT)
        TURNS_AT = {2: (0, 1), 3: (2,)}
        TURNS_AFTER = {0: (0, 1), 2: (2,)}
        CUTS = [(0, slice(0, 1)), (0, slice(1, KT)), (1, slice(0, FT // 2)), (1, slice(FT // 2, FT))]
        NCUT = len(CUTS)

        const_loaded = sem("p4_const")
        eps_set = sem("p4_eps_set")
        w_loaded = sem("p4_w")
        w_hi_ready = sem("w_hi_ready")
        w_lo_ready = sem("w_lo_ready")
        xe_loaded = [sem(f"p4_xe{i}") for i in range(2)]
        turned = sem("turned")
        x_hi_ready = sem("x_hi_ready")
        x_lo_ready = sem("x_lo_ready")
        up_done = sem("up_done")
        relu_done = sem("relu_done")
        h_hi_ready = sem("h_hi_ready")
        h_lo_ready = sem("h_lo_ready")
        y_done = sem("y_done")
        eo_ready = sem("eo_ready")
        z_ready = sem("z_ready")
        stat_ready = sem("p4_stat")
        mv_ready = sem("p4_mvr")
        std_ready = sem("p4_stdr")
        rstd_ready = sem("p4_rstdr")
        fin_ready = sem("fin_ready")
        token_ready = sem("token_ready")
        sent = [sem(f"sent{i}") for i in range(2)]

        block = ctx.enter_context(nc.Block())

        @block.sync
        def _(sp):
            def load_weights(e):
                for dst, src in zip(w_whole, (w1, w2)):
                    sp.dma_start(dst[:], src[e]).then_inc(w_loaded, 16)

            def load_rows(e, i):
                for dst, src in ((xe, slots_d), (b1_s, b1), (b2_s, b2)):
                    sp.dma_start(dst[i][:], src[e]).then_inc(xe_loaded[i], 16)

            sp.dma_start(id_s[:], ident).then_inc(const_loaded, 16)
            load_rows(0, 0)
            load_rows(1, 1)
            sp.wait_ge(w_lo_ready, NCUT)
            load_weights(1)
            with sp.Fori(0, E // 2 - 1) as k:
                for i in range(2):
                    e = 2 * k + i
                    cut = in_register(sp, NCUT * (e + 2))
                    used = in_register(sp, NBLK * (e + 1))
                    sp.wait_ge(const_loaded, 16)
                    sp.wait_ge(z_ready, used)
                    load_rows(e + 2, i)
                    sp.wait_ge(const_loaded, 16)
                    sp.wait_ge(w_lo_ready, cut)
                    load_weights(e + 2)

        @block.tensor
        def _(pe):
            def turn(e, i, uses, groups):
                if groups[0] == 0:
                    pe.wait_ge(xe_loaded[i], 48 * uses)
                for s in groups:
                    group = TURNS[s]
                    if not (isinstance(e, int) and e == 0 and s < 2):
                        pe.wait_ge(x_lo_ready, NT * e + s - 1)
                    for at, (blk, kt) in enumerate(group):
                        last = nc.tensor.transpose(psX[s % 2][:, at * P:(at + 1) * P],
                                                   xe[i][:, blk, kt * P:(kt + 1) * P], id_s[:])
                    last.then_inc(turned, 1)

            def up(e, i):
                pe.wait_ge(w_lo_ready, NCUT * e + NCUT // 2)
                pe.wait_ge(x_lo_ready, NT * (e + 1))
                for ft in range(FT):
                    cols = slice(ft * P, (ft + 1) * P)
                    if not (isinstance(e, int) and e == 0 and ft < 2):
                        pe.wait_ge(relu_done, 2 * FT * e + 2 * (ft - 1))
                    for part, (b0, b1_) in enumerate(PARTS):
                        out = psH[2 * (ft % 2) + part][:, 0:(b1_ - b0) * P]
                        for kt in range(KT):
                            hi, lo = (x[i][:].rearrange("p (b k) q -> p b k q", k=KT)[:, b0:b1_, kt, :]
                                      for x in (x_hi, x_lo))
                            nc.tensor.matmul(out, w_hi[i][0][:, kt, cols], hi, start=(kt == 0), stop=False)
                            nc.tensor.matmul(out, w_hi[i][0][:, kt, cols], lo, start=False, stop=False)
                            last = nc.tensor.matmul(out, w_lo[i][0][:, kt, cols], hi,
                                                    start=False, stop=(kt == KT - 1))
                        last.then_inc(up_done, 1)

            def down(e, i, uses_next):
                pe.wait_ge(w_lo_ready, NCUT * (e + 1))
                for blk in range(NBLK):
                    n, slots = NBLK * e + blk, slice(blk * P, (blk + 1) * P)
                    if blk in TURNS_AT and uses_next is not None:
                        turn(e + 1, 1 - i, uses_next, TURNS_AT[blk])
                    if not (isinstance(e, int) and e == 0 and blk < 2):
                        pe.wait_ge(eo_ready, n - 1)
                    out = psY[blk % 2][:, 0:C]
                    for ft in range(FT):
                        if blk == 0:
                            pe.wait_ge(h_lo_ready, FT * e + ft + 1)
                        nc.tensor.matmul(out, h_hi[:, ft, slots], w_hi[i][1][:, ft, :], start=(ft == 0), stop=False)
                        nc.tensor.matmul(out, h_hi[:, ft, slots], w_lo[i][1][:, ft, :], start=False, stop=False)
                        last = nc.tensor.matmul(out, h_lo[:, ft, slots], w_hi[i][1][:, ft, :],
                                                start=False, stop=(ft == FT - 1))
                    last.then_inc(y_done, 1)

            pe.wait_ge(const_loaded, 16)
            turn(0, 0, 1, ALL_TURNS)
            up(0, 0)
            down(0, 0, 1)
            with pe.Fori(0, E // 2 - 1) as k:
                for i in range(2):
                    e = 2 * k + 1 + i
                    up(e, 1 - i)
                    down(e, 1 - i, k + 2)
            up(E - 1, 1)
            down(E - 1, 1, None)

        @block.scalar
        def _(act):
            def take_turn(e, i, groups):
                for s in groups:
                    group = TURNS[s]
                    act.wait_ge(turned, NT * e + s + 1)
                    nc.scalar.activation(x_hi[i][:, 4 * s:4 * s + len(group), :].rearrange("p a q -> p (a q)"),
                                         psX[s % 2][:, 0:len(group) * P], ACT.Copy).then_inc(x_hi_ready, 1)

            def relu(e, i):
                for ft in range(FT):
                    for part, (b0, b1_) in enumerate(PARTS):
                        act.wait_ge(up_done, 2 * (FT * e + ft) + part + 1)
                        if part == 0 and not (isinstance(e, int) and e == 0 and ft < 2):
                            act.wait_ge(h_lo_ready, FT * e + ft - 1)
                        nc.scalar.activation(h_whole[ft % 2][:, b0 * P:b1_ * P],
                                             psH[2 * (ft % 2) + part][:, 0:(b1_ - b0) * P],
                                             ACT.Relu, bias=b1_s[i][:, ft:ft + 1]).then_inc(relu_done, 1)

            def cut_weights(e, i, piece):
                if piece == 0 and not (isinstance(e, int) and e == 0):
                    act.wait_ge(w_loaded, 32 * e)
                m, part = CUTS[piece]
                nc.scalar.activation(w_hi[i][m][:, part, :], w_whole[m][:, part, :],
                                     ACT.Copy).then_inc(w_hi_ready, 1)

            def deviation(e, blk):
                act.wait_ge(mv_ready, NBLK * e + blk + 1)
                nc.scalar.activation(std[blk % 2][:], mv[blk % 2][:, 1:2], ACT.Sqrt,
                                     bias=eps_s[:]).then_inc(std_ready, 1)

            def expert(e, i):
                relu(e, i)
                for blk in range(NBLK):
                    if blk < NCUT:
                        cut_weights(e + 1, 1 - i, blk)
                    deviation(e, blk)
                    take_turn(e + 1, 1 - i, TURNS_AFTER.get(blk, ()))

            act.wait_ge(eps_set, 1)
            for piece in range(NCUT):
                cut_weights(0, 0, piece)
            take_turn(0, 0, ALL_TURNS)
            expert(0, 0)
            with act.Fori(0, E // 2 - 1) as k:
                for i in range(2):
                    expert(2 * k + 1 + i, 1 - i)
            relu(E - 1, 1)
            for blk in range(NBLK):
                deviation(E - 1, blk)

        @block.vector
        def _(dve):
            nc.vector.memset(eps_s[:], EPS).then_inc(eps_set, 1)

            def cut_rows(e, i, groups):
                for s in groups:
                    group = TURNS[s]
                    dve.wait_ge(x_hi_ready, NT * e + s + 1)
                    hi, lo = (x[i][:, 4 * s:4 * s + len(group), :].rearrange("p a q -> p (a q)") for x in (x_hi, x_lo))
                    nc.vector.tensor_tensor(lo, psX[s % 2][:, 0:len(group) * P], hi, ALU.subtract).then_inc(x_lo_ready, 1)

            def cut_hidden(e):
                for ft in range(FT):
                    dve.wait_ge(relu_done, 2 * (FT * e + ft + 1))
                    nc.vector.tensor_copy(h_hi[:, ft, :], h_whole[ft % 2][:]).then_inc(h_hi_ready, 1)
                    dve.wait_ge(h_hi_ready, FT * e + ft + 1)
                    nc.vector.tensor_tensor(h_lo[:, ft, :], h_whole[ft % 2][:], h_hi[:, ft, :],
                                            ALU.subtract).then_inc(h_lo_ready, 1)

            def combine(e, i, blk):
                n, h = NBLK * e + blk, blk % 2
                dve.wait_ge(y_done, n + 1)
                nc.vector.tensor_tensor(eo[h][:], psY[h][:, 0:C], b2_s[i][:], ALU.add).then_inc(eo_ready, 1)
                dve.wait_ge(eo_ready, n + 1)
                nc.vector.scalar_tensor_tensor(z[h][:], eo[h][:], xe[i][:, blk, PROB:PROB + 1],
                                               xe[i][:, blk, 0:C], ALU.mult, ALU.add).then_inc(z_ready, 1)
                dve.wait_ge(z_ready, n + 1)
                nc.vector.bn_stats(stats[h][:], z[h][:]).then_inc(stat_ready, 1)
                done = in_register(dve, n + 1)
                dve.wait_ge(eps_set, 1)
                dve.wait_ge(stat_ready, done)
                nc.vector.bn_aggr(mv[h][:], stats[h][:]).then_inc(mv_ready, 1)

            def norm(e, i, blk):
                n, h = NBLK * e + blk, blk % 2
                dve.wait_ge(std_ready, n + 1)
                nc.vector.reciprocal(rstd[h][:], std[h][:]).then_inc(rstd_ready, 1)
                dve.wait_ge(rstd_ready, n + 1)
                nc.vector.tensor_scalar(fin[i][:, blk, :], z[h][:], mv[h][:, 0:1], rstd[h][:, 0:1],
                                        ALU.subtract, ALU.mult).then_inc(fin_ready, 1)

            def finish(e, i, uses, last=False):
                dve.wait_ge(xe_loaded[i], 48 * uses)
                dve.wait_ge(sent[i], 16 + 16 * NBLK * (uses - 1))
                nc.vector.tensor_copy(token[i][:], xe[i][:, :, TOKEN]).then_inc(token_ready, 1)
                for blk in range(NBLK):
                    combine(e, i, blk)
                    if blk:
                        norm(e, i, blk - 1)
                    if blk and not last:
                        cut_rows(e + 1, 1 - i, TURNS_AFTER.get(blk - 1, ()))
                norm(e, i, NBLK - 1)

            for piece, (m, part) in enumerate(CUTS):
                dve.wait_ge(w_hi_ready, piece + 1)
                nc.vector.tensor_tensor(w_lo[0][m][:, part, :], w_whole[m][:, part, :], w_hi[0][m][:, part, :],
                                        ALU.subtract).then_inc(w_lo_ready, 1)
            cut_rows(0, 0, ALL_TURNS)
            with dve.Fori(0, E // 2 - 1) as k:
                for i in range(2):
                    e = 2 * k + i
                    cut_hidden(e)
                    finish(e, i, k + 1)
            cut_hidden(E - 2)
            finish(E - 2, 0, E // 2)
            cut_hidden(E - 1)
            finish(E - 1, 1, E // 2, last=True)

        @block.gpsimd
        def _(pool):
            for i in range(2):
                nc.gpsimd.dma_start(primer[i:i + 1, :], ident[i:i + 1, :]).then_inc(sent[i], 16)

            def cut_weights(e, i, piece):
                pool.wait_ge(w_hi_ready, NCUT * e + piece + 1)
                m, part = CUTS[piece]
                nc.gpsimd.tensor_tensor(w_lo[i][m][:, part, :], w_whole[m][:, part, :], w_hi[i][m][:, part, :],
                                        ALU.subtract).then_inc(w_lo_ready, 1)

            def expert(e, i, last):
                for blk in range(NBLK):
                    if blk < NCUT and not last:
                        cut_weights(e + 1, 1 - i, blk)
                    done = in_register(pool, NBLK * e + blk + 1)
                    pool.wait_ge(eps_set, 1)
                    if blk == 0:
                        pool.wait_ge(token_ready, e + 1)
                    pool.wait_ge(fin_ready, done)
                    nc.gpsimd.indirect_dma_start(
                        out_d, bass.IndirectOffsetOnAxis(ap=token[i][:, blk:blk + 1], axis=0),
                        fin[i][:, blk, :], None, bounds_check=B * T - 1, oob_is_err=False,
                    ).then_inc(sent[i], 16)

            with pool.Fori(0, E // 2 - 1) as k:
                for i in range(2):
                    expert(2 * k + i, i, False)
            expert(E - 2, 0, False)
            expert(E - 1, 1, True)
            for i in range(2):
                pool.wait_ge(sent[i], 16 + 16 * NBLK * (E // 2))


def constants():
    bf = mybir.dt.np(BF16)
    row = np.arange(P)
    pos = np.arange(T, dtype=np.float32)[None]
    theta = (1.0 / np.float32(10000.0) ** (2.0 * (row % HS // 2).astype(np.float32) / HS)).astype(np.float32)
    angle = pos * theta[:, None]
    sign = np.where(row % 2 == 0, -1.0, 1.0).astype(np.float32)[:, None]
    causal = np.zeros((P, CHUNK), np.float32)
    causal[:, CHUNK - P:] = np.where(row[:, None] >= row[None], 0.0, LOWEST)
    no_row = np.zeros((P, RW), np.float32)
    no_row[:, TOKEN] = NOWHERE
    eye = np.eye(P, dtype=np.float32)
    return {
        "rope_cos": np.cos(angle).astype(np.float32),
        "rope_sin": (np.sin(angle) * sign).astype(np.float32),
        "causal": causal,
        "no_row": no_row,
        "ident": eye,
        "ident16": eye.astype(bf),
        "before": (row[:, None] < row[None]).astype(bf),
        "ones16": np.ones((P, P), bf),
        "prefer": np.broadcast_to((E - np.arange(E)).astype(np.float32), (P, TPC, E)).copy(),
        "slot_base": np.broadcast_to((CAP * np.arange(E)).astype(np.float32), (P, TPC, E)).copy(),
        "tok0": (row[:, None] + P * np.arange(TPC)[None]).astype(np.float32),
    }


def program(nc, a, out, scratch):
    x = a["x"].rearrange("b (c t p) d -> b c p t d", t=TPC, p=P)
    pieces, v, o, slots = scratch
    project_qkv(nc, x, a["wqk"].rearrange("(k p) n -> p k n", p=P), a["wv"].rearrange("(k p) n -> p k n", p=P),
                a["bqk"], a["bv2"], a["rope_cos"], a["rope_sin"], a["ident"],
                a["no_row"].unsqueeze(1).to_broadcast([P, E * NBLK, RW]),
                pieces.rearrange("b n (g p) t -> b n p g t", p=P),
                v.rearrange("b (c t p) w -> b c p t w", t=TPC, p=P),
                slots.rearrange("(n p) w -> p n w", p=P))
    attention(nc, pieces.rearrange("b n (s g j d) t -> b n s g d j t", s=2, g=NG, j=HPU),
              v.rearrange("b (t p) (g w) -> b p t w g", p=P, g=NG), a["causal"], a["ident16"], o)
    w1, w2 = a["w1"].rearrange("e (k p) n -> e p k n", p=P), a["w2"].rearrange("e (f p) n -> e p f n", p=P)
    with (nc.sbuf_tensor("w1_whole", [P, KT, DFF], F32) as w1_whole,
          nc.sbuf_tensor("w2_whole", [P, FT, C], F32) as w2_whole):
        w_whole = (w1_whole, w2_whole)
        project_and_gate(nc, x.rearrange("b c p t d -> (b c) p t d"), o.rearrange("n g p q -> n p g q"),
                         a["wproj"].rearrange("(k p) n -> p k n", p=P), a["bproj"],
                         a["gate"].rearrange("(k p) e -> p k e", p=P), a["ident"], a["before"], a["ones16"],
                         a["prefer"], a["slot_base"], a["tok0"], slots,
                         out.rearrange("b (c t p) d -> (b c) p t d", t=TPC, p=P), w_whole, (w1[0], w2[0]))
        experts(nc, slots.rearrange("(e n p) w -> e p n w", e=E, p=P), w_whole, w1, a["b1"], w2, a["b2"],
                a["ident"], out.rearrange("b t d -> (b t) d"))


def kernel(L0_attn_x, L0_attn_W_qkv, L0_attn_b_qkv, L0_attn_W_proj, L0_attn_b_proj, L0_ffn_gate_w,
           L0_ffn_w1, L0_ffn_b1, L0_ffn_w2, L0_ffn_b2):
    import concourse.bacc as bacc
    from concourse.bass_utils import run_bass_kernel_spmd

    w = np.asarray(L0_attn_W_qkv).reshape(C, H, 3, HS)
    bias = np.asarray(L0_attn_b_qkv).reshape(H, 3, HS)
    arrays = {
        "x": np.asarray(L0_attn_x),
        "wqk": w[:, :, 0:2].transpose(0, 2, 1, 3).reshape(C, 2 * C),
        "wv": w[:, :, 2].reshape(C, C),
        "bqk": bias[:, 0:2].transpose(1, 0, 2).reshape(QKG, P).T,
        "bv2": np.broadcast_to(bias[:, 2].reshape(C), (P, 2, C)),
        "wproj": np.asarray(L0_attn_W_proj),
        "bproj": np.broadcast_to(np.asarray(L0_attn_b_proj), (P, C)),
        "gate": np.asarray(L0_ffn_gate_w).T,
        "w1": np.asarray(L0_ffn_w1),
        "b1": np.asarray(L0_ffn_b1).reshape(E, FT, P).transpose(0, 2, 1),
        "w2": np.asarray(L0_ffn_w2),
        "b2": np.broadcast_to(np.asarray(L0_ffn_b2)[:, None, :], (E, P, C)),
        **constants(),
    }
    arrays = {k: np.ascontiguousarray(a) for k, a in arrays.items()}
    nc = bacc.Bacc("TRN2", target_bir_lowering=False, num_devices=1)
    a = {k: nc.dram_tensor(k, v.shape, mybir.dt.from_np(v.dtype), kind="ExternalInput").ap() for k, v in arrays.items()}
    out = nc.dram_tensor("out", [B, T, C], F32, kind="ExternalOutput").ap()
    scratch = [nc.dram_tensor(n, s, dt, kind="Internal").ap() for n, s, dt in (
        ("pieces_d", [B, NPIECE, 2 * C, T], BF16), ("v_d", [B, T, H * VW], F32),
        ("o_d", [B * NCH, NG, P, CHUNK], F32), ("slots_d", [E * CAP, RW], F32))]
    program(nc, a, out, scratch)
    return run_bass_kernel_spmd(nc, [arrays], core_ids=[0]).results[0]["out"]
```
